# Optimizing a Trainium2 kernel written in Bass

```python
import numpy as np
import jax
import jax.numpy as jnp

def _softmax(x, axis=-1):
    return jax.nn.softmax(x, axis=axis)

def _gelu(x):
    return jax.nn.gelu(x, approximate=True)

def _silu(x):
    return jax.nn.silu(x)

def _sigmoid(x):
    return jax.nn.sigmoid(x)

def _layernorm(x, axis=-1, eps=1e-05):
    m = jnp.mean(x, axis=axis, keepdims=True)
    v = jnp.var(x, axis=axis, keepdims=True)
    return (x - m) / jnp.sqrt(v + eps)

def _scatter_add(tgt, idx, src, axis=0):
    return tgt.at[idx].add(src)

def _segment_sum(src, seg, n):
    return jax.ops.segment_sum(src, seg, n)
kernel_name = 'mk_prb_d2_jaxref_r8_30a255'

def setup_inputs(seed: int=0):
    np.random.seed(seed)
    _w = jnp.asarray

    def _L0_attn_setup():
        import jax, jax.numpy as jnp
        import numpy as np
        LN_EPS = 1e-05
        key = jax.random.key(seed)
        ks = jax.random.split(key, 8)
        B, L, d_model = (2, 256, 128)
        d_inner, d_state, dt_rank, d_conv = (256, 16, 64, 4)
        f32 = jnp.float32
        A_init = jnp.broadcast_to(jnp.arange(1, d_state + 1, dtype=f32), (d_inner, d_state))
        return {'x': jax.random.normal(ks[0], (B, L, d_model), f32), 'norm_g': jnp.ones((d_model,), f32), 'norm_b': jnp.zeros((d_model,), f32), 'in_w': jax.random.normal(ks[1], (2 * d_inner, d_model), f32) / np.sqrt(d_model), 'conv_w': jax.random.normal(ks[2], (d_inner, 1, d_conv), f32) / np.sqrt(d_conv), 'conv_b': jnp.zeros((d_inner,), f32), 'xproj_w': jax.random.normal(ks[3], (dt_rank + 2 * d_state, d_inner), f32) / np.sqrt(d_inner), 'dt_w': jax.random.normal(ks[4], (d_inner, dt_rank), f32) / np.sqrt(dt_rank), 'dt_b': jax.random.uniform(ks[5], (d_inner,), f32, np.log(0.0001), np.log(0.1)), 'A_log': jnp.log(A_init), 'D': jnp.ones((d_inner,), f32), 'out_w': jax.random.normal(ks[6], (d_model, d_inner), f32) / np.sqrt(d_inner)}
    _L0_attn_in = _L0_attn_setup()

    def _L0_ffn_setup():
        import jax, jax.numpy as jnp
        import numpy as np
        NUM_EXPERTS = 8
        TOP_K = 2
        DIM = 128
        HIDDEN = 512
        B, S = (2, 128)
        key = jax.random.key(seed)
        k_x, k_g, k_1, k_2, k_3 = jax.random.split(key, 5)
        s_d = 1.0 / np.sqrt(DIM)
        s_h = 1.0 / np.sqrt(HIDDEN)
        return {'x': jax.random.normal(k_x, (B, S, DIM), dtype=jnp.float32), 'gate_w': jax.random.normal(k_g, (NUM_EXPERTS, DIM), dtype=jnp.float32) * s_d, 'w1': jax.random.normal(k_1, (NUM_EXPERTS, HIDDEN, DIM), dtype=jnp.float32) * s_d, 'w2': jax.random.normal(k_2, (NUM_EXPERTS, DIM, HIDDEN), dtype=jnp.float32) * s_h, 'w3': jax.random.normal(k_3, (NUM_EXPERTS, HIDDEN, DIM), dtype=jnp.float32) * s_d}
    _L0_ffn_in = _L0_ffn_setup()

    def _L1_attn_setup():
        import jax, jax.numpy as jnp
        import numpy as np
        import math
        B, S, E, H = (2, 256, 128, 8)
        Dh = E // H

        def _pos_encoding(s, e):
            pos = jnp.arange(s, dtype=jnp.float32)[:, None]
            div = jnp.exp(jnp.arange(0, e, 2, dtype=jnp.float32) * (-math.log(10000.0) / e))
            pe = jnp.zeros((s, e), jnp.float32)
            pe = pe.at[:, 0::2].set(jnp.sin(pos * div))
            pe = pe.at[:, 1::2].set(jnp.cos(pos * div))
            return pe

        def _rel_shift(ps):
            b, h, s1, s2 = ps.shape
            padded = jnp.pad(ps, ((0, 0), (0, 0), (0, 0), (1, 0)))
            return padded.reshape(b, h, s2 + 1, s1)[:, :, 1:, :].reshape(b, h, s1, s2)

        def _forward(inputs, ln_gamma, ln_beta, Wq, bq, Wk, bk, Wv, bv, Wp, u_bias, v_bias, Wo, bo):
            b, s, e = inputs.shape
            mu = inputs.mean(-1, keepdims=True)
            var = inputs.var(-1, keepdims=True)
            xn = (inputs - mu) / jnp.sqrt(var + 1e-05) * ln_gamma + ln_beta
            xh = xn.reshape(b, s, H, Dh)
            q = xh @ Wq + bq
            k = xh @ Wk + bk
            v = xh @ Wv + bv
            pe = _pos_encoding(s, e).reshape(s, H, Dh)
            p = pe @ Wp
            content = jnp.einsum('bqhd,bkhd->bhqk', q + u_bias, k)
            pos_score = jnp.einsum('bqhd,khd->bhqk', q + v_bias, p)
            pos_score = _rel_shift(pos_score)
            score = (content + pos_score) / jnp.sqrt(jnp.float32(e))
            attn = jax.nn.softmax(score, axis=-1)
            ctx = jnp.einsum('bhqk,bkhd->bqhd', attn, v).reshape(b, s, e)
            return ctx @ Wo + bo
        key = jax.random.key(seed)
        ks = jax.random.split(key, 9)
        g = lambda k, shp: jax.random.normal(k, shp, jnp.float32) * 0.02
        return {'inputs': jax.random.normal(ks[0], (B, S, E), jnp.float32), 'ln_gamma': jnp.ones((E,), jnp.float32), 'ln_beta': jnp.zeros((E,), jnp.float32), 'Wq': g(ks[1], (Dh, Dh)), 'bq': jnp.zeros((Dh,), jnp.float32), 'Wk': g(ks[2], (Dh, Dh)), 'bk': jnp.zeros((Dh,), jnp.float32), 'Wv': g(ks[3], (Dh, Dh)), 'bv': jnp.zeros((Dh,), jnp.float32), 'Wp': g(ks[4], (Dh, Dh)), 'u_bias': g(ks[5], (H, Dh)), 'v_bias': g(ks[6], (H, Dh)), 'Wo': g(ks[7], (E, E)), 'bo': jnp.zeros((E,), jnp.float32)}
    _L1_attn_in = _L1_attn_setup()

    def _L1_ffn_setup():
        import jax, jax.numpy as jnp
        import numpy as np
        H = 128
        E = 8
        B, S = (4, 256)
        key = jax.random.key(seed)
        k1, k2, k3, k4 = jax.random.split(key, 4)
        x = jax.random.normal(k1, (B, S, H), dtype=jnp.float32)
        wg = jax.random.normal(k2, (H, E), dtype=jnp.float32) * 0.02
        W = jax.random.normal(k3, (E, H, H), dtype=jnp.float32) * 0.02
        b = jax.random.normal(k4, (E, H), dtype=jnp.float32) * 0.02
        return {'x': x, 'wg': wg, 'W': W, 'b': b}
    _L1_ffn_in = _L1_ffn_setup()
    _d = {'L0_attn_x': _L0_attn_in['x'], 'L0_attn_norm_g': _L0_attn_in['norm_g'], 'L0_attn_norm_b': _L0_attn_in['norm_b'], 'L0_attn_in_w': _L0_attn_in['in_w'], 'L0_attn_conv_w': _L0_attn_in['conv_w'], 'L0_attn_conv_b': _L0_attn_in['conv_b'], 'L0_attn_xproj_w': _L0_attn_in['xproj_w'], 'L0_attn_dt_w': _L0_attn_in['dt_w'], 'L0_attn_dt_b': _L0_attn_in['dt_b'], 'L0_attn_A_log': _L0_attn_in['A_log'], 'L0_attn_D': _L0_attn_in['D'], 'L0_attn_out_w': _L0_attn_in['out_w'], 'L0_ffn_gate_w': _L0_ffn_in['gate_w'], 'L0_ffn_w1': _L0_ffn_in['w1'], 'L0_ffn_w2': _L0_ffn_in['w2'], 'L0_ffn_w3': _L0_ffn_in['w3'], 'L1_attn_ln_gamma': _L1_attn_in['ln_gamma'], 'L1_attn_ln_beta': _L1_attn_in['ln_beta'], 'L1_attn_Wq': _L1_attn_in['Wq'], 'L1_attn_bq': _L1_attn_in['bq'], 'L1_attn_Wk': _L1_attn_in['Wk'], 'L1_attn_bk': _L1_attn_in['bk'], 'L1_attn_Wv': _L1_attn_in['Wv'], 'L1_attn_bv': _L1_attn_in['bv'], 'L1_attn_Wp': _L1_attn_in['Wp'], 'L1_attn_u_bias': _L1_attn_in['u_bias'], 'L1_attn_v_bias': _L1_attn_in['v_bias'], 'L1_attn_Wo': _L1_attn_in['Wo'], 'L1_attn_bo': _L1_attn_in['bo'], 'L1_ffn_wg': _L1_ffn_in['wg'], 'L1_ffn_W': _L1_ffn_in['W'], 'L1_ffn_b': _L1_ffn_in['b']}
    _x0 = _d['L0_attn_x']
    _d['L0_attn_x'] = jax.random.normal(jax.random.fold_in(jax.random.key(seed), 1), (2, 1024, 128), dtype=_x0.dtype)
    del _x0
    return _d

def reference(L0_attn_x, L0_attn_norm_g, L0_attn_norm_b, L0_attn_in_w, L0_attn_conv_w, L0_attn_conv_b, L0_attn_xproj_w, L0_attn_dt_w, L0_attn_dt_b, L0_attn_A_log, L0_attn_D, L0_attn_out_w, L0_ffn_gate_w, L0_ffn_w1, L0_ffn_w2, L0_ffn_w3, L1_attn_ln_gamma, L1_attn_ln_beta, L1_attn_Wq, L1_attn_bq, L1_attn_Wk, L1_attn_bk, L1_attn_Wv, L1_attn_bv, L1_attn_Wp, L1_attn_u_bias, L1_attn_v_bias, L1_attn_Wo, L1_attn_bo, L1_ffn_wg, L1_ffn_W, L1_ffn_b):

    def _L0_attn_ref(x, norm_g, norm_b, in_w, conv_w, conv_b, xproj_w, dt_w, dt_b, A_log, D, out_w):
        import jax, jax.numpy as jnp
        import numpy as np
        LN_EPS = 1e-05
        Bsz, L, d_model = x.shape
        d_inner, d_state = A_log.shape
        dt_rank = dt_w.shape[1]
        d_conv = conv_w.shape[-1]
        residual = x
        mu = jnp.mean(x, axis=-1, keepdims=True)
        var = jnp.var(x, axis=-1, keepdims=True)
        xn = (x - mu) * jax.lax.rsqrt(var + LN_EPS) * norm_g + norm_b
        xz = xn @ in_w.T
        x_, z = (xz[..., :d_inner], xz[..., d_inner:])
        xp = jnp.pad(x_, ((0, 0), (d_conv - 1, 0), (0, 0)))
        w = conv_w[:, 0, :]
        xc = conv_b + sum((xp[:, k:k + L, :] * w[:, k] for k in range(d_conv)))
        u = jax.nn.silu(xc)
        dbc = u @ xproj_w.T
        delta_raw = dbc[..., :dt_rank]
        Bm = dbc[..., dt_rank:dt_rank + d_state]
        Cm = dbc[..., dt_rank + d_state:]
        delta = jax.nn.softplus(delta_raw @ dt_w.T + dt_b)
        A = -jnp.exp(A_log)

        def step(h, ins):
            d_t, B_t, C_t, u_t = ins
            dA = jnp.exp(d_t[..., None] * A)
            dB = d_t[..., None] * B_t[:, None, :]
            h = dA * h + dB * u_t[..., None]
            y_t = jnp.einsum('bdn,bn->bd', h, C_t)
            return (h, y_t)
        h0 = jnp.zeros((Bsz, d_inner, d_state), x.dtype)
        xs = (jnp.swapaxes(delta, 0, 1), jnp.swapaxes(Bm, 0, 1), jnp.swapaxes(Cm, 0, 1), jnp.swapaxes(u, 0, 1))
        _, ys = jax.lax.scan(step, h0, xs)
        y = jnp.swapaxes(ys, 0, 1) + u * D
        y = y * jax.nn.silu(z)
        return y @ out_w.T + residual

    def _L0_ffn_ref(x, gate_w, w1, w2, w3):
        import jax, jax.numpy as jnp
        import numpy as np
        NUM_EXPERTS = 8
        TOP_K = 2
        DIM = 128
        HIDDEN = 512
        B, S = (2, 128)
        orig_shape = x.shape
        xt = x.reshape(-1, orig_shape[-1])
        scores = xt @ gate_w.T
        top_vals, top_idx = jax.lax.top_k(scores, TOP_K)
        top_w = jax.nn.softmax(top_vals, axis=-1)
        combine = jnp.einsum('tke,tk->te', jax.nn.one_hot(top_idx, NUM_EXPERTS, dtype=xt.dtype), top_w)
        h = jax.nn.silu(jnp.einsum('td,ehd->eth', xt, w1)) * jnp.einsum('td,ehd->eth', xt, w3)
        ye = jnp.einsum('eth,edh->etd', h, w2)
        y = jnp.einsum('te,etd->td', combine, ye)
        return y.reshape(orig_shape)

    def _L1_attn_ref(inputs, ln_gamma, ln_beta, Wq, bq, Wk, bk, Wv, bv, Wp, u_bias, v_bias, Wo, bo):
        import jax, jax.numpy as jnp
        import numpy as np
        import math
        B, S, E, H = (2, 256, 128, 8)
        Dh = E // H

        def _pos_encoding(s, e):
            pos = jnp.arange(s, dtype=jnp.float32)[:, None]
            div = jnp.exp(jnp.arange(0, e, 2, dtype=jnp.float32) * (-math.log(10000.0) / e))
            pe = jnp.zeros((s, e), jnp.float32)
            pe = pe.at[:, 0::2].set(jnp.sin(pos * div))
            pe = pe.at[:, 1::2].set(jnp.cos(pos * div))
            return pe

        def _rel_shift(ps):
            b, h, s1, s2 = ps.shape
            padded = jnp.pad(ps, ((0, 0), (0, 0), (0, 0), (1, 0)))
            return padded.reshape(b, h, s2 + 1, s1)[:, :, 1:, :].reshape(b, h, s1, s2)

        def _forward(inputs, ln_gamma, ln_beta, Wq, bq, Wk, bk, Wv, bv, Wp, u_bias, v_bias, Wo, bo):
            b, s, e = inputs.shape
            mu = inputs.mean(-1, keepdims=True)
            var = inputs.var(-1, keepdims=True)
            xn = (inputs - mu) / jnp.sqrt(var + 1e-05) * ln_gamma + ln_beta
            xh = xn.reshape(b, s, H, Dh)
            q = xh @ Wq + bq
            k = xh @ Wk + bk
            v = xh @ Wv + bv
            pe = _pos_encoding(s, e).reshape(s, H, Dh)
            p = pe @ Wp
            content = jnp.einsum('bqhd,bkhd->bhqk', q + u_bias, k)
            pos_score = jnp.einsum('bqhd,khd->bhqk', q + v_bias, p)
            pos_score = _rel_shift(pos_score)
            score = (content + pos_score) / jnp.sqrt(jnp.float32(e))
            attn = jax.nn.softmax(score, axis=-1)
            ctx = jnp.einsum('bhqk,bkhd->bqhd', attn, v).reshape(b, s, e)
            return ctx @ Wo + bo
        return _forward(inputs, ln_gamma, ln_beta, Wq, bq, Wk, bk, Wv, bv, Wp, u_bias, v_bias, Wo, bo)

    def _L1_ffn_ref(x, wg, W, b):
        import jax, jax.numpy as jnp
        import numpy as np
        H = 128
        E = 8
        B, S = (4, 256)
        Bb, Ss, Hh = x.shape
        Ee = wg.shape[1]
        T = Bb * Ss
        C = T // Ee
        xt = x.reshape(T, Hh)
        logits = xt @ wg
        probs = jax.nn.softmax(logits, axis=-1)
        idx = jnp.argmax(probs, axis=-1)
        mask = jax.nn.one_hot(idx, Ee, dtype=xt.dtype)
        locations = jnp.cumsum(mask, axis=0) - mask
        mask = mask * (locations < C).astype(xt.dtype)
        gate = jnp.sum(probs * mask, axis=-1)
        loc_s = jnp.sum(locations * mask, axis=-1).astype(jnp.int32)
        loc_oh = jax.nn.one_hot(loc_s, C, dtype=xt.dtype)
        dispatch = mask[:, :, None] * loc_oh[:, None, :]
        combine = gate[:, None, None] * dispatch
        exp_in = jnp.einsum('tec,th->ech', dispatch, xt)
        exp_out = jnp.einsum('ech,efh->ecf', exp_in, W) + b[:, None, :]
        out = jnp.einsum('tec,ecf->tf', combine, exp_out)
        return out.reshape(Bb, Ss, Hh)
    x = L0_attn_x
    xn = _layernorm(x, axis=-1)
    x = x + _L0_attn_ref(xn, L0_attn_norm_g, L0_attn_norm_b, L0_attn_in_w, L0_attn_conv_w, L0_attn_conv_b, L0_attn_xproj_w, L0_attn_dt_w, L0_attn_dt_b, L0_attn_A_log, L0_attn_D, L0_attn_out_w) + _L0_ffn_ref(xn, L0_ffn_gate_w, L0_ffn_w1, L0_ffn_w2, L0_ffn_w3)
    xn = _layernorm(x, axis=-1)
    x = x + _L1_attn_ref(xn, L1_attn_ln_gamma, L1_attn_ln_beta, L1_attn_Wq, L1_attn_bq, L1_attn_Wk, L1_attn_bk, L1_attn_Wv, L1_attn_bv, L1_attn_Wp, L1_attn_u_bias, L1_attn_v_bias, L1_attn_Wo, L1_attn_bo) + _L1_ffn_ref(xn, L1_ffn_wg, L1_ffn_W, L1_ffn_b)
    return x

_drawn_inputs = setup_inputs


def setup_inputs(seed=0):
    import zlib

    import numpy as np

    out = dict(_drawn_inputs(seed))
    spreads = {'L0_attn_norm_g': (1.0, 0.2),
     'L0_attn_norm_b': (0.0, 0.1),
     'L0_attn_conv_b': (0.0, 0.358),
     'L0_attn_D': (1.0, 0.2),
     'L1_attn_ln_gamma': (1.0, 0.6),
     'L1_attn_ln_beta': (0.0, 0.8),
     'L1_attn_bq': (0.0, 0.8),
     'L1_attn_bk': (0.0, 2.0),
     'L1_attn_bv': (0.0, 0.67),
     'L1_attn_bo': (0.0, 0.1)}
    factors = {'L0_attn_A_log': 9.332,
     'L1_attn_Wq': 8.0,
     'L1_attn_Wk': 8.0,
     'L1_attn_Wv': 8.0,
     'L1_attn_Wp': 64.0,
     'L1_attn_u_bias': 64.0,
     'L1_attn_v_bias': 64.0,
     'L1_attn_Wo': 4.994,
     'L1_ffn_wg': 3.327,
     'L1_ffn_W': 3.127,
     'L1_ffn_b': 22.294}
    for name, (base, spread) in spreads.items():
        noise = np.random.default_rng([zlib.crc32(name.encode()), seed]).standard_normal(out[name].shape)
        drawn = base * np.exp(spread * noise) if base else spread * noise
        out[name] = jnp.asarray(drawn.astype(out[name].dtype))
    for name, factor in factors.items():
        out[name] = (out[name] * factor).astype(out[name].dtype)
    return out
```

```python
from contextlib import ExitStack

import concourse.bass as bass
from concourse import mybir

F32 = mybir.dt.float32
BF16 = mybir.dt.bfloat16
I32 = mybir.dt.int32
U32 = mybir.dt.uint32
ALU = mybir.AluOpType
ACT = mybir.ActivationFunctionType
AX = mybir.AxisListType

P = 128
B, L, D = 2, 1024, 128
T = B * L
NT = T // P
DG = 2
NS = 16
R = 64
KC = 4
CH = 512
NCH = T // CH
EPS = 1e-5


class Tally:

    def __init__(self, sem):
        self.sem, self.n = sem, 0

    def by(self, ins):
        ins.then_inc(self.sem, 1)
        self.n += 1
        return self.n


def bc(ap, shape):
    return ap.to_broadcast(shape)


class Shared:
    pass


def norms_and_projections(nc, s, I):
    sem = s.sem
    x_in, w_in = sem("x_loaded"), sem("weights_loaded")
    dve_done, act_done, pool_done = sem("a_dve"), sem("a_act"), sem("a_pool")
    var_ready, rstd_ready = sem("var_ready"), sem("rstd_ready")
    xn_ready, xa_ready = sem("xn_ready"), sem("xa_ready")
    tr_done, tr_copied = sem("transposes_done"), sem("transposes_copied")
    proj_done, proj_copied = sem("in_proj_done"), sem("in_proj_copied")
    conv_done, u_ready = sem("conv_done"), sem("u_ready")
    score_done = sem("scores_done")
    dbc_done, draw_copied, bc_copied = sem("dbc_done"), sem("draw_copied"), sem("bc_copied")
    dt_done, abs_done, exp_done, one_done, ln_done, delta_ready = (
        sem("dt_done"), sem("softplus_abs"), sem("softplus_exp"), sem("softplus_one"), sem("softplus_ln"), sem("delta_ready"))
    pads_ready, scores_copied = sem("pads_ready"), sem("scores_copied")
    bank = s.bank
    with ExitStack() as ctx:
        def sb(name, shape, dt=F32):
            return ctx.enter_context(nc.sbuf_tensor(name, shape, dt))

        work = sb("norm_work", [P, NT, D])
        sq = sb("norm_squares", [P, NT, D])
        mean = sb("norm_mean", [P, NT])
        var = sb("norm_var", [P, NT])
        rstd = sb("norm_rstd", [P, NT])
        half = sb("minus_half", [P, NT])
        xaT = sb("xaT", [P, T])
        xp = sb("x_padded", [P, DG, B, L + KC - 1])
        xc = sb("x_conv", [P, DG, B, L])
        draw = sb("delta_low_rank", [R, T])
        in_w = sb("in_w_t", [P, 4 * P])
        xw = sb("xproj_w_t", [P, DG, R])
        xbc = sb("xproj_bc_t", [P, DG, 96])
        dtw = sb("dt_w_t", [R, DG * P])
        spe = sb("softplus_e", [P, 2, CH])
        spw = sb("softplus_w", [P, 2, CH])
        spc = sb("softplus_c", [P, 2, CH])
        spr = sb("softplus_r", [P, 2, CH])
        spl = sb("softplus_l", [P, 2, CH])
        bcr = sb("bc_rest", [96, T])
        bcm = sb("bc_middle", [96, T], BF16)
        bcl = sb("bc_low", [96, T], BF16)

        block = ctx.enter_context(nc.Block())

        NW = 9

        @block.sync
        def _(sp):
            sp.dma_start(s.x[:], I["L0_attn_x"].rearrange("b (t p) d -> p (b t) d", p=P)).then_inc(x_in, 16)
            for dst, src in ((s.ident[:], I["ident"]), (in_w[:], I["in_w_t"]), (s.vec[:], I["vectors"]),
                             (xw[:], I["xproj_t"].rearrange("(g p) r -> p g r", p=P)),
                             (xbc[:], I["xproj_bc_t"].rearrange("(g p) r -> p g r", p=P)),
                             (dtw[:], I["dt_w_t"]), (s.gate_w[:], I["gate_w_t"]),
                             (s.A[:], I["L0_attn_A_log"].rearrange("(g p) n -> p g n", p=P)),
                             (s.taps[:], I["L0_attn_conv_w"].rearrange("(g p) k -> p g k", p=P))):
                sp.dma_start(dst, src).then_inc(w_in, 16)

        @block.gpsimd
        def _(pool):
            t = Tally(pool_done)
            t.by(nc.gpsimd.memset(half[:], -0.5))
            t.by(nc.gpsimd.memset(xp[:, :, :, 0:KC - 1], 0.0))
            pool.wait_ge(pool_done, t.n)
            pool.sem_inc(pads_ready, 1)
            for k in range(2):
                pool.wait_ge(var_ready, k + 1)
                nc.gpsimd.tensor_tensor(rstd[:], var[:], half[:], ALU.pow).then_inc(rstd_ready, 1)
            for i in range(DG * NCH):
                g, c = i // NCH, i % NCH
                cols = slice(c * CH, (c + 1) * CH)
                pool.wait_ge(delta_ready, i + 1)
                nc.gpsimd.tensor_tensor(s.du[:, g, cols], s.delta[:, g, cols], s.u[:, g, cols], ALU.mult)

        @block.vector
        def _(dve):
            t = Tally(dve_done)

            def link(ins):
                dve.wait_ge(dve_done, t.by(ins))

            def norm(src, dst, k, ready):
                b3 = [P, NT, D]
                link(nc.vector.reduce_sum(mean[:], src, AX.X))
                link(nc.vector.tensor_scalar(mean[:], mean[:], 1.0 / D, None, ALU.mult))
                link(nc.vector.tensor_tensor(work[:], src, bc(mean[:, :, None], b3), ALU.subtract))
                link(nc.vector.tensor_tensor(sq[:], work[:], work[:], ALU.mult))
                link(nc.vector.reduce_sum(var[:], sq[:], AX.X))
                link(nc.vector.tensor_scalar(var[:], var[:], 1.0 / D, EPS, ALU.mult, ALU.add))
                dve.sem_inc(var_ready, 1)
                dve.wait_ge(rstd_ready, k + 1)
                link(nc.vector.tensor_tensor(dst, work[:], bc(rstd[:, :, None], b3), ALU.mult))
                dve.sem_inc(ready, 1)

            dve.wait_ge(x_in, 16)
            norm(s.x[:], s.xn[:], 0, xn_ready)
            norm(s.xn[:], work[:], 1, xa_ready)
            for g in range(DG):
                dve.wait_ge(proj_copied, 4 * (g + 1))
                dve.wait_ge(pads_ready, 1)
                link(nc.vector.tensor_scalar(xc[:, g], xp[:, g, :, 0:L], s.taps[:, g, 0:1], None, ALU.mult))
                for k in range(1, KC):
                    link(nc.vector.scalar_tensor_tensor(out=xc[:, g], in0=xp[:, g, :, k:k + L], scalar=s.taps[:, g, k:k + 1],
                                                        in1=xc[:, g], op0=ALU.mult, op1=ALU.add))
                dve.sem_inc(conv_done, 1)
            dve.wait_ge(score_done, 1)
            link(nc.vector.tensor_copy(s.scores[:].rearrange("p t e -> p (t e)"), bank(4)[:, 0:8 * NT]))
            dve.sem_inc(scores_copied, 1)
            for c in range(NCH):
                cols = slice(c * CH, (c + 1) * CH)
                dve.wait_ge(bc_copied, 2 * c + 1)
                link(nc.vector.tensor_tensor(bcr[:, cols], bank(4 + c % 2)[0:96, :], s.bc3[:, cols], ALU.subtract))
                link(nc.vector.tensor_copy(bcm[:, cols], bcr[:, cols]))
                link(nc.vector.tensor_tensor(bcl[:, cols], bcr[:, cols], bcm[:, cols], ALU.subtract))
                nc.vector.tensor_copy(s.bc3[32:64, cols], bcm[32:64, cols])
                link(nc.vector.tensor_copy(s.bc3[64:96, cols], bcl[64:96, cols]))
                dve.sem_inc(bc_copied, 1)
            for i in range(DG * NCH):
                g, c = i // NCH, i % NCH
                h = i % 2
                cols = slice(c * CH, (c + 1) * CH)
                dve.wait_ge(exp_done, i + 1)
                link(nc.vector.tensor_scalar(spw[:, h], spe[:, h], 1.0, None, ALU.add))
                dve.sem_inc(one_done, 1)
                link(nc.vector.scalar_tensor_tensor(out=spc[:, h], in0=spw[:, h], scalar=-1.0, in1=spe[:, h],
                                                    op0=ALU.add, op1=ALU.subtract))
                link(nc.vector.tensor_scalar(spr[:, h], bank(h)[:], s.vec[:, 4 + g:5 + g], 0.0, ALU.add, ALU.max))
                link(nc.vector.tensor_tensor(spr[:, h], spr[:, h], spc[:, h], ALU.subtract))
                dve.wait_ge(ln_done, i + 1)
                nc.vector.tensor_tensor(s.delta[:, g, cols], spr[:, h], spl[:, h], ALU.add).then_inc(delta_ready, 1)

        @block.scalar
        def _(act):
            a = Tally(act_done)
            for c in range(NCH):
                act.wait_ge(tr_done, c + 1)
                nc.scalar.activation(s.xnT[:, c * CH:(c + 1) * CH], bank(c)[:], ACT.Copy).then_inc(tr_copied, 1)
            for c in range(NCH):
                act.wait_ge(w_in, 16 * NW)
                act.wait_ge(tr_done, NCH + c + 1)
                nc.scalar.activation(xaT[:, c * CH:(c + 1) * CH], bank(4 + c)[:], ACT.Identity,
                                     scale=s.vec[:, 0:1], bias=s.vec[:, 1:2]).then_inc(tr_copied, 1)
            for i in range(2 * DG * NCH):
                q, c = i // NCH, i % NCH
                act.wait_ge(proj_done, i + 1)
                if q < DG:
                    b, l0 = c // (NCH // B), c % (NCH // B) * CH
                    nc.scalar.activation(xp[:, q, b, KC - 1 + l0:KC - 1 + l0 + CH], bank(i % 4)[:], ACT.Copy).then_inc(proj_copied, 1)
                else:
                    nc.scalar.activation(s.zs[:, q - DG, c * CH:(c + 1) * CH], bank(i % 4)[:], ACT.Silu).then_inc(proj_copied, 1)
            for g in range(DG):
                act.wait_ge(conv_done, g + 1)
                nc.scalar.activation(s.u[:, g], xc[:, g].rearrange("p b l -> p (b l)"), ACT.Silu, bias=s.vec[:, 2 + g:3 + g]).then_inc(u_ready, 1)
            a.by(nc.scalar.activation(s.A[:], s.A[:], ACT.Exp))
            act.wait_ge(act_done, a.n)
            a.by(nc.scalar.mul(s.A[:], s.A[:], -1.0))
            for c in range(NCH):
                cols = slice(c * CH, (c + 1) * CH)
                act.wait_ge(dbc_done, 2 * c + 1)
                nc.scalar.activation(draw[:, cols], bank(6 + c % 2)[0:R, :], ACT.Copy).then_inc(draw_copied, 1)
                act.wait_ge(dbc_done, 2 * c + 2)
                nc.scalar.activation(s.bc3[:, cols], bank(4 + c % 2)[0:96, :], ACT.Copy).then_inc(bc_copied, 1)
                act.wait_ge(bc_copied, 2 * c + 2)
            for i in range(DG * NCH):
                g, h = i // NCH, i % 2
                act.wait_ge(dt_done, i + 1)
                if i >= 2:
                    act.wait_ge(delta_ready, i - 1)
                nc.scalar.activation(spl[:, h], bank(h)[:], ACT.Abs, bias=s.vec[:, 4 + g:5 + g]).then_inc(abs_done, 1)
                act.wait_ge(abs_done, i + 1)
                nc.scalar.activation(spe[:, h], spl[:, h], ACT.Exp, scale=-1.0).then_inc(exp_done, 1)
                act.wait_ge(one_done, i + 1)
                nc.scalar.activation(spl[:, h], spw[:, h], ACT.Ln).then_inc(ln_done, 1)

        @block.tensor
        def _(pe):
            pe.wait_ge(w_in, 16 * NW)
            for k, (src, ready) in enumerate(((s.xn, xn_ready), (work, xa_ready))):
                pe.wait_ge(ready, 1)
                for c in range(NCH):
                    for q in range(4):
                        last = nc.tensor.transpose(bank(4 * k + c)[:, q * P:(q + 1) * P], src[:, 4 * c + q, :], s.ident[:])
                    last.then_inc(tr_done, 1)
            for i in range(2 * DG * NCH):
                q, c = i // NCH, i % NCH
                pe.wait_ge(tr_copied, NCH + c + 1 if q == 0 else 2 * NCH)
                if i >= 4:
                    pe.wait_ge(proj_copied, i - 3)
                nc.tensor.matmul(bank(i % 4)[:], in_w[:, q * P:(q + 1) * P], xaT[:, c * CH:(c + 1) * CH],
                                 start=True, stop=True).then_inc(proj_done, 1)
            pe.wait_ge(tr_copied, 2 * NCH)
            for t in range(NT):
                last = nc.tensor.matmul(bank(4)[:, 8 * t:8 * t + 8], s.xnT[:, t * P:(t + 1) * P], s.gate_w[:], start=True, stop=True)
            last.then_inc(score_done, 1)
            for c in range(NCH):
                cols = slice(c * CH, (c + 1) * CH)
                pe.wait_ge(u_ready, DG)
                pe.wait_ge(scores_copied, 1)
                if c >= 2:
                    pe.wait_ge(draw_copied, c - 1)
                    pe.wait_ge(bc_copied, 2 * (c - 1))
                for g in range(DG):
                    last = nc.tensor.matmul(bank(6 + c % 2)[0:R, :], xw[:, g, :], s.u[:, g, cols], start=(g == 0), stop=(g == DG - 1))
                last.then_inc(dbc_done, 1)
                for g in range(DG):
                    last = nc.tensor.matmul(bank(4 + c % 2)[0:96, :], xbc[:, g, :], s.u[:, g, cols], start=(g == 0), stop=(g == DG - 1))
                last.then_inc(dbc_done, 1)
            for i in range(DG * NCH):
                g, c, h = i // NCH, i % NCH, i % 2
                pe.wait_ge(draw_copied, NCH)
                pe.wait_ge(proj_copied, 2 * DG * NCH)
                if i >= 2:
                    pe.wait_ge(delta_ready, i - 1)
                nc.tensor.matmul(bank(h)[:], dtw[:, g * P:(g + 1) * P], draw[:, c * CH:(c + 1) * CH],
                                 start=True, stop=True).then_inc(dt_done, 1)


SLOTS = 2 * T // P + 8


def count_before(nc, s, dve, link, mask, counted, tot, incl, keep, pos, rank_bank, total_bank, E=8):
    dve.wait_ge(counted, 1)
    link(nc.vector.tensor_copy(tot[:], total_bank.rearrange("p (t e) -> p e t", e=E)))
    link(nc.vector.tensor_tensor_scan(incl[:].rearrange("p e t -> p (e t)"), keep[:].rearrange("p e t -> p (e t)"),
                                      tot[:].rearrange("p e t -> p (e t)"), 0.0, ALU.mult, ALU.add))
    link(nc.vector.tensor_tensor(tot[:], incl[:], tot[:], ALU.subtract))
    link(nc.vector.tensor_tensor(pos[:], rank_bank.rearrange("p (t e) -> p t e", e=E), tot[:].rearrange("p e t -> p t e"), ALU.add))


def route(nc, s, I):
    sem = s.sem
    consts, dve_done = sem("route_constants"), sem("route_dve")
    diff_ready, e2_ready, mask_ready, counted = sem("gap_ready"), sem("gap_exp"), sem("mask_ready"), sem("counted")
    pos_ready, zero_ready, zeroed, scattered = sem("positions_ready"), sem("zeros_ready"), sem("rows_zeroed"), sem("rows_scattered")
    weights_in = s.expert_w_in
    bank = s.bank
    with ExitStack() as ctx:
        def sb(name, shape, dt=F32):
            return ctx.enter_context(nc.sbuf_tensor(name, shape, dt))

        before = sb("before", [P, P])
        every = sb("every", [P, P])
        slot_no = sb("slot_no", [P, SLOTS])
        exp_no = sb("expert_no", [P, 8])
        top = sb("top", [P, NT, 8])
        idx = sb("top_index", [P, NT, 8], U32)
        idf = sb("top_index_f", [P, NT, 2])
        gap = sb("gap", [P, NT])
        one = sb("one_hot", [P, 2, NT, 8])
        mask = sb("mask", [P, NT, 8])
        tot = sb("totals", [P, 8, NT])
        incl = sb("inclusive", [P, 8, NT])
        keep = sb("keep", [P, 8, NT])
        pos = sb("pos", [P, NT, 8])
        picked = sb("picked", [P, NT, 8])
        posf = sb("pos_f", [P, 2, NT])
        tiles = sb("expert_tiles", [P, 8])
        tiles_i = sb("expert_tiles_i", [P, 8], I32)
        ends = sb("expert_ends", [P, 8])
        ones8 = sb("ones8", [P, 8])
        past = sb("slots_past", [P, SLOTS, 8])
        slot_f = sb("slot_expert_f", [P, SLOTS])
        zeros = sb("zeros", [P, 1024])
        block = ctx.enter_context(nc.Block())
        ROWS = SLOTS * P // 1024 * D

        @block.sync
        def _(sp):
            for dst, src in ((before[:], I["before"]), (every[:], I["every"]), (slot_no[:], I["slot_numbers"]), (exp_no[:], I["expert_numbers"])):
                sp.dma_start(dst, src).then_inc(consts, 16)
            sp.wait_ge(zero_ready, 1)
            flat = s.rows_in.rearrange("(c p q) d -> c p (q d)", p=P, q=8)
            for c in range(SLOTS // 8):
                sp.dma_start(flat[c], zeros[:]).then_inc(zeroed, 16)
            for dst, src in ((s.w1[:], I["w1_t"]), (s.w3[:], I["w3_t"]), (s.w2[:], I["w2_t"])):
                sp.dma_start(dst, src).then_inc(weights_in, 16)

        @block.tensor
        def _(pe):
            pe.wait_ge(consts, 64)
            pe.wait_ge(mask_ready, 1)
            flat = mask[:].rearrange("p t e -> p (t e)")
            nc.tensor.matmul(bank(0)[:, 0:P], before[:], flat, start=True, stop=True)
            nc.tensor.matmul(bank(1)[:, 0:P], every[:], flat, start=True, stop=True).then_inc(counted, 1)

        @block.scalar
        def _(act):
            act.wait_ge(diff_ready, 1)
            nc.scalar.activation(s.wt[:, 1], gap[:], ACT.Exp).then_inc(e2_ready, 1)

        @block.vector
        def _(dve):
            t = Tally(dve_done)

            def link(ins):
                dve.wait_ge(dve_done, t.by(ins))

            nc.vector.memset(zeros[:], 0.0).then_inc(zero_ready, 1)
            t.by(nc.vector.memset(ones8[:], 1.0))
            link(nc.vector.memset(keep[:], 1.0))
            link(nc.vector.memset(keep[:, :, 0:1], 0.0))
            for i in range(NT):
                last = t.by(nc.vector.max(top[:, i, :], s.scores[:, i, :]))
            dve.wait_ge(dve_done, last)
            for i in range(NT):
                last = t.by(nc.vector.max_index(idx[:, i, :], top[:, i, :], s.scores[:, i, :]))
            nc.vector.tensor_tensor(gap[:], top[:, :, 1], top[:, :, 0], ALU.subtract).then_inc(diff_ready, 1)
            dve.wait_ge(dve_done, last)
            dve.wait_ge(consts, 64)
            link(nc.vector.tensor_copy(idf[:], idx[:, :, 0:2]))
            full = [P, NT, 8]
            for k in range(2):
                last = t.by(nc.vector.tensor_tensor(one[:, k], bc(idf[:, :, k:k + 1], full), bc(exp_no[:, None, :], full), ALU.is_equal))
            dve.wait_ge(dve_done, last)
            nc.vector.tensor_tensor(mask[:], one[:, 0], one[:, 1], ALU.add).then_inc(mask_ready, 1)
            dve.wait_ge(e2_ready, 1)
            link(nc.vector.tensor_scalar(gap[:], s.wt[:, 1], 1.0, None, ALU.add))
            link(nc.vector.reciprocal(s.wt[:, 0], gap[:]))
            link(nc.vector.tensor_tensor(s.wt[:, 1], s.wt[:, 1], s.wt[:, 0], ALU.mult))
            count_before(nc, s, dve, link, mask, counted, tot, incl, keep, pos, bank(0)[:, 0:P], bank(1)[:, 0:P])
            link(nc.vector.tensor_scalar(tiles_i[:], incl[:, :, NT - 1], float(P - 1), None, ALU.add))
            link(nc.vector.tensor_single_scalar(tiles_i[:], tiles_i[:], 7, ALU.arith_shift_right))
            link(nc.vector.tensor_copy(tiles[:], tiles_i[:]))
            link(nc.vector.tensor_tensor_scan(ends[:], ones8[:], tiles[:], 0.0, ALU.mult, ALU.add))
            link(nc.vector.tensor_tensor(tiles[:], ends[:], tiles[:], ALU.subtract))
            link(nc.vector.tensor_scalar(tiles[:], tiles[:], float(P), None, ALU.mult))
            link(nc.vector.tensor_tensor(pos[:], pos[:], bc(tiles[:, None, :], full), ALU.add))
            for k in range(2):
                link(nc.vector.tensor_tensor(picked[:], pos[:], one[:, k], ALU.mult))
                link(nc.vector.reduce_sum(posf[:, k], picked[:], AX.X))
            link(nc.vector.tensor_copy(s.pos[:], posf[:]))
            dve.sem_inc(pos_ready, 1)
            wide = [P, SLOTS, 8]
            link(nc.vector.tensor_tensor(past[:], bc(slot_no[:, :, None], wide), bc(ends[:, None, :], wide), ALU.is_ge))
            link(nc.vector.reduce_sum(slot_f[:], past[:], AX.X))
            link(nc.vector.tensor_scalar(s.slot_e[:], slot_f[:], 7.0, None, ALU.min))

        @block.gpsimd
        def _(pool):
            pool.wait_ge(pos_ready, 1)
            pool.wait_ge(zeroed, 16 * (SLOTS // 8))
            for i in range(NT):
                for k in range(2):
                    nc.gpsimd.indirect_dma_start(out=s.rows_in, out_offset=bass.IndirectOffsetOnAxis(ap=s.pos[:, k, i:i + 1], axis=0),
                                                 in_=s.xn[:, i, :], in_offset=None,
                                                 bounds_check=SLOTS * P - 1).then_inc(scattered, 16)
            pool.wait_ge(scattered, 32 * NT)


SQ = 512
ROUNDS = T // SQ


def selective_scan(nc, s, I):
    sem = s.sem
    sel_in, zeroed = sem("selectors_loaded"), sem("carry_zeroed")
    B_ready, C_ready, C_copied = sem("B_spread"), sem("C_spread"), sem("C_copied")
    dA_ready, dbu_done, h_done = sem("dA_ready"), sem("dBu_done"), sem("h_done")
    carry_done, prod_done, added = sem("carry_done"), sem("product_done"), sem("product_added")
    y_read, gated = sem("y_read"), sem("y_gated")
    bank = s.bank
    with ExitStack() as ctx:
        def sb(name, shape, dt=F32):
            return ctx.enter_context(nc.sbuf_tensor(name, shape, dt))

        sel = sb("selectors", [96, 2, NS, P], BF16)
        dA = sb("dA", [P, 2, DG, SQ])
        dbu = sb("dBu", [P, 2, DG, SQ])
        h = sb("h", [P, 2, DG, SQ])
        prod = sb("products", [P, 2, DG, SQ])
        Cs = sb("C_in_sbuf", [P, 2, SQ])
        carry = sb("carry", [P, NS, DG])
        yt = sb("y_skip", [P, DG, SQ])
        block = ctx.enter_context(nc.Block())
        Bb, Cb, Yb = (0, 1), (2, 3), (4, 5)

        @block.sync
        def _(sp):
            sp.dma_start(sel[:], I["selectors"]).then_inc(sel_in, 16)

        @block.tensor
        def _(pe):
            pe.sem_inc(added, 2)
            pe.wait_ge(sel_in, 16)
            with pe.Fori(0, ROUNDS) as r:
                cols = bass.ts(r, SQ)

                def add_up(n):
                    pe.wait_ge(prod_done, r * NS + n + 3)
                    for g in range(DG):
                        last = nc.tensor.matmul(bank(Yb[g]), s.ident[:], prod[:, n % 2, g, :], start=(n == 0), stop=(n == NS - 1))
                    last.then_inc(added, 1)

                for n in range(NS):
                    m, k = n % 2, r * NS + n
                    pe.wait_ge(dbu_done, k + 1)
                    nc.tensor.matmul(bank(Bb[m]), sel[:, 0, n, :], s.bc3[:, cols], start=True, stop=True).then_inc(B_ready, 1)
                    pe.wait_ge(C_copied, k + 1)
                    nc.tensor.matmul(bank(Cb[m]), sel[:, 1, n, :], s.bc3[:, cols], start=True, stop=True).then_inc(C_ready, 1)
                    if n == 1:
                        pe.wait_ge(y_read, r + 1)
                    if n >= 1:
                        add_up(n - 1)
                add_up(NS - 1)

        @block.scalar
        def _(act):
            act.sem_inc(C_copied, 2)
            with act.Fori(0, ROUNDS) as r:
                cols = bass.ts(r, SQ)
                for n in range(NS):
                    m, k = n % 2, r * NS + n
                    act.wait_ge(h_done, k + 1)
                    act.wait_ge(prod_done, k + 1)
                    act.wait_ge(C_ready, k + 1)
                    nc.scalar.activation(Cs[:, m, :], bank(Cb[m]), ACT.Copy).then_inc(C_copied, 1)
                    for g in range(DG):
                        last = nc.scalar.activation(dA[:, m, g, :], s.delta[:, g, cols], ACT.Exp, scale=s.A[:, g, n:n + 1])
                    last.then_inc(dA_ready, 1)

        @block.vector
        def _(dve):
            dve.sem_inc(dbu_done, 2)
            dve.sem_inc(h_done, 2)
            dve.sem_inc(y_read, 1)
            def a_round(r, first):
                cols = bass.ts(r, SQ)
                if first:
                    dve.wait_ge(h_done, r * NS + 2)
                    nc.vector.memset(carry[:], 0.0).then_inc(zeroed, 1)

                def input_of(n):
                    m, k = n % 2, r * NS + n
                    dve.wait_ge(B_ready, k + 1)
                    dve.wait_ge(h_done, k + 1)
                    nc.vector.tensor_tensor(dbu[:, m], s.du[:, :, cols], bc(bank(Bb[m])[:, None, :], [P, DG, SQ]),
                                            ALU.mult).then_inc(dbu_done, 1)

                def carry_of(n):
                    k = r * NS + n
                    dve.wait_ge(h_done, k + 3)
                    nc.vector.tensor_copy(carry[:, n, :], h[:, n % 2, :, SQ - 1]).then_inc(carry_done, 1)

                input_of(0)
                for n in range(NS):
                    m, k = n % 2, r * NS + n
                    if n + 1 < NS:
                        input_of(n + 1)
                    if first and n == 0:
                        dve.wait_ge(zeroed, b + 1)
                    dve.wait_ge(dbu_done, k + 3)
                    dve.wait_ge(dA_ready, k + 1)
                    dve.wait_ge(prod_done, k + 1)
                    if n >= 2:
                        dve.wait_ge(carry_done, k - 1)
                    for g in range(DG):
                        last = nc.vector.tensor_tensor_scan(h[:, m, g, :], dA[:, m, g, :], dbu[:, m, g, :], carry[:, n, g:g + 1],
                                                            ALU.mult, ALU.add)
                    last.then_inc(h_done, 1)
                    if n:
                        carry_of(n - 1)
                carry_of(NS - 1)
                dve.wait_ge(carry_done, (r + 1) * NS)
                dve.wait_ge(added, (r + 1) * NS + 2)
                for g in range(DG):
                    last = nc.vector.scalar_tensor_tensor(out=yt[:, g, :], in0=s.u[:, g, cols], scalar=s.vec[:, 6 + g:7 + g],
                                                          in1=bank(Yb[g]), op0=ALU.mult, op1=ALU.add)
                last.then_inc(y_read, 1)
                dve.wait_ge(y_read, r + 2)
                nc.vector.tensor_tensor(s.u[:, :, cols], yt[:], s.zs[:, :, cols], ALU.mult).then_inc(gated, 1)
                dve.wait_ge(gated, r + 1)

            with dve.Fori(0, B) as b:
                for half in range(ROUNDS // B):
                    a_round(b * (ROUNDS // B) + half, half == 0)

        @block.gpsimd
        def _(pool):
            pool.sem_inc(prod_done, 2)
            with pool.Fori(0, ROUNDS) as r:
                for n in range(NS):
                    m, k = n % 2, r * NS + n
                    pool.wait_ge(h_done, k + 3)
                    pool.wait_ge(C_copied, k + 3)
                    pool.wait_ge(added, k + 1)
                    nc.gpsimd.tensor_tensor(prod[:, m], h[:, m], bc(Cs[:, m, None, :], [P, DG, SQ]), ALU.mult).then_inc(prod_done, 1)


def experts(nc, s, I):
    sem = s.sem
    rows_in = [sem(f"slot_rows_in_{m}") for m in range(2)]
    xt_done, xt_copied = sem("slot_xT_done"), sem("slot_xT_copied")
    up_done, silu_done, g_done = sem("slot_up_done"), sem("slot_silu_done"), sem("slot_gated")
    gt_done, gt_copied, y_done, y_copied = sem("slot_gT_done"), sem("slot_gT_copied"), sem("slot_y_done"), sem("slot_y_copied")
    y_out = [sem(f"slot_y_out_{m}") for m in range(2)]
    bank = s.bank
    with ExitStack() as ctx:
        def sb(name, shape, dt=F32):
            return ctx.enter_context(nc.sbuf_tensor(name, shape, dt))

        xs = sb("slot_x", [P, 2, D])
        xsT = sb("slot_xT", [P, 2, P])
        sg = sb("slot_silu", [P, 2, 512])
        gg = sb("slot_g", [P, 2, 512])
        gT = sb("slot_gT", [P, 2, 512])
        ys = sb("slot_y", [P, 2, D])
        block = ctx.enter_context(nc.Block())

        @block.sync
        def _(sp):
            with sp.Fori(0, SLOTS // 2) as q:
                for m in range(2):
                    k = q * 2 + m
                    sp.wait_ge(xt_done, k + 1)
                    sp.dma_start(xs[:, m, :], s.rows_in[bass.ts(k, P), :]).then_inc(rows_in[m], 16)

        @block.gpsimd
        def _(pool):
            with pool.Fori(0, SLOTS // 2) as q:
                for m in range(2):
                    k = q * 2 + m
                    pool.wait_ge(y_copied, k + 3)
                    pool.dma_start(s.rows_out[bass.ts(k, P), :], ys[:, m, :]).then_inc(y_out[m], 16)
            for m in range(2):
                pool.wait_ge(y_out[m], 16 * (SLOTS // 2))

        @block.tensor
        def _(pe):
            pe.sem_inc(xt_done, 2)
            pe.sem_inc(y_done, 2)
            pe.sem_inc(up_done, 2)
            pe.sem_inc(gt_done, 2)
            pe.wait_ge(s.expert_w_in, 48)
            with pe.Fori(0, SLOTS // 2) as q:
                for m in range(2):
                    k = q * 2 + m
                    e = pe.value_load(s.slot_e[0:1, bass.ts(k, 1)], min_val=0, max_val=7)
                    pe.wait_ge(rows_in[m], 16 * (q + 1))
                    pe.wait_ge(y_copied, k + 1)
                    nc.tensor.transpose(bank(m)[:, 0:P], xs[:, m, :], s.ident[:]).then_inc(xt_done, 1)
                    pe.wait_ge(xt_copied, k + 3)
                    pe.wait_ge(g_done, k + 1)
                    nc.tensor.matmul(bank(2 + m), xsT[:, m, :], s.w1[:, e, :], start=True, stop=True)
                    nc.tensor.matmul(bank(4 + m), xsT[:, m, :], s.w3[:, e, :], start=True, stop=True).then_inc(up_done, 1)
                    pe.wait_ge(g_done, k + 3)
                    pe.wait_ge(gt_copied, k + 1)
                    for c in range(4):
                        last = nc.tensor.transpose(bank(6 + m)[:, c * P:(c + 1) * P], gg[:, m, c * P:(c + 1) * P], s.ident[:])
                    last.then_inc(gt_done, 1)
                    pe.wait_ge(gt_copied, k + 3)
                    for c in range(4):
                        last = nc.tensor.matmul(bank(m)[:, 0:D], gT[:, m, c * P:(c + 1) * P], s.w2[:, e, c, :], start=(c == 0), stop=(c == 3))
                    last.then_inc(y_done, 1)

        @block.scalar
        def _(act):
            act.sem_inc(xt_copied, 2)
            act.sem_inc(silu_done, 2)
            act.sem_inc(gt_copied, 2)
            with act.Fori(0, SLOTS // 2) as q:
                for m in range(2):
                    k = q * 2 + m
                    act.wait_ge(xt_done, k + 3)
                    act.wait_ge(up_done, k + 1)
                    nc.scalar.activation(xsT[:, m, :], bank(m)[:, 0:P], ACT.Copy).then_inc(xt_copied, 1)
                    act.wait_ge(g_done, k + 1)
                    act.wait_ge(up_done, k + 3)
                    nc.scalar.activation(sg[:, m], bank(2 + m), ACT.Silu).then_inc(silu_done, 1)
                    act.wait_ge(gt_done, k + 3)
                    act.wait_ge(y_done, k + 1)
                    nc.scalar.activation(gT[:, m], bank(6 + m), ACT.Copy).then_inc(gt_copied, 1)

        @block.vector
        def _(dve):
            dve.sem_inc(g_done, 2)
            dve.sem_inc(y_copied, 2)

            def pair(q, first):
                for m in range(2):
                    k = q * 2 + m
                    dve.wait_ge(silu_done, k + 3)
                    dve.wait_ge(gt_done, k + 1)
                    nc.vector.tensor_tensor(gg[:, m], sg[:, m], bank(4 + m), ALU.mult).then_inc(g_done, 1)
                    dve.wait_ge(y_done, k + 3)
                    if not first:
                        dve.wait_ge(y_out[m], 16 * q)
                    nc.vector.tensor_copy(ys[:, m], bank(m)[:, 0:D]).then_inc(y_copied, 1)

            pair(0, True)
            with dve.Fori(1, SLOTS // 2) as q:
                pair(q, False)


def first_layer_out(nc, s, I):
    sem = s.sem
    w_in, gathered, o_done, o_added, dve_done = sem("out_w_loaded"), sem("rows_gathered"), sem("out_done"), sem("out_added"), sem("sum_dve")
    bank = s.bank
    with ExitStack() as ctx:
        def sb(name, shape, dt=F32):
            return ctx.enter_context(nc.sbuf_tensor(name, shape, dt))

        ow = sb("out_w_t", [P, DG, D])
        yr = sb("expert_rows", [P, 2, NT, D])
        block = ctx.enter_context(nc.Block())

        @block.sync
        def _(sp):
            sp.dma_start(ow[:], I["out_w_t"].rearrange("(g p) d -> p g d", p=P)).then_inc(w_in, 16)

        @block.gpsimd
        def _(pool):
            for i in range(NT):
                for k in range(2):
                    nc.gpsimd.indirect_dma_start(out=yr[:, k, i, :], out_offset=None, in_=s.rows_out,
                                                 in_offset=bass.IndirectOffsetOnAxis(ap=s.pos[:, k, i:i + 1], axis=0),
                                                 bounds_check=SLOTS * P - 1).then_inc(gathered, 16)

        @block.tensor
        def _(pe):
            pe.wait_ge(w_in, 16)
            for i in range(NT):
                for g in range(DG):
                    last = nc.tensor.matmul(bank(i // 4)[:, i % 4 * P:(i % 4 + 1) * P], s.u[:, g, i * P:(i + 1) * P], ow[:, g, :],
                                            start=(g == 0), stop=(g == DG - 1))
                if i % 4 == 3:
                    last.then_inc(o_done, 1)

        @block.vector
        def _(dve):
            t = Tally(dve_done)

            def link(ins):
                dve.wait_ge(dve_done, t.by(ins))

            t.by(nc.vector.tensor_tensor(s.x[:], s.x[:], s.xn[:], ALU.add))
            for i in range(4):
                dve.wait_ge(o_done, i + 1)
                dve.wait_ge(dve_done, 1)
                v = s.x[:, 4 * i:4 * i + 4, :]
                t.by(nc.vector.tensor_tensor(v, v, bank(i).rearrange("p (t d) -> p t d", t=4), ALU.add))
            dve.wait_ge(gathered, 32 * NT)
            for k in range(2):
                link(nc.vector.tensor_tensor(yr[:, k], yr[:, k], bc(s.wt[:, k, :, None], [P, NT, D]), ALU.mult))
                link(nc.vector.tensor_tensor(s.x[:], s.x[:], yr[:, k], ALU.add))


NH = 8
DH = D // NH
HG = 4
TPB = L // P
Q_PARTS = ((0, 0, 1), (0, 2, 1))
K_PARTS = ((0, 1, 0), (2, 0, 1))
SCALE = float(D) ** -0.5


def attention_operands(nc, s, I):
    sem = s.sem
    consts, dve_done, act_done = sem("l1_constants"), sem("l1_dve"), sem("l1_act")
    var_ready, rstd_ready = sem("l1_var_ready"), sem("l1_rstd_ready")
    xb_ready, xq_ready, half_ready = sem("xb_ready"), sem("xq_ready"), sem("l1_half_ready")
    tr_done, tr_copied, pad_ready = sem("l1_transposed"), sem("l1_transposes_copied"), sem("xqT_padded")
    tok_done, tok_read = sem("token_projections"), sem("token_projections_read")
    q_done, k_done, q_biased, k_biased = sem("q_done"), sem("k_done"), sem("q_biased"), sem("k_biased")
    psi_done, turned, his, rest, mids, parts_ready = (
        sem("psi_done"), sem("turned"), sem("high_parts"), sem("rests"), sem("middle_parts"), sem("parts_ready"))
    parts_out = [sem(f"parts_out_{m}") for m in range(2)]
    bias_ready = sem("l1_biases")
    bank = s.bank
    with ExitStack() as ctx:
        def sb(name, shape, dt=F32):
            return ctx.enter_context(nc.sbuf_tensor(name, shape, dt))

        work = sb("l1_work", [P, NT, D])
        sq = sb("l1_squares", [P, NT, D])
        xb = sb("xb", [P, NT, D])
        mean, var, rstd, half = (sb(n, [P, NT]) for n in ("l1_mean", "l1_var", "l1_rstd", "l1_half"))
        xqT = sb("xqT", [P, T + 1])
        hw = sb("head_w", [P, 5, D])
        turns = sb("turns", [P, 4, L])
        rows = sb("bias_rows", [P, 4, D])
        qtok = sb("q_tok", [P, D])
        ktok = sb("k_tok", [P, D])
        full = sb("operands", [P, 4, CH])
        vq = sb("q_plus_v", [P, T + 1])
        t2 = sb("turn_work", [P, CH])
        rem = sb("remainder", [P, 4, CH])
        part = sb("parts", [P, 2, 3, 4, CH], BF16)
        bias2 = sb("l1_bias", [P, 2])
        corner = sb("last_token", [P, 2], BF16)
        block = ctx.enter_context(nc.Block())

        @block.sync
        def _(sp):
            for dst, src in ((hw[:], I["head_w"]), (rows[:], I["rows"][0:4].partition_broadcast(P)), (turns[:], I["turns"]),
                             (corner[:], I["masks"][:, 4 * P:4 * P + 2])):
                sp.dma_start(dst, src).then_inc(consts, 16)
            n = [0, 0]
            for c in range(NCH):
                b, cc = c // 2, c % 2
                sp.wait_ge(parts_ready, c + 1)
                for g in range(NH // HG):
                    src = part[64 * g:64 * g + 64, c % 2]
                    for ps in range(2):
                        for slot in range(3):
                            pq, pk = Q_PARTS[ps][slot], K_PARTS[ps][slot]
                            for which in range(2):
                                to = s.q_stacks[b, g, :, ps, which, :, cc * CH:(cc + 1) * CH]
                                at = 32 * slot
                                sp.dma_start(to[at:at + DH].rearrange("d h c -> h d c"), src[:, pq, 0]).then_inc(parts_out[c % 2], 16)
                                sp.dma_start(to[at + DH:at + 2 * DH].rearrange("d h c -> h d c"), src[:, pq, 1 + which]).then_inc(parts_out[c % 2], 16)
                            to = s.k_stacks[b, g, :, ps, :, cc * CH:(cc + 1) * CH]
                            sp.dma_start(to[DH * slot:DH * slot + DH].rearrange("d h c -> h d c"), src[:, pk, 3]).then_inc(parts_out[c % 2], 16)
                            n[c % 2] += 80
            for m in range(2):
                sp.wait_ge(parts_out[m], n[m])

        @block.gpsimd
        def _(pool):
            nc.gpsimd.memset(half[:], -0.5).then_inc(half_ready, 1)
            nc.gpsimd.memset(s.vals[:], 0.0).then_inc(half_ready, 1)
            pool.wait_ge(half_ready, 2)
            nc.gpsimd.memset(s.vals[:, :, :, DH:DH + 1], 1.0).then_inc(half_ready, 1)
            nc.gpsimd.memset(vq[:, T:T + 1], 0.0).then_inc(pad_ready, 1)
            nc.gpsimd.memset(xqT[:, T:T + 1], 0.0).then_inc(pad_ready, 1)
            for k in range(2):
                pool.wait_ge(var_ready, k + 1)
                nc.gpsimd.tensor_tensor(rstd[:], var[:], half[:], ALU.pow).then_inc(rstd_ready, 1)

        @block.vector
        def _(dve):
            t = Tally(dve_done)

            def link(ins):
                dve.wait_ge(dve_done, t.by(ins))

            def norm(src, dst, k, ready):
                b3 = [P, NT, D]
                link(nc.vector.reduce_sum(mean[:], src, AX.X))
                link(nc.vector.tensor_scalar(mean[:], mean[:], 1.0 / D, None, ALU.mult))
                link(nc.vector.tensor_tensor(work[:], src, bc(mean[:, :, None], b3), ALU.subtract))
                link(nc.vector.tensor_tensor(sq[:], work[:], work[:], ALU.mult))
                link(nc.vector.reduce_sum(var[:], sq[:], AX.X))
                link(nc.vector.tensor_scalar(var[:], var[:], 1.0 / D, EPS, ALU.mult, ALU.add))
                dve.sem_inc(var_ready, 1)
                dve.wait_ge(rstd_ready, k + 1)
                link(nc.vector.tensor_tensor(dst, work[:], bc(rstd[:, :, None], b3), ALU.mult))
                dve.sem_inc(ready, 1)

            norm(s.x[:], xb[:], 0, xb_ready)
            norm(xb[:], work[:], 1, xq_ready)
            dve.wait_ge(consts, 64)
            t.by(nc.vector.tensor_tensor(rows[:, 0], rows[:, 0], rows[:, 1], ALU.add))
            t.by(nc.vector.tensor_tensor(bias2[:, 0:1], s.vec[:, 10:11], s.vec[:, 12:13], ALU.add))
            link(nc.vector.tensor_tensor(bias2[:, 1:2], s.vec[:, 10:11], s.vec[:, 13:14], ALU.add))
            dve.sem_inc(bias_ready, 1)
            dve.wait_ge(half_ready, 3)
            for i in range(NT):
                dve.wait_ge(tok_done, i + 1)
                y = bank(i % 2)
                t.by(nc.vector.tensor_tensor(qtok[:], y[:, 0:D], rows[:, 0], ALU.add))
                t.by(nc.vector.tensor_tensor(ktok[:], y[:, D:2 * D], rows[:, 2], ALU.add))
                t.by(nc.vector.tensor_tensor(s.v_next[:, i, :], y[:, 2 * D:3 * D], rows[:, 3], ALU.add))
                link(nc.vector.tensor_tensor(s.vals[:, i, :, 0:DH], y[:, 3 * D:4 * D].rearrange("p (h d) -> p h d", h=NH),
                                             rows[:, 3].rearrange("p (h d) -> p h d", h=NH), ALU.add))
                dve.sem_inc(tok_read, 1)
                link(nc.vector.tensor_tensor(qtok[:], qtok[:], ktok[:], ALU.mult))
                link(nc.vector.reduce_sum(s.s3[:, i, :], qtok[:].rearrange("p (h d) -> p h d", h=NH), AX.X))
            for b in range(B):
                i = (b + 1) * TPB - 1
                link(nc.vector.tensor_tensor(s.s3[:, i, :], s.s3[:, i, :], bc(corner[:, 0:1], [P, NH]), ALU.add))
            for c in range(NCH):
                cc = slice(c % 2 * CH, (c % 2 + 1) * CH)
                dve.wait_ge(psi_done, c + 1)
                if c:
                    dve.wait_ge(his, c)
                    dve.wait_ge(parts_ready, c)
                for k in range(2):
                    link(nc.vector.tensor_tensor(full[:, 1 + k], bank(4 + 2 * k), turns[:, 2 * k, cc], ALU.mult))
                    link(nc.vector.tensor_tensor(t2[:], bank(5 + 2 * k), turns[:, 2 * k + 1, cc], ALU.mult))
                    link(nc.vector.tensor_tensor(full[:, 1 + k], full[:, 1 + k], t2[:], ALU.add))
                dve.sem_inc(turned, 1)
                dve.wait_ge(his, c + 1)
                link(nc.vector.tensor_tensor(rem[:], full[:], part[:, c % 2, 0], ALU.subtract))
                dve.sem_inc(rest, 1)
                dve.wait_ge(mids, c + 1)
                nc.vector.tensor_tensor(part[:, c % 2, 2], rem[:], part[:, c % 2, 1], ALU.subtract).then_inc(parts_ready, 1)

        @block.scalar
        def _(act):
            for c in range(NCH):
                act.wait_ge(tr_done, c + 1)
                nc.scalar.activation(s.xbT[:, c * CH:(c + 1) * CH], bank(c), ACT.Copy).then_inc(tr_copied, 1)
            for c in range(NCH):
                act.wait_ge(tr_done, NCH + c + 1)
                nc.scalar.activation(xqT[:, c * CH:(c + 1) * CH], bank(4 + c), ACT.Identity,
                                     scale=s.vec[:, 8:9], bias=s.vec[:, 9:10]).then_inc(tr_copied, 1)
            act.wait_ge(bias_ready, 1)
            for c in range(NCH):
                act.wait_ge(q_done, c + 1)
                nc.scalar.activation(vq[:, c * CH:(c + 1) * CH], bank(2), ACT.Identity, bias=bias2[:, 1:2]).then_inc(q_biased, 1)
            for c in range(NCH):
                act.wait_ge(q_done, NCH + c + 1)
                if c:
                    act.wait_ge(rest, c)
                nc.scalar.activation(full[:, 0], bank(2), ACT.Identity, bias=bias2[:, 0:1]).then_inc(act_done, 1)
                act.wait_ge(k_done, c + 1)
                nc.scalar.activation(full[:, 3], bank(3), ACT.Identity, bias=s.vec[:, 11:12]).then_inc(k_biased, 1)
                act.wait_ge(turned, c + 1)
                act.wait_ge(act_done, c + 1)
                act.wait_ge(k_biased, c + 1)
                if c >= 2:
                    act.wait_ge(parts_out[c % 2], 16 * 60)
                nc.scalar.activation(part[:, c % 2, 0], full[:], ACT.Copy).then_inc(his, 1)
                act.wait_ge(rest, c + 1)
                nc.scalar.activation(part[:, c % 2, 1], rem[:], ACT.Copy).then_inc(mids, 1)

        @block.tensor
        def _(pe):
            for k, (src, ready) in enumerate(((xb, xb_ready), (work, xq_ready))):
                pe.wait_ge(ready, 1)
                for c in range(NCH):
                    for q in range(4):
                        last = nc.tensor.transpose(bank(4 * k + c)[:, q * P:(q + 1) * P], src[:, 4 * c + q, :], s.ident[:])
                    last.then_inc(tr_done, 1)
            pe.wait_ge(tr_copied, 2 * NCH)
            pe.wait_ge(consts, 64)
            pe.wait_ge(pad_ready, 2)
            for i in range(NT):
                if i >= 2:
                    pe.wait_ge(tok_read, i - 1)
                y, now, nxt = bank(i % 2), xqT[:, i * P:(i + 1) * P], xqT[:, i * P + 1:(i + 1) * P + 1]
                nc.tensor.matmul(y[:, 0:D], now, hw[:, 0], start=True, stop=True)
                nc.tensor.matmul(y[:, D:3 * D], nxt, hw[:, 1:3].rearrange("p w d -> p (w d)"), start=True, stop=True)
                nc.tensor.matmul(y[:, 3 * D:4 * D], now, hw[:, 2], start=True, stop=True).then_inc(tok_done, 1)
            for c in range(NCH):
                if c:
                    pe.wait_ge(q_biased, c)
                nc.tensor.matmul(bank(2), hw[:, 0], xqT[:, c * CH:(c + 1) * CH], start=True, stop=True).then_inc(q_done, 1)
            pe.wait_ge(q_biased, NCH)
            for c in range(NCH):
                cols, nxt = slice(c * CH, (c + 1) * CH), slice(c * CH + 1, (c + 1) * CH + 1)
                if c:
                    pe.wait_ge(act_done, c)
                    pe.wait_ge(k_biased, c)
                    pe.wait_ge(turned, c)
                nc.tensor.matmul(bank(2), hw[:, 0], xqT[:, cols], start=True, stop=True).then_inc(q_done, 1)
                nc.tensor.matmul(bank(3), hw[:, 1], xqT[:, cols], start=True, stop=True).then_inc(k_done, 1)
                for k in range(2):
                    nc.tensor.matmul(bank(4 + 2 * k), hw[:, 3], vq[:, (cols, nxt)[k]], start=True, stop=True)
                    last = nc.tensor.matmul(bank(5 + 2 * k), hw[:, 4], vq[:, (cols, nxt)[k]], start=True, stop=True)
                last.then_inc(psi_done, 1)


UNITS = 2 * HG + 1
GROUPS = B * NH // HG
LOADS = 16 * 4


def attention(nc, s, I):
    sem = s.sem
    consts, ones_ready, v_copied = sem("attention_constants"), sem("ones_rows_ready"), sem("group_values_ready")
    first_in = [sem(f"stack_first_pass_{g}") for g in range(2)]
    second_in = [sem(f"stack_second_pass_{g}") for g in range(2)]
    max_in = [sem(f"max_rows_in_{g}") for g in range(2)]
    max_done, max_read = sem("max_scores_done"), sem("max_scores_read")
    mx_ready, split = sem("max_ready"), sem("max_split")
    score_done, exp_done, pv_done, pv2_done = sem("score_done"), sem("exp_done"), sem("pv_done"), sem("pv_diagonal_done")
    ctx_done, ctx_read, dve_done = sem("context_done"), sem("context_read"), sem("attention_dve")
    bank = s.bank
    PV, RING, MAXRING = (0, 1), (2, 3, 4), (5, 6, 7)
    with ExitStack() as ctx:
        def sb(name, shape, dt=F32):
            return ctx.enter_context(nc.sbuf_tensor(name, shape, dt))

        Q = sb("query_stacks", [99, 2, 2, 2, HG, L], BF16)
        K = sb("key_stacks", [99, 2, 2, HG, L], BF16)
        W = sb("exp_scores", [P, 2, HG, CH])
        W2 = sb("exp_diagonal", [P, 2, HG, P])
        V = sb("group_values", [P, 2, TPB, HG, 32])
        masks = sb("diagonal_masks", [P, 4 * P + 2], BF16)
        identb = sb("identity_bf16", [P, P], BF16)
        cm = sb("chunk_maxima", [P, TPB, HG, 3])
        mx = sb("row_maxima", [P, HG, TPB])
        mrest = sb("max_rest", [HG * TPB, P])
        mparts = sb("max_parts", [HG * TPB, 3, P], BF16)
        block = ctx.enter_context(nc.Block())

        def by_group(b, g, each, n):
            return b * (2 * each) + (g * each + n)

        STEP = TPB * UNITS
        MAXSTEP = STEP + 1
        FIRST, SECOND, FIRST_T, SECOND_T = (masks[:, q * P:(q + 1) * P] for q in range(4))

        @block.sync
        def _(sp):
            sp.dma_start(masks[:], I["masks"]).then_inc(consts, 16)
            sp.dma_start(identb[:], I["ident_bf"]).then_inc(consts, 16)
            for g in range(2):
                for ps in range(2):
                    for slot in range(3):
                        sp.dma_start(K[32 * slot + DH:32 * slot + 2 * DH, g, ps],
                                     I["sinusoids"][64 * g:64 * g + 64, K_PARTS[ps][slot], :].rearrange("(h m) c -> m h c", h=HG)).then_inc(consts, 16)
            with sp.Fori(0, B) as b:
                for g in range(2):
                    sp.wait_ge(ctx_done, b * 2 + g + 1)
                    for ps, done in enumerate((first_in[g], second_in[g])):
                        sp.dma_start(Q[0:96, g, ps], s.q_stacks[bass.ts(b, 1), g, :, ps].squeeze(0)).then_inc(done, 16)
                        for slot in range(3):
                            sp.dma_start(K[32 * slot:32 * slot + DH, g, ps],
                                         s.k_stacks[bass.ts(b, 1), g, DH * slot:DH * (slot + 1), ps].squeeze(0)).then_inc(done, 16)
                for g in range(2):
                    sp.wait_ge(split, b * 2 + g + 2)
                    for form in range(2):
                        for part in range(3):
                            sp.dma_start(Q[96 + part:97 + part, g, 0, form].rearrange("r h (t c) -> r (h t) c", t=TPB),
                                         mparts[:, part]).then_inc(max_in[g], 16)

        @block.gpsimd
        def _(pool):
            nc.gpsimd.memset(K[96:99, :, 0], 1.0).then_inc(ones_ready, 1)
            pool.wait_ge(ones_ready, 1)
            pool.sem_inc(v_copied, 1)
            with pool.Fori(0, B) as b:
                for g in range(2):
                    pool.wait_ge(ctx_done, b * 2 + g + 1)
                    pool.wait_ge(v_copied, b * 2 + g + 1)
                    nc.gpsimd.tensor_copy(V[:, g], s.vals[:, bass.ts(b, TPB), HG * g:HG * (g + 1), :]).then_inc(v_copied, 1)

        @block.tensor
        def _(pe):
            pe.sem_inc(ctx_done, 2)
            pe.sem_inc(pv_done, 2)
            pe.sem_inc(pv2_done, 2)
            pe.wait_ge(consts, 16 * 14)
            pe.wait_ge(ones_ready, 1)

            def max_unit(b, g, it, u):
                y = bank(MAXRING[u % 3])
                pe.wait_ge(max_read, by_group(b, g, MAXSTEP, max(it * UNITS + u + 1, 3)))
                a, z = it * P, (it + 1) * P

                def product(h, form, lo, hi, at, start, stop):
                    return nc.tensor.matmul(y[:, lo - at:hi - at], Q[0:96, g, 0, form, h, a:z], K[0:96, g, 0, h, lo:hi], start=start, stop=stop)

                if u == 0:
                    for h in range(HG):
                        nc.tensor.matmul(y[:, h * P:(h + 1) * P], identb[:], SECOND, start=True, stop=False)
                        last = product(h, 1, a, z, a - h * P, False, True)
                    last.then_inc(max_done, 1)
                    return
                h, c = (u - 1) % HG, (u - 1) // HG
                lo, hi = c * CH, (c + 1) * CH
                if lo <= a < hi:
                    nc.tensor.matmul(y[:, a - lo:z - lo], identb[:], FIRST, start=True, stop=False)
                    last = product(h, 0, a, z, lo, False, True)
                if lo < min(a, hi):
                    last = product(h, 0, lo, min(a, hi), lo, True, True)
                if max(z, lo) < hi:
                    last = product(h, 1, max(z, lo), hi, lo, True, lo > z)
                    if lo <= z:
                        last = nc.tensor.matmul(y[:, z - lo:z - lo + 1], identb[:], masks[:, 4 * P:4 * P + 1], start=False, stop=True)
                last.then_inc(max_done, 1)

            def max_turned(b, g):
                pe.wait_ge(mx_ready, by_group(b, g, 1, 2))
                nc.tensor.transpose(bank(MAXRING[0])[0:HG * TPB, 0:P], mx[:].rearrange("p h t -> p (h t)"), s.ident[:]).then_inc(max_done, 1)

            def score_unit(b, g, jt, u):
                y = bank(RING[u % 3])
                pe.wait_ge(exp_done, by_group(b, g, STEP, jt * UNITS + u + 1))
                a, z = jt * P, (jt + 1) * P

                def product(h, form, lo, hi, at, start, stop):
                    to = y[:, lo - at:hi - at]
                    nc.tensor.matmul(to, K[0:99, g, 0, h, a:z], Q[0:99, g, 0, form, h, lo:hi], start=start, stop=False)
                    return nc.tensor.matmul(to, K[0:96, g, 1, h, a:z], Q[0:96, g, 1, form, h, lo:hi], start=False, stop=stop)

                if u == 0:
                    for h in range(HG):
                        nc.tensor.matmul(y[:, h * P:(h + 1) * P], identb[:], SECOND_T, start=True, stop=False)
                        last = product(h, 1, a, z, a - h * P, False, True)
                    last.then_inc(score_done, 1)
                    return
                h, c = (u - 1) % HG, (u - 1) // HG
                lo, hi = c * CH, (c + 1) * CH
                if lo <= a < hi:
                    nc.tensor.matmul(y[:, a - lo:z - lo], identb[:], FIRST_T, start=True, stop=False)
                    last = product(h, 0, a, z, lo, False, True)
                if max(z, lo) < hi:
                    last = product(h, 0, max(z, lo), hi, lo, True, True)
                if lo < min(a, hi):
                    last = product(h, 1, lo, min(a, hi), lo, True, a > hi)
                    if a <= hi:
                        last = nc.tensor.matmul(y[:, a - 1 - lo:a - lo], identb[:], masks[:, 4 * P + 1:4 * P + 2], start=False, stop=True)
                last.then_inc(score_done, 1)

            def values(b, g, jt, c):
                pe.wait_ge(exp_done, by_group(b, g, STEP, jt * UNITS + 1 + HG * (c + 1) + 3))
                for h in range(HG):
                    last = nc.tensor.matmul(bank(PV[c])[32 * h:32 * h + 32, :], V[:, g, jt, h, :], W[:, c, h, :],
                                            start=(jt == 0), stop=(jt == TPB - 1))
                last.then_inc(pv_done, 1)

            def diagonal_values(g, jt):
                y, at = bank(PV[jt // 4]), jt % 4 * P
                for h in range(HG):
                    last = nc.tensor.matmul(y[32 * h:32 * h + 32, at:at + P], V[:, g, jt, h, :], W2[:, jt % 2, h, :], start=False, stop=False)
                last.then_inc(pv2_done, 1)

            def scores_and_values(b, g, between):
                for jt in range(TPB):
                    more = list(between[jt])
                    for u in range(0, 1 + HG):
                        score_unit(b, g, jt, u)
                    if jt == 0:
                        pe.wait_ge(ctx_read, by_group(b, g, 2, 2))
                        pe.wait_ge(v_copied, by_group(b, g, 1, 2))
                    else:
                        values(b, g, jt - 1, 1)
                    for it, u in more[:len(more) // 2]:
                        max_unit(b, g + 1, it, u)
                    for u in range(1 + HG, UNITS):
                        score_unit(b, g, jt, u)
                    values(b, g, jt, 0)
                    diagonal_values(g, jt)
                    for it, u in more[len(more) // 2:]:
                        max_unit(b, g + 1, it, u)
                values(b, g, TPB - 1, 1)
                pe.wait_ge(pv_done, by_group(b, g, 2 * TPB, 2 * TPB + 2))
                pe.wait_ge(pv2_done, by_group(b, g, TPB, TPB + 2))
                pe.sem_inc(ctx_done, 1)

            with pe.Fori(0, B) as b:
                pe.wait_ge(first_in[0], LOADS * (b + 1))
                for it in range(TPB):
                    for u in range(UNITS):
                        max_unit(b, 0, it, u)
                max_turned(b, 0)
                pe.wait_ge(first_in[1], LOADS * (b + 1))
                steps = [[0], [1], [2], [3], [4], [5], [6, 7], []]
                pe.wait_ge(second_in[0], LOADS * (b + 1))
                pe.wait_ge(max_in[0], 96 * (b + 1))
                scores_and_values(b, 0, [[(it, u) for it in its for u in range(UNITS)] for its in steps])
                max_turned(b, 1)
                pe.wait_ge(second_in[1], LOADS * (b + 1))
                pe.wait_ge(max_in[1], 96 * (b + 1))
                scores_and_values(b, 1, [[]] * TPB)

        @block.scalar
        def _(act):
            act.sem_inc(exp_done, 3)
            with act.Fori(0, B) as b:
                for g in range(2):
                    for jt in range(TPB):
                        for u in range(UNITS):
                            act.wait_ge(score_done, by_group(b, g, STEP, jt * UNITS + u + 1))
                            if u == 0:
                                act.wait_ge(pv2_done, by_group(b, g, TPB, jt + 1))
                                to = W2[:, jt % 2].rearrange("p h c -> p (h c)")
                            else:
                                h, c = (u - 1) % HG, (u - 1) // HG
                                if h == 0:
                                    act.wait_ge(pv_done, by_group(b, g, 2 * TPB, jt * 2 + c + 1))
                                to = W[:, c, h, :]
                            nc.scalar.activation(to, bank(RING[u % 3]), ACT.Exp, scale=SCALE).then_inc(exp_done, 1)

        @block.vector
        def _(dve):
            dve.sem_inc(max_read, 3)
            dve.sem_inc(mx_ready, 1)
            dve.sem_inc(split, 1)
            dve.sem_inc(ctx_read, 2)

            LINKS = 4

            def maxima(b, g):
                s3 = s.s3[:, bass.ts(b, TPB), HG * g:HG * (g + 1)]
                dve.wait_ge(mx_ready, by_group(b, g, 1, 1))
                for it in range(TPB):
                    for u in range(UNITS):
                        dve.wait_ge(max_done, by_group(b, g, MAXSTEP, it * UNITS + u + 1))
                        y = bank(MAXRING[u % 3])
                        if u == 0:
                            nc.vector.reduce_max(cm[:, it, :, 2], y.rearrange("p (h c) -> p h c", h=HG), AX.X).then_inc(max_read, 1)
                        else:
                            h, c = (u - 1) % HG, (u - 1) // HG
                            nc.vector.reduce_max(cm[:, it, h, c:c + 1], y, AX.X).then_inc(max_read, 1)
                dve.wait_ge(max_read, by_group(b, g, MAXSTEP, STEP + 3))
                nc.vector.reduce_max(mx[:].rearrange("p h t -> p t h"), cm[:], AX.X).then_inc(dve_done, 1)
                dve.wait_ge(dve_done, by_group(b, g, LINKS, 1))
                mt = mx[:].rearrange("p h t -> p t h")
                nc.vector.tensor_tensor(mt, mt, s3, ALU.max).then_inc(mx_ready, 1)
                dve.wait_ge(mx_ready, by_group(b, g, 1, 2))
                nc.vector.tensor_tensor(s.next_gap[:, bass.ts(b, TPB), HG * g:HG * (g + 1)], s3, mt, ALU.subtract).then_inc(dve_done, 1)
                if g:
                    dve.wait_ge(max_in[0], 96 * (b + 1))
                turned = bank(MAXRING[0])[0:HG * TPB, 0:P]
                dve.wait_ge(max_done, by_group(b, g, MAXSTEP, MAXSTEP))
                nc.vector.tensor_scalar(mparts[:, 0], turned, -1.0, None, ALU.mult).then_inc(dve_done, 1)
                dve.wait_ge(dve_done, by_group(b, g, LINKS, 3))
                nc.vector.scalar_tensor_tensor(out=mrest[:], in0=turned, scalar=-1.0, in1=mparts[:, 0],
                                               op0=ALU.mult, op1=ALU.subtract).then_inc(max_read, 1)
                dve.wait_ge(max_read, by_group(b, g, MAXSTEP, MAXSTEP + 3))
                nc.vector.tensor_copy(mparts[:, 1], mrest[:]).then_inc(dve_done, 1)
                dve.wait_ge(dve_done, by_group(b, g, LINKS, 4))
                nc.vector.tensor_tensor(mparts[:, 2], mrest[:], mparts[:, 1], ALU.subtract).then_inc(split, 1)

            def context(b, g):
                dve.wait_ge(ctx_done, by_group(b, g, 1, 3))
                nc.vector.tensor_copy(s.U[:, g, bass.ts(b * 2, CH)], bank(PV[0])).then_inc(ctx_read, 1)
                nc.vector.tensor_copy(s.U[:, g, bass.ts(b * 2 + 1, CH)], bank(PV[1])).then_inc(ctx_read, 1)

            with dve.Fori(0, B) as b:
                maxima(b, 0)
                maxima(b, 1)
                context(b, 0)
                context(b, 1)


def second_layer_out(nc, s, I, out):
    E, CAPACITY = 8, T // 8
    sem = s.sem
    consts, dve_done, act_done = sem("l1_out_constants"), sem("l1_out_dve"), sem("l1_out_act")
    logits_done, gap_ready, exps_ready, mask_ready, counted = (
        sem("logits_done"), sem("logit_gap_ready"), sem("logit_exps_ready"), sem("l1_mask_ready"), sem("l1_counted"))
    gates_ready, gT_done, gT_copied = sem("gates_ready"), sem("gates_turned"), sem("gates_turned_copied")
    e3_ready, u_turned, u_read, ctx_ready, cT_done, cT_copied = (
        sem("next_exp_ready"), sem("context_turned"), sem("context_turned_read"), sem("token_context_ready"), sem("ctxT_done"), sem("ctxT_copied"))
    y_done, y_read, o_done, o_read = sem("expert_y_done"), sem("expert_y_read"), sem("l1_o_done"), sem("l1_o_read")
    out_ready, out_sent = sem("out_ready"), sem("out_sent")
    bank = s.bank
    with ExitStack() as ctx:
        def sb(name, shape, dt=F32):
            return ctx.enter_context(nc.sbuf_tensor(name, shape, dt))

        wo = sb("Wo", [P, D])
        wg = sb("wg", [P, E])
        we = sb("moe_w", [P, E, D])
        be = sb("moe_b", [E, D])
        bo = sb("bo_row", [P, D])
        before = sb("l1_before", [P, P])
        every = sb("l1_every", [P, P])
        exp_no = sb("l1_expert_no", [P, E])
        lg = sb("logit_gap", [P, NT, E])
        lmax = sb("logit_max", [P, NT])
        ex = sb("logit_exp", [P, NT, E])
        top = sb("l1_top", [P, NT, 8])
        idx = sb("l1_top_index", [P, NT, 8], U32)
        idf = sb("l1_top_index_f", [P, NT])
        mask = sb("l1_mask", [P, NT, E])
        tot = sb("l1_totals", [P, E, NT])
        incl = sb("l1_inclusive", [P, E, NT])
        keep = sb("l1_keep", [P, E, NT])
        pos = sb("l1_pos", [P, NT, E])
        gates = sb("l1_gates", [P, NT, E])
        gT = sb("gates_by_expert", [E, T])
        e3 = sb("next_exp", [P, NT, NH])
        ev = sb("next_exp_v", [P, NT * NH, DH])
        num = sb("context_num", [P, 2, 2 * NH, DH])
        den = sb("context_den", [P, 2, 2 * NH])
        rden = sb("context_rden", [P, 2, 2 * NH])
        cT = sb("ctxT", [P, 2, 2 * P])
        yw = sb("weighed_y", [P, E, D])
        ys = sb("weighed_sum", [P, 2, D])
        block = ctx.enter_context(nc.Block())

        @block.sync
        def _(sp):
            for dst, src in ((wo[:], I["L1_attn_Wo"]), (wg[:], I["L1_ffn_wg"]), (we[:], I["moe_w"]), (be[:], I["L1_ffn_b"]),
                             (bo[:], I["rows"][4:5].squeeze(0).partition_broadcast(P)), (before[:], I["before"]), (every[:], I["every"]),
                             (exp_no[:], I["expert_numbers"])):
                sp.dma_start(dst, src).then_inc(consts, 16)
            flat = out.rearrange("b (t p) d -> p (b t) d", p=P)
            for q in range(4):
                sp.wait_ge(out_ready, 4 * (q + 1))
                sp.dma_start(flat[:, 4 * q:4 * q + 4], s.x[:, 4 * q:4 * q + 4]).then_inc(out_sent, 16)
            sp.wait_ge(out_sent, 64)

        @block.tensor
        def _(pe):
            pe.wait_ge(consts, 16 * 8)
            for t in range(NT):
                last = nc.tensor.matmul(bank(0)[:, E * t:E * t + E], s.xbT[:, t * P:(t + 1) * P], wg[:], start=True, stop=True)
            last.then_inc(logits_done, 1)

            def turned(k):
                if k >= 2:
                    pe.wait_ge(u_read, k - 1)
                for i in range(2):
                    for g in range(2):
                        t = 2 * k + i
                        last = nc.tensor.transpose(bank(1 + k % 2)[:, (2 * i + g) * P:(2 * i + g + 1) * P], s.U[:, g, t * P:(t + 1) * P], s.ident[:])
                last.then_inc(u_turned, 1)

            turned(0)
            turned(1)
            pe.wait_ge(mask_ready, 1)
            pe.wait_ge(gap_ready, 1)
            flat = mask[:].rearrange("p t e -> p (t e)")
            nc.tensor.matmul(bank(0)[:, 0:P], before[:], flat, start=True, stop=True)
            nc.tensor.matmul(bank(3)[:, 0:P], every[:], flat, start=True, stop=True).then_inc(counted, 1)
            pe.wait_ge(gates_ready, 1)
            for c in range(NCH):
                if c:
                    pe.wait_ge(gT_copied, c)
                for q in range(4):
                    last = nc.tensor.transpose(bank(7)[0:E, q * P:(q + 1) * P], gates[:, 4 * c + q, :], s.ident[:])
                last.then_inc(gT_done, 1)
            pe.wait_ge(gT_copied, NCH)
            for k in range(NT // 2):
                if k >= 2:
                    turned(k)
                pe.wait_ge(ctx_ready, k + 1)
                pe.wait_ge(cT_copied, k) if k else None
                for i in range(2):
                    last = nc.tensor.transpose(bank(3)[:, i * P:(i + 1) * P], num[:, k % 2, NH * i:NH * (i + 1), :].rearrange("p h d -> p (h d)"), s.ident[:])
                last.then_inc(cT_done, 1)
                pe.wait_ge(cT_copied, k + 1)
                for i in range(2):
                    t = 2 * k + i
                    for half in range(2):
                        if t:
                            pe.wait_ge(y_read, 2 * (t - 1) + half + 1)
                        nc.tensor.matmul(bank(4 + half), s.xbT[:, t * P:(t + 1) * P],
                                         we[:, 4 * half:4 * half + 4, :].rearrange("p e f -> p (e f)"), start=True, stop=True).then_inc(y_done, 1)
                    if t:
                        pe.wait_ge(o_read, t)
                    nc.tensor.matmul(bank(6)[:, 0:D], cT[:, k % 2, i * P:(i + 1) * P], wo[:], start=True, stop=False)
                    nc.tensor.matmul(bank(6)[:, 0:D], gT[:, t * P:(t + 1) * P], be[:], start=False, stop=True).then_inc(o_done, 1)

        @block.scalar
        def _(act):
            nc.scalar.activation(e3[:], s.next_gap[:], ACT.Exp, scale=SCALE).then_inc(e3_ready, 1)
            act.wait_ge(gap_ready, 1)
            nc.scalar.activation(ex[:], lg[:], ACT.Exp).then_inc(exps_ready, 1)
            for c in range(NCH):
                act.wait_ge(gT_done, c + 1)
                nc.scalar.activation(gT[:, c * CH:(c + 1) * CH], bank(7)[0:E, :], ACT.Copy).then_inc(gT_copied, 1)
            for k in range(NT // 2):
                act.wait_ge(cT_done, k + 1)
                if k >= 2:
                    act.wait_ge(o_done, 2 * (k - 1))
                nc.scalar.activation(cT[:, k % 2], bank(3)[:, 0:2 * P], ACT.Copy).then_inc(cT_copied, 1)

        @block.vector
        def _(dve):
            t = Tally(dve_done)

            def link(ins):
                dve.wait_ge(dve_done, t.by(ins))

            full = [P, NT, E]
            t.by(nc.vector.memset(keep[:], 1.0))
            dve.wait_ge(consts, 16 * 8)
            dve.wait_ge(dve_done, 1)
            link(nc.vector.memset(keep[:, :, 0:1], 0.0))
            link(nc.vector.tensor_tensor(s.x[:], s.x[:], bc(bo[:, None, :], [P, NT, D]), ALU.add))
            dve.wait_ge(logits_done, 1)
            logits = bank(0)[:, 0:P].rearrange("p (t e) -> p t e", e=E)
            link(nc.vector.reduce_max(lmax[:], logits, AX.X))
            nc.vector.tensor_tensor(lg[:], logits, bc(lmax[:, :, None], full), ALU.subtract).then_inc(gap_ready, 1)
            dve.wait_ge(e3_ready, 1)
            link(nc.vector.tensor_tensor(ev[:], s.v_next[:].rearrange("p t (h d) -> p (t h) d", h=NH),
                                         bc(e3[:].rearrange("p t h -> p (t h)")[:, :, None], [P, NT * NH, DH]), ALU.mult))
            dve.wait_ge(exps_ready, 1)
            for i in range(NT):
                last = t.by(nc.vector.max(top[:, i, :], ex[:, i, :]))
            dve.wait_ge(dve_done, last)
            for i in range(NT):
                last = t.by(nc.vector.max_index(idx[:, i, :], top[:, i, :], ex[:, i, :]))
            dve.wait_ge(dve_done, last)
            link(nc.vector.tensor_copy(idf[:], idx[:, :, 0]))
            nc.vector.tensor_tensor(mask[:], bc(idf[:, :, None], full), bc(exp_no[:, None, :], full), ALU.is_equal).then_inc(mask_ready, 1)
            link(nc.vector.reduce_sum(lmax[:], ex[:], AX.X))
            link(nc.vector.reciprocal(lmax[:], lmax[:]))
            count_before(nc, s, dve, link, mask, counted, tot, incl, keep, pos, bank(0)[:, 0:P], bank(3)[:, 0:P])
            link(nc.vector.tensor_scalar(pos[:], pos[:], float(CAPACITY), None, ALU.is_lt))
            link(nc.vector.tensor_tensor(pos[:], pos[:], mask[:], ALU.mult))
            nc.vector.tensor_tensor(gates[:], pos[:], bc(lmax[:, :, None], full), ALU.mult).then_inc(gates_ready, 1)
            dve.wait_ge(gates_ready, 1)
            e3f = e3[:].rearrange("p t h -> p (t h)")
            for k in range(NT // 2):
                m = k % 2
                dve.wait_ge(u_turned, k + 1)
                if k >= 2:
                    dve.wait_ge(cT_done, k - 1)
                y = bank(1 + m).rearrange("p (h d) -> p h d", d=32)
                hs = slice(2 * NH * k, 2 * NH * (k + 1))
                t.by(nc.vector.tensor_tensor(num[:, m], y[:, :, 0:DH], ev[:, hs, :], ALU.add))
                link(nc.vector.tensor_tensor(den[:, m], y[:, :, DH], e3f[:, hs], ALU.add))
                dve.sem_inc(u_read, 1)
                link(nc.vector.reciprocal(rden[:, m], den[:, m]))
                nc.vector.tensor_tensor(num[:, m], num[:, m], bc(rden[:, m, :, None], [P, 2 * NH, DH]), ALU.mult).then_inc(ctx_ready, 1)
                for i in range(2):
                    tt = 2 * k + i
                    for half in range(2):
                        dve.wait_ge(y_done, 2 * tt + half + 1)
                        nc.vector.tensor_tensor(yw[:, 4 * half:4 * half + 4], bank(4 + half).rearrange("p (e f) -> p e f", e=4),
                                                bc(gates[:, tt, 4 * half:4 * half + 4, None], [P, 4, D]), ALU.mult).then_inc(y_read, 1)
                    dve.wait_ge(y_read, 2 * tt + 2)
                    link(nc.vector.reduce_sum(ys[:, i], yw[:].rearrange("p e f -> p f e"), AX.X))
                    link(nc.vector.tensor_tensor(s.x[:, tt], s.x[:, tt], ys[:, i], ALU.add))
                    dve.wait_ge(o_done, tt + 1)
                    nc.vector.tensor_tensor(s.x[:, tt], s.x[:, tt], bank(6)[:, 0:D], ALU.add).then_inc(o_read, 1)
                    dve.wait_ge(o_read, tt + 1)
                    dve.sem_inc(out_ready, 1)


def build(nc, I, out):
    with ExitStack() as ctx:
        s = Shared()

        def sb(name, shape, dt=F32):
            return ctx.enter_context(nc.sbuf_tensor(name, shape, dt))

        s.sem = lambda name: ctx.enter_context(nc.semaphore(name))
        banks = [ctx.enter_context(nc.psum_tensor(f"bank{i}", [P, CH], F32)) for i in range(8)]
        s.bank = lambda i: banks[i][:]
        s.rows_in = nc.dram_tensor("rows_by_expert", (SLOTS * P, D), F32, kind="Internal").ap()
        s.rows_out = nc.dram_tensor("expert_results", (SLOTS * P, D), F32, kind="Internal").ap()
        s.expert_w_in = s.sem("expert_weights_loaded")
        s.ident = sb("identity", [P, P])
        s.vec = sb("vectors_sb", [P, 24])
        s.x = sb("x", [P, NT, D])
        with ExitStack() as l0:
            def sb0(name, shape, dt=F32, c=l0):
                return c.enter_context(nc.sbuf_tensor(name, shape, dt))
            s.xn = sb0("xn", [P, NT, D])
            s.scores = sb0("scores", [P, NT, 8])
            s.wt = sb0("expert_weights_of_tokens", [P, 2, NT])
            s.pos = sb0("positions", [P, 2, NT], U32)
            s.slot_e = sb0("slot_expert", [P, SLOTS], I32)
            s.A = sb0("A", [P, DG, NS])
            s.zs = sb0("silu_z", [P, DG, T])
            s.u = sb0("u", [P, DG, T])
            s.delta = sb0("delta", [P, DG, T])
            s.du = sb0("delta_u", [P, DG, T])
            s.bc3 = sb0("bc_parts", [96, T], BF16)
            with ExitStack() as c:
                s.xnT = sb0("xnT", [P, T], c=c)
                s.gate_w = sb0("gate_w", [P, 8], c=c)
                s.taps = sb0("taps", [P, DG, KC], c=c)
                norms_and_projections(nc, s, I)
            with ExitStack() as c:
                s.w1 = sb0("w1", [P, 8, 512], c=c)
                s.w3 = sb0("w3", [P, 8, 512], c=c)
                s.w2 = sb0("w2", [P, 8, 4, P], c=c)
                route(nc, s, I)
                selective_scan(nc, s, I)
                experts(nc, s, I)
            first_layer_out(nc, s, I)
        with ExitStack() as l1:
            def sb1(name, shape, dt=F32, c=l1):
                return c.enter_context(nc.sbuf_tensor(name, shape, dt))
            s.q_stacks = nc.dram_tensor("q_stacks", (B, 2, 96, 2, 2, HG, L), BF16, kind="Internal").ap()
            s.k_stacks = nc.dram_tensor("k_stacks", (B, 2, 48, 2, HG, L), BF16, kind="Internal").ap()
            s.xbT = sb1("xbT", [P, T])
            s.vals = sb1("values", [P, NT, NH, 32])
            s.v_next = sb1("next_values", [P, NT, D])
            s.s3 = sb1("next_key_scores", [P, NT, NH])
            s.next_gap = sb1("next_key_gap", [P, NT, NH])
            s.U = sb1("contexts", [P, 2, T])
            attention_operands(nc, s, I)
            attention(nc, s, I)
            second_layer_out(nc, s, I, out)


BIG = -1e30


def constants():
    import numpy as np

    bf = mybir.dt.np(BF16)
    k, m = np.arange(P)[:, None], np.arange(P)[None, :]
    out = {"ident": np.eye(P, dtype=np.float32), "ident_bf": np.eye(P).astype(bf)}
    out["before"] = (k < m).astype(np.float32)
    out["every"] = np.ones((P, P), np.float32)
    sel = np.zeros((96, 2, NS, P), np.float32)
    for part in range(3):
        for which in range(2):
            for n in range(NS):
                sel[32 * part + NS * which + n, which, n, :] = 1.0
    out["selectors"] = sel.astype(bf)
    first = np.where(m > k, BIG, 0.0)
    second = np.where(m < k + 2, BIG, 0.0)
    corner = np.zeros((P, 2))
    corner[P - 1, 0] = BIG
    corner[0, 1] = BIG
    out["masks"] = np.concatenate([first, second, first.T, second.T, corner], 1).astype(bf)
    w = np.exp(np.arange(0, D, 2, dtype=np.float32) * np.float32(-np.log(10000.0) / D)).astype(np.float64)
    w = np.repeat(w, 2)[:, None]
    sign = np.where(np.arange(D) % 2 == 0, -1.0, 1.0)[:, None]
    i = np.arange(L)[None, :]
    turn = [np.cos((L - 1 - i) * w), sign * np.sin((L - 1 - i) * w), np.cos((i + 2) * w), -sign * np.sin((i + 2) * w)]
    out["turns"] = np.stack(turn, 1).astype(np.float32)
    table = np.where(sign < 0, np.sin(i * w), np.cos(i * w)).astype(np.float32)
    hi = table.astype(bf)
    mid = (table - hi.astype(np.float32)).astype(bf)
    lo = (table - hi.astype(np.float32) - mid.astype(np.float32)).astype(bf)
    out["sinusoids"] = np.stack([hi, mid, lo], 1)
    slot = np.arange(NT * 2 + 8, dtype=np.float32)
    out["slot_numbers"] = np.broadcast_to(slot, (P, slot.size)).copy()
    out["expert_numbers"] = np.broadcast_to(np.arange(8, dtype=np.float32), (P, 8)).copy()
    return out


def layouts(v):
    import numpy as np

    a = {k: np.asarray(x) for k, x in v.items()}
    o = {k: a[k] for k in ("L0_attn_x", "L0_attn_A_log", "L1_attn_Wo", "L1_ffn_wg", "L1_ffn_b")}
    o["L0_attn_conv_w"] = a["L0_attn_conv_w"][:, 0, :]
    o["in_w_t"] = a["L0_attn_in_w"].T
    xw = a["L0_attn_xproj_w"].T
    o["xproj_t"] = xw[:, :R]
    o["xproj_bc_t"] = np.concatenate([xw[:, R:]] * 3, 1)
    o["dt_w_t"] = a["L0_attn_dt_w"].T
    o["out_w_t"] = a["L0_attn_out_w"].T
    o["gate_w_t"] = a["L0_ffn_gate_w"].T
    o["w1_t"] = a["L0_ffn_w1"].transpose(2, 0, 1)
    o["w3_t"] = a["L0_ffn_w3"].transpose(2, 0, 1)
    o["w2_t"] = a["L0_ffn_w2"].reshape(8, D, 4, P).transpose(3, 0, 2, 1)
    heads = D // 16

    def blocks(w):
        z = np.zeros((D, D), w.dtype)
        for h in range(heads):
            z[16 * h:16 * h + 16, 16 * h:16 * h + 16] = w
        return z

    wpt = a["L1_attn_Wp"].T
    swapped = wpt.reshape(16, 8, 2)[:, :, ::-1].reshape(16, 16)
    o["head_w"] = np.stack([blocks(a["L1_attn_Wq"]), blocks(a["L1_attn_Wk"]), blocks(a["L1_attn_Wv"]),
                            blocks(wpt), blocks(swapped)], 1)
    rep = lambda x: np.concatenate([x] * heads)
    two = lambda x: [x[:P], x[P:]]
    cols = [a["L0_attn_norm_g"], a["L0_attn_norm_b"], *two(a["L0_attn_conv_b"]), *two(a["L0_attn_dt_b"]), *two(a["L0_attn_D"]),
            a["L1_attn_ln_gamma"], a["L1_attn_ln_beta"], rep(a["L1_attn_bq"]), rep(a["L1_attn_bk"]),
            a["L1_attn_u_bias"].reshape(D), a["L1_attn_v_bias"].reshape(D)]
    cols += [np.zeros(P, np.float32)] * (24 - len(cols))
    o["vectors"] = np.stack(cols, 1)
    o["rows"] = np.stack([rep(a["L1_attn_bq"]), a["L1_attn_u_bias"].reshape(D), rep(a["L1_attn_bk"]), rep(a["L1_attn_bv"]),
                          a["L1_attn_bo"]], 0)
    o["moe_w"] = a["L1_ffn_W"].transpose(2, 0, 1)
    o.update(constants())
    return {k: np.ascontiguousarray(x) for k, x in o.items()}


def kernel(**inputs):
    import concourse.bacc as bacc
    from concourse.bass_utils import run_bass_kernel_spmd

    nc = bacc.Bacc("TRN2", target_bir_lowering=False, num_devices=1)
    arrays = layouts(inputs)
    aps = {k: nc.dram_tensor("in_" + k, x.shape, mybir.dt.from_np(x.dtype), kind="ExternalInput").ap() for k, x in arrays.items()}
    out = nc.dram_tensor("out", (B, L, D), F32, kind="ExternalOutput").ap()
    build(nc, aps, out)
    r = run_bass_kernel_spmd(nc, [{"in_" + k: x for k, x in arrays.items()}], core_ids=[0])
    return r.results[0]["out"]
```

```python
from contextlib import ExitStack

import concourse.bass as bass
from concourse import mybir

F32 = mybir.dt.float32
BF16 = mybir.dt.bfloat16
I32 = mybir.dt.int32
U32 = mybir.dt.uint32
ALU = mybir.AluOpType
ACT = mybir.ActivationFunctionType
AX = mybir.AxisListType

P = 128
B, L, D = 2, 1024, 128
T = B * L
NT = T // P
DG = 2
NS = 16
R = 64
KC = 4
CH = 512
NCH = T // CH
TPS = L // P
EPS = 1e-5


class Tally:

    def __init__(self, sem):
        self.sem, self.n = sem, 0

    def by(self, ins):
        ins.then_inc(self.sem, 1)
        self.n += 1
        return self.n


def bc(ap, shape):
    return ap.to_broadcast(shape)


class Shared:
    pass


NQ = 4
SLOTS = 2 * T // P + 8


def two_norms(nc, dve, t, src, mid, dst, tmp, have, var_ready, rstd_ready, mid_ready, dst_ready):
    stats, mv, ve, rstd = tmp

    def link(ins):
        dve.wait_ge(dve_done, t.by(ins))

    dve_done = t.sem

    def statistics(x, k, q):
        for i in range(NQ * q, NQ * (q + 1)):
            last = t.by(nc.vector.bn_stats(stats[:, k, i, :], x[:, i, :]))
        dve.wait_ge(dve_done, last)
        for i in range(NQ * q, NQ * (q + 1)):
            last = t.by(nc.vector.bn_aggr(mv[:, k, i, :], stats[:, k, i, :]))
        dve.wait_ge(dve_done, last)
        nc.vector.tensor_scalar(ve[:, k, NQ * q:NQ * (q + 1)], mv[:, k, NQ * q:NQ * (q + 1), 1], EPS, None, ALU.add).then_inc(var_ready, 1)

    def scale(x, y, k, q, ready):
        dve.wait_ge(rstd_ready, k * NT // NQ + q + 1)
        for i in range(NQ * q, NQ * (q + 1)):
            last = t.by(nc.vector.tensor_scalar(y[:, i, :], x[:, i, :], mv[:, k, i, 0:1], rstd[:, k, i:i + 1], ALU.subtract, ALU.mult))
        dve.wait_ge(dve_done, last)
        dve.sem_inc(ready, 1)

    for q in range(NT // NQ):
        if have:
            dve.wait_ge(have[q], 16)
        statistics(src, 0, q)
    for q in range(NT // NQ):
        scale(src, mid, 0, q, mid_ready)
        statistics(mid, 1, q)
    for q in range(NT // NQ):
        scale(mid, dst, 1, q, dst_ready)


def reciprocal_roots(nc, pool, tmp, half, var_ready, rstd_ready):
    ve, rstd = tmp[2:]
    for k in range(2):
        for q in range(NT // NQ):
            pool.wait_ge(var_ready, k * NT // NQ + q + 1)
            cols = slice(NQ * q, NQ * (q + 1))
            nc.gpsimd.tensor_tensor(rstd[:, k, cols], ve[:, k, cols], half[:, 0:NQ], ALU.pow).then_inc(rstd_ready, 1)


def norm_tensors(sb, name):
    return (sb(name + "_stats", [P, 2, NT, 6]), sb(name + "_mean_var", [P, 2, NT, 2]), sb(name + "_var_eps", [P, 2, NT]),
            sb(name + "_rstd", [P, 2, NT]))


def count_before(nc, s, dve, link, mask, counted, tot, incl, keep, pos, rank_bank, total_bank, E=8):
    dve.wait_ge(counted, 1)
    link(nc.vector.tensor_copy(tot[:], total_bank.rearrange("p (t e) -> p e t", e=E)))
    link(nc.vector.tensor_tensor_scan(incl[:].rearrange("p e t -> p (e t)"), keep[:].rearrange("p e t -> p (e t)"),
                                      tot[:].rearrange("p e t -> p (e t)"), 0.0, ALU.mult, ALU.add))
    link(nc.vector.tensor_tensor(tot[:], incl[:], tot[:], ALU.subtract))
    link(nc.vector.tensor_tensor(pos[:], rank_bank.rearrange("p (t e) -> p t e", e=E), tot[:].rearrange("p e t -> p t e"), ALU.add))


def norms_and_projections(nc, s, I):
    sem = s.sem
    x_in, w_in, ident_in, route_in = [sem(f"x_loaded_{q}") for q in range(NT // NQ)], sem("weights_loaded"), sem("identity_loaded"), sem("route_constants")
    dve_done, act_done, pool_done = s.tally.sem, sem("a_act"), sem("a_pool")
    var_ready, rstd_ready = sem("var_ready"), sem("rstd_ready")
    xn_ready, xa_ready = sem("xn_ready"), sem("xa_ready")
    tr_done, tr_copied = sem("transposes_done"), sem("transposes_copied")
    proj_done, proj_copied = sem("in_proj_done"), sem("in_proj_copied")
    conv_done, u_ready = sem("conv_done"), sem("u_ready")
    score_done, scores_copied = sem("scores_done"), sem("scores_copied")
    dbc_done, draw_copied, bc_copied, bc_split = sem("dbc_done"), sem("draw_copied"), sem("bc_copied"), sem("bc_split")
    dt_done, relu_done, abs_done, exp_done, one_done, rest_done, ln_done, given_back, delta_ready = (
        sem("dt_done"), sem("softplus_relu"), sem("softplus_abs"), sem("softplus_exp"), sem("softplus_one"),
        sem("softplus_rest"), sem("softplus_ln"), sem("softplus_given_back"), sem("delta_ready"))
    pads_ready = sem("pads_ready")
    diff_ready, e2_ready, mask_ready, counted, counts_read = (
        sem("gap_ready"), sem("gap_exp"), sem("mask_ready"), sem("counted"), sem("counts_read"))
    zeroed_2 = sem("second_rows_zeroed")
    pos_ready, zero_ready, zeroed, scattered = sem("positions_ready"), sem("zeros_ready"), sem("rows_zeroed"), sem("rows_scattered")
    bank = s.bank
    with ExitStack() as ctx:
        def sb(name, shape, dt=F32):
            return ctx.enter_context(nc.sbuf_tensor(name, shape, dt))

        xa = sb("xa", [P, NT, D])
        norm_tmp = norm_tensors(sb, "norm")
        half = sb("minus_half", [P, NT])
        xaT = sb("xaT", [P, T])
        xp = sb("x_padded", [P, DG, B, L + KC - 1])
        draw = sb("delta_low_rank", [R, T])
        in_w = sb("in_w_t", [P, 4 * P])
        xw = sb("xproj_w_t", [P, DG, R])
        xbc = sb("xproj_bc_t", [P, DG, 96])
        dtw = sb("dt_w_t", [R, DG * P])
        bcr = sb("bc_rest", [96, T])
        bcm = sb("bc_middle", [96, T], BF16)
        bcl = sb("bc_low", [96, T], BF16)
        before = sb("before", [P, P])
        every = sb("every", [P, P])
        slot_no = sb("slot_no", [P, SLOTS])
        exp_no = sb("expert_no", [P, 8])
        top = sb("top", [P, NT, 8])
        idx = sb("top_index", [P, NT, 8], U32)
        idf = sb("top_index_f", [P, NT, 2])
        gap = sb("gap", [P, NT])
        one = sb("one_hot", [P, 2, NT, 8])
        mask = sb("mask", [P, NT, 8])
        tot = sb("totals", [P, 8, NT])
        incl = sb("inclusive", [P, 8, NT])
        keep = sb("keep", [P, 8, NT])
        pos = sb("pos", [P, NT, 8])
        picked = sb("picked", [P, NT, 8])
        posf = sb("pos_f", [P, 2, NT])
        tiles = sb("expert_tiles", [P, 8])
        tiles_i = sb("expert_tiles_i", [P, 8], I32)
        ends = sb("expert_ends", [P, 8])
        ones8 = sb("ones8", [P, 8])
        past = sb("slots_past", [P, SLOTS, 8])
        slot_f = sb("slot_expert_f", [P, SLOTS])
        zeros = sb("zeros", [P, 1024])
        spe = xp[:].rearrange("p g b l -> p (g b l)")[:, 0:DG * T].rearrange("p (g t) -> p g t", g=DG)
        spw = s.du
        block = ctx.enter_context(nc.Block())

        NW = 8
        COUNT_BANK = 7

        @block.sync
        def _(sp):
            for q in range(NT // NQ):
                b, t0 = q // (TPS // NQ), q % (TPS // NQ) * NQ
                sp.dma_start(s.x[:, NQ * q:NQ * (q + 1)],
                             I["L0_attn_x"][b, t0 * P:(t0 + NQ) * P].rearrange("(t p) d -> p t d", p=P)).then_inc(x_in[q], 16)
            sp.dma_start(s.ident[:], I["ident"]).then_inc(ident_in, 16)
            for dst, src in ((s.gate_w[:], I["gate_w_t"]), (in_w[:], I["in_w_t"]), (s.vec[:], I["vectors"]),
                             (s.A[:], I["L0_attn_A_log"].rearrange("(g p) n -> p g n", p=P)),
                             (s.taps[:], I["L0_attn_conv_w"].rearrange("(g p) k -> p g k", p=P)),
                             (xw[:], I["xproj_t"].rearrange("(g p) r -> p g r", p=P)),
                             (xbc[:], I["xproj_bc_t"].rearrange("(g p) r -> p g r", p=P)),
                             (dtw[:], I["dt_w_t"])):
                sp.dma_start(dst, src).then_inc(w_in, 16)
            for dst, src in ((before[:], I["before"]), (every[:], I["every"]), (slot_no[:], I["slot_numbers"]), (exp_no[:], I["expert_numbers"])):
                sp.dma_start(dst, src).then_inc(route_in, 16)
            sp.wait_ge(zero_ready, 1)
            flat = s.rows_in.rearrange("(c p q) d -> c p (q d)", p=P, q=8)
            for c in range(SLOTS // 8):
                sp.dma_start(flat[c], zeros[:]).then_inc(zeroed, 16)
            sp.dma_start(s.sel[:], I["selectors"]).then_inc(s.sel_in, 16)
            flat = s.rows2_in[0:T].rearrange("(c p q) d -> c p (q d)", p=P, q=8)
            for c in range(NT // 8):
                sp.dma_start(flat[c], zeros[:]).then_inc(zeroed_2, 16)
            sp.wait_ge(zeroed_2, 16 * (NT // 8))

        def delta_u(pool, i):
            g, cols = i // NCH, slice(i % NCH * CH, (i % NCH + 1) * CH)
            pool.wait_ge(delta_ready, i + 1)
            nc.gpsimd.tensor_tensor(s.du[:, g, cols], s.delta[:, g, cols], s.u[:, g, cols], ALU.mult)

        @block.gpsimd
        def _(pool):
            t = Tally(pool_done)

            def link(ins):
                pool.wait_ge(pool_done, t.by(ins))

            link(nc.gpsimd.memset(half[:], -0.5))
            link(nc.gpsimd.memset(zeros[:], 0.0))
            pool.sem_inc(zero_ready, 1)
            link(nc.gpsimd.memset(xp[:, :, :, 0:KC - 1], 0.0))
            pool.sem_inc(pads_ready, 1)
            reciprocal_roots(nc, pool, norm_tmp, half, var_ready, rstd_ready)
            pool.wait_ge(pos_ready, 1)
            pool.wait_ge(zeroed, 16 * (SLOTS // 8))
            for i in range(NT):
                for k in range(2):
                    nc.gpsimd.indirect_dma_start(out=s.rows_in, out_offset=bass.IndirectOffsetOnAxis(ap=s.pos[:, k, i:i + 1], axis=0),
                                                 in_=s.xn[:, i, :], in_offset=None,
                                                 bounds_check=SLOTS * P - 1).then_inc(scattered, 16)
            for i in range(DG * NCH):
                g, cols = i // NCH, slice(i % NCH * CH, (i % NCH + 1) * CH)
                pool.wait_ge(rest_done, i + 1)
                pool.wait_ge(relu_done, i + 1)
                nc.gpsimd.tensor_tensor(s.delta[:, g, cols], s.delta[:, g, cols], spe[:, g, cols], ALU.subtract).then_inc(given_back, 1)
                if i:
                    delta_u(pool, i - 1)
            delta_u(pool, DG * NCH - 1)
            pool.wait_ge(scattered, 32 * NT)

        @block.vector
        def _(dve):
            t = s.tally

            def link(ins):
                dve.wait_ge(dve_done, t.by(ins))

            two_norms(nc, dve, t, s.x, s.xn, xa, norm_tmp, x_in, var_ready, rstd_ready, xn_ready, xa_ready)

            full = [P, NT, 8]
            t.by(nc.vector.memset(ones8[:], 1.0))
            link(nc.vector.memset(keep[:], 1.0))
            t.by(nc.vector.memset(keep[:, :, 0:1], 0.0))
            dve.wait_ge(scores_copied, 1)
            for i in range(NT):
                last = t.by(nc.vector.max(top[:, i, :], s.scores[:, i, :]))
            dve.wait_ge(dve_done, last)
            for i in range(NT):
                last = t.by(nc.vector.max_index(idx[:, i, :], top[:, i, :], s.scores[:, i, :]))
            nc.vector.tensor_tensor(gap[:], top[:, :, 1], top[:, :, 0], ALU.subtract).then_inc(diff_ready, 1)
            dve.wait_ge(dve_done, last)
            dve.wait_ge(route_in, 64)
            link(nc.vector.tensor_copy(idf[:], idx[:, :, 0:2]))
            for k in range(2):
                last = t.by(nc.vector.tensor_tensor(one[:, k], bc(idf[:, :, k:k + 1], full), bc(exp_no[:, None, :], full), ALU.is_equal))
            dve.wait_ge(dve_done, last)
            nc.vector.tensor_tensor(mask[:], one[:, 0], one[:, 1], ALU.add).then_inc(mask_ready, 1)

            def convolve(g):
                dve.wait_ge(proj_copied, 4 * (g + 1))
                dve.wait_ge(pads_ready, 1)
                out = s.u[:, g].rearrange("p (b l) -> p b l", b=B)
                link(nc.vector.tensor_scalar(out, xp[:, g, :, 0:L], s.taps[:, g, 0:1], None, ALU.mult))
                for k in range(1, KC):
                    link(nc.vector.scalar_tensor_tensor(out=out, in0=xp[:, g, :, k:k + L], scalar=s.taps[:, g, k:k + 1],
                                                        in1=out, op0=ALU.mult, op1=ALU.add))
                dve.sem_inc(conv_done, 1)

            convolve(0)
            y = bank(COUNT_BANK)
            count_before(nc, s, dve, link, mask, counted, tot, incl, keep, pos, y[:, 0:P], y[:, P:2 * P])
            dve.sem_inc(counts_read, 1)
            link(nc.vector.tensor_scalar(tiles_i[:], incl[:, :, NT - 1], float(P - 1), None, ALU.add))
            link(nc.vector.tensor_single_scalar(tiles_i[:], tiles_i[:], 7, ALU.arith_shift_right))
            link(nc.vector.tensor_copy(tiles[:], tiles_i[:]))
            link(nc.vector.tensor_tensor_scan(ends[:], ones8[:], tiles[:], 0.0, ALU.mult, ALU.add))
            link(nc.vector.tensor_tensor(tiles[:], ends[:], tiles[:], ALU.subtract))
            link(nc.vector.tensor_scalar(tiles[:], tiles[:], float(P), None, ALU.mult))
            link(nc.vector.tensor_tensor(pos[:], pos[:], bc(tiles[:, None, :], full), ALU.add))
            for k in range(2):
                link(nc.vector.tensor_tensor(picked[:], pos[:], one[:, k], ALU.mult))
                link(nc.vector.reduce_sum(posf[:, k], picked[:], AX.X))
            link(nc.vector.tensor_copy(s.pos[:], posf[:]))
            dve.sem_inc(pos_ready, 1)
            convolve(1)
            wide = [P, SLOTS, 8]
            link(nc.vector.tensor_tensor(past[:], bc(slot_no[:, :, None], wide), bc(ends[:, None, :], wide), ALU.is_ge))
            link(nc.vector.reduce_sum(slot_f[:], past[:], AX.X))
            link(nc.vector.tensor_scalar(s.slot_e[:], slot_f[:], 7.0, None, ALU.min))
            for c in range(NCH):
                cols = slice(c * CH, (c + 1) * CH)
                dve.wait_ge(bc_copied, c + 1)
                link(nc.vector.tensor_tensor(bcr[:, cols], bank(4 + c % 2)[0:96, :], s.bc3[:, cols], ALU.subtract))
                dve.sem_inc(bc_split, 1)
                link(nc.vector.tensor_copy(bcm[:, cols], bcr[:, cols]))
                link(nc.vector.tensor_tensor(bcl[64:96, cols], bcr[64:96, cols], bcm[64:96, cols], ALU.subtract))
                nc.vector.tensor_copy(s.bc3[32:64, cols], bcm[32:64, cols])
                link(nc.vector.tensor_copy(s.bc3[64:96, cols], bcl[64:96, cols]))
            dve.wait_ge(e2_ready, 1)
            link(nc.vector.tensor_scalar(gap[:], s.wt[:, 1], 1.0, None, ALU.add))
            link(nc.vector.reciprocal(s.wt[:, 0], gap[:]))
            link(nc.vector.tensor_tensor(s.wt[:, 1], s.wt[:, 1], s.wt[:, 0], ALU.mult))
            n = DG * NCH

            def place(i):
                return i // NCH, slice(i % NCH * CH, (i % NCH + 1) * CH)

            for i in range(n):
                g, cols = place(i)
                dve.wait_ge(dt_done, i + 1)
                nc.vector.tensor_scalar(s.delta[:, g, cols], bank(i % 4), s.vec[:, 4 + g:5 + g], 0.0, ALU.add, ALU.max).then_inc(relu_done, 1)
            for i in range(n):
                g, cols = place(i)
                dve.wait_ge(exp_done, i + 1)
                nc.vector.tensor_scalar(spw[:, g, cols], spe[:, g, cols], 1.0, None, ALU.add).then_inc(one_done, 1)
                dve.wait_ge(one_done, i + 1)
                nc.vector.scalar_tensor_tensor(out=spe[:, g, cols], in0=spw[:, g, cols], scalar=-1.0, in1=spe[:, g, cols],
                                               op0=ALU.add, op1=ALU.subtract).then_inc(rest_done, 1)
            for i in range(n):
                g, cols = place(i)
                dve.wait_ge(ln_done, i + 1)
                dve.wait_ge(given_back, i + 1)
                nc.vector.tensor_tensor(s.delta[:, g, cols], s.delta[:, g, cols], spw[:, g, cols], ALU.add).then_inc(delta_ready, 1)

        @block.scalar
        def _(act):
            a = Tally(act_done)
            for c in range(NCH):
                act.wait_ge(tr_done, c + 1)
                nc.scalar.activation(s.xnT[:, c * CH:(c + 1) * CH], bank(c), ACT.Copy).then_inc(tr_copied, 1)
            act.wait_ge(score_done, 1)
            nc.scalar.activation(s.scores[:].rearrange("p t e -> p (t e)"), bank(0)[:, 0:8 * NT], ACT.Copy).then_inc(scores_copied, 1)
            act.wait_ge(w_in, 16 * NW)
            for c in range(NCH):
                act.wait_ge(tr_done, NCH + c + 1)
                nc.scalar.activation(xaT[:, c * CH:(c + 1) * CH], bank(4 + c), ACT.Identity,
                                     scale=s.vec[:, 0:1], bias=s.vec[:, 1:2]).then_inc(tr_copied, 1)
            for i in range(2 * DG * NCH):
                q, c = i // NCH, i % NCH
                act.wait_ge(proj_done, i + 1)
                if q < DG:
                    b, l0 = c // (NCH // B), c % (NCH // B) * CH
                    nc.scalar.activation(xp[:, q, b, KC - 1 + l0:KC - 1 + l0 + CH], bank(i % 4), ACT.Copy).then_inc(proj_copied, 1)
                else:
                    nc.scalar.activation(s.zs[:, q - DG, c * CH:(c + 1) * CH], bank(i % 4), ACT.Silu).then_inc(proj_copied, 1)
            for g in range(DG):
                act.wait_ge(conv_done, g + 1)
                nc.scalar.activation(s.u[:, g], s.u[:, g], ACT.Silu, bias=s.vec[:, 2 + g:3 + g]).then_inc(u_ready, 1)
            for c in range(NCH):
                cols = slice(c * CH, (c + 1) * CH)
                act.wait_ge(dbc_done, 2 * c + 1)
                nc.scalar.activation(draw[:, cols], bank(6 + c % 2)[0:R, :], ACT.Copy).then_inc(draw_copied, 1)
                act.wait_ge(dbc_done, 2 * c + 2)
                nc.scalar.activation(s.bc3[:, cols], bank(4 + c % 2)[0:96, :], ACT.Copy).then_inc(bc_copied, 1)
            act.wait_ge(diff_ready, 1)
            nc.scalar.activation(s.wt[:, 1], gap[:], ACT.Exp).then_inc(e2_ready, 1)
            a.by(nc.scalar.activation(s.A[:], s.A[:], ACT.Exp))
            act.wait_ge(act_done, a.n)
            nc.scalar.mul(s.A[:], s.A[:], -1.0)
            for i in range(DG * NCH):
                g, cols = i // NCH, slice(i % NCH * CH, (i % NCH + 1) * CH)
                act.wait_ge(dt_done, i + 1)
                act.wait_ge(relu_done, i + 1)
                nc.scalar.activation(spe[:, g, cols], bank(i % 4), ACT.Abs, bias=s.vec[:, 4 + g:5 + g]).then_inc(abs_done, 1)
            for i in range(DG * NCH):
                g, cols = i // NCH, slice(i % NCH * CH, (i % NCH + 1) * CH)
                act.wait_ge(abs_done, i + 1)
                nc.scalar.activation(spe[:, g, cols], spe[:, g, cols], ACT.Exp, scale=-1.0).then_inc(exp_done, 1)
            for i in range(DG * NCH):
                g, cols = i // NCH, slice(i % NCH * CH, (i % NCH + 1) * CH)
                act.wait_ge(rest_done, i + 1)
                nc.scalar.activation(spw[:, g, cols], spw[:, g, cols], ACT.Ln).then_inc(ln_done, 1)

        @block.tensor
        def _(pe):
            pe.wait_ge(ident_in, 16)

            def turn(src, k, ready):
                for c in range(NCH):
                    pe.wait_ge(ready, c + 1)
                    for q in range(4):
                        last = nc.tensor.transpose(bank(4 * k + c)[:, q * P:(q + 1) * P], src[:, 4 * c + q, :], s.ident[:])
                    last.then_inc(tr_done, 1)

            turn(s.xn, 0, xn_ready)
            pe.wait_ge(w_in, 16 * NW)
            pe.wait_ge(tr_copied, NCH)
            for t in range(NT):
                last = nc.tensor.matmul(bank(0)[:, 8 * t:8 * t + 8], s.xnT[:, t * P:(t + 1) * P], s.gate_w[:], start=True, stop=True)
            last.then_inc(score_done, 1)
            turn(xa, 1, xa_ready)
            pe.wait_ge(scores_copied, 1)
            for i in range(2 * DG * NCH):
                q, c = i // NCH, i % NCH
                pe.wait_ge(tr_copied, NCH + c + 1 if q == 0 else 2 * NCH)
                if i >= 4:
                    pe.wait_ge(proj_copied, i - 3)
                nc.tensor.matmul(bank(i % 4), in_w[:, q * P:(q + 1) * P], xaT[:, c * CH:(c + 1) * CH],
                                 start=True, stop=True).then_inc(proj_done, 1)
                if i == DG * NCH - 1:
                    pe.wait_ge(route_in, 64)
                    pe.wait_ge(mask_ready, 1)
                    pe.wait_ge(tr_copied, 2 * NCH)
                    flat = mask[:].rearrange("p t e -> p (t e)")
                    nc.tensor.matmul(bank(COUNT_BANK)[:, 0:P], before[:], flat, start=True, stop=True)
                    nc.tensor.matmul(bank(COUNT_BANK)[:, P:2 * P], every[:], flat, start=True, stop=True).then_inc(counted, 1)
            pe.wait_ge(counts_read, 1)
            for c in range(NCH):
                cols = slice(c * CH, (c + 1) * CH)
                pe.wait_ge(u_ready, DG)
                if c >= 2:
                    pe.wait_ge(draw_copied, c - 1)
                    pe.wait_ge(bc_split, c - 1)
                for g in range(DG):
                    last = nc.tensor.matmul(bank(6 + c % 2)[0:R, :], xw[:, g, :], s.u[:, g, cols], start=(g == 0), stop=(g == DG - 1))
                last.then_inc(dbc_done, 1)
                for g in range(DG):
                    last = nc.tensor.matmul(bank(4 + c % 2)[0:96, :], xbc[:, g, :], s.u[:, g, cols], start=(g == 0), stop=(g == DG - 1))
                last.then_inc(dbc_done, 1)
            pe.wait_ge(proj_copied, 2 * DG * NCH)
            for i in range(DG * NCH):
                g, c = i // NCH, i % NCH
                if i < NCH:
                    pe.wait_ge(draw_copied, c + 1)
                else:
                    pe.wait_ge(abs_done, i - 3)
                nc.tensor.matmul(bank(i % 4), dtw[:, g * P:(g + 1) * P], draw[:, c * CH:(c + 1) * CH],
                                 start=True, stop=True).then_inc(dt_done, 1)


SQ = 512
HALVES = L // SQ
UN = HALVES * NS
LAG = 3


def selective_scan(nc, s, I):
    sem = s.sem
    zeroed = sem("carry_zeroed")
    B_ready, C_ready, C_copied = sem("B_spread"), sem("C_spread"), sem("C_copied")
    dA_ready, dbu_done, h_done = sem("dA_ready"), sem("dBu_done"), sem("h_done")
    carry_done, prod_done, added = sem("carry_done"), sem("product_done"), sem("product_added")
    y_read, gated = sem("y_read"), sem("y_gated")
    bank = s.bank
    with ExitStack() as ctx:
        def sb(name, shape, dt=F32):
            return ctx.enter_context(nc.sbuf_tensor(name, shape, dt))

        sel = s.sel
        dA = sb("dA", [P, 2, DG, SQ])
        h = sb("h", [P, 4, DG, SQ])
        prod = sb("products", [P, 2, DG, SQ])
        Cs = sb("C_in_sbuf", [P, 2, SQ])
        carry = sb("carry", [P, NS, DG])
        yt = sb("y_skip", [P, DG, SQ])
        block = ctx.enter_context(nc.Block())
        Bb, Cb, Yb = (0, 1), (2, 3), ((4, 5), (6, 7))

        @block.sync
        def _(sp):
            for dst, src in ((s.w1[:], I["w1_t"]), (s.w3[:], I["w3_t"]), (s.w2[:], I["w2_t"])):
                sp.dma_start(dst, src).then_inc(s.expert_w_in, 16)

        @block.tensor
        def _(pe):
            pe.sem_inc(added, 2)
            pe.wait_ge(s.sel_in, 16)
            with pe.Fori(0, B) as b:
                def add_up(j):
                    half, n = j // NS, j % NS
                    if n == 0:
                        pe.wait_ge(y_read, b * HALVES + half + 1)
                    pe.wait_ge(prod_done, b * UN + j + 3)
                    for g in range(DG):
                        last = nc.tensor.matmul(bank(Yb[half][g]), s.ident[:], prod[:, j % 2, g, :], start=(n == 0), stop=(n == NS - 1))
                    last.then_inc(added, 1)

                for j in range(UN):
                    half, n = j // NS, j % NS
                    cols = bass.ts(b * HALVES + half, SQ)
                    pe.wait_ge(dbu_done, b * UN + j + 1)
                    nc.tensor.matmul(bank(Bb[j % 2]), sel[:, 0, n, :], s.bc3[:, cols], start=True, stop=True).then_inc(B_ready, 1)
                    pe.wait_ge(C_copied, b * UN + j + 1)
                    nc.tensor.matmul(bank(Cb[j % 2]), sel[:, 1, n, :], s.bc3[:, cols], start=True, stop=True).then_inc(C_ready, 1)
                    if j >= LAG:
                        add_up(j - LAG)
                for j in range(UN - LAG, UN):
                    add_up(j)

        @block.scalar
        def _(act):
            act.sem_inc(C_copied, 2)
            with act.Fori(0, B) as b:
                for j in range(UN):
                    half, n = j // NS, j % NS
                    m, k = j % 2, b * UN + j
                    cols = bass.ts(b * HALVES + half, SQ)
                    act.wait_ge(h_done, k + 1)
                    act.wait_ge(prod_done, k + 1)
                    act.wait_ge(C_ready, k + 1)
                    nc.scalar.activation(Cs[:, m, :], bank(Cb[m]), ACT.Copy).then_inc(C_copied, 1)
                    for g in range(DG):
                        last = nc.scalar.activation(dA[:, m, g, :], s.delta[:, g, cols], ACT.Exp, scale=s.A[:, g, n:n + 1])
                    last.then_inc(dA_ready, 1)

        @block.vector
        def _(dve):
            dve.sem_inc(dbu_done, 2)
            dve.sem_inc(h_done, 2)
            dve.sem_inc(y_read, HALVES)
            with dve.Fori(0, B) as b:
                def input_of(j):
                    k = b * UN + j
                    dve.wait_ge(B_ready, k + 1)
                    if j >= 4:
                        dve.wait_ge(prod_done, k - 1)
                        dve.wait_ge(carry_done, k - 3)
                    nc.vector.tensor_tensor(h[:, j % 4], s.du[:, :, bass.ts(b * HALVES + j // NS, SQ)],
                                            bc(bank(Bb[j % 2])[:, None, :], [P, DG, SQ]), ALU.mult).then_inc(dbu_done, 1)

                def carry_of(j):
                    dve.wait_ge(h_done, b * UN + j + 3)
                    nc.vector.tensor_copy(carry[:, j % NS, :], h[:, j % 4, :, SQ - 1]).then_inc(carry_done, 1)

                def gate(half):
                    cols = bass.ts(b * HALVES + half, SQ)
                    dve.wait_ge(added, b * UN + (half + 1) * NS + 2)
                    for g in range(DG):
                        last = nc.vector.scalar_tensor_tensor(out=yt[:, g, :], in0=s.u[:, g, cols], scalar=s.vec[:, 6 + g:7 + g],
                                                              in1=bank(Yb[half][g]), op0=ALU.mult, op1=ALU.add)
                    last.then_inc(y_read, 1)
                    dve.wait_ge(y_read, b * HALVES + half + HALVES + 1)
                    nc.vector.tensor_tensor(s.u[:, :, cols], yt[:], s.zs[:, :, cols], ALU.mult).then_inc(gated, 1)
                    dve.wait_ge(gated, b * HALVES + half + 1)

                dve.wait_ge(prod_done, b * UN + 2)
                nc.vector.memset(carry[:], 0.0).then_inc(zeroed, 1)
                input_of(0)
                dve.wait_ge(zeroed, b + 1)
                for j in range(UN):
                    m, n, k = j % 4, j % NS, b * UN + j
                    if j + 1 < UN:
                        input_of(j + 1)
                    dve.wait_ge(dbu_done, k + 3)
                    dve.wait_ge(dA_ready, k + 1)
                    if j >= NS:
                        dve.wait_ge(carry_done, k - NS + 1)
                    for g in range(DG):
                        last = nc.vector.tensor_tensor_scan(h[:, m, g, :], dA[:, j % 2, g, :], h[:, m, g, :], carry[:, n, g:g + 1],
                                                            ALU.mult, ALU.add)
                    last.then_inc(h_done, 1)
                    if j:
                        carry_of(j - 1)
                    if j == NS + LAG + 2:
                        gate(0)
                carry_of(UN - 1)
                dve.wait_ge(carry_done, (b + 1) * UN)
                gate(HALVES - 1)

        @block.gpsimd
        def _(pool):
            pool.sem_inc(prod_done, 2)
            with pool.Fori(0, B) as b:
                for j in range(UN):
                    m, k = j % 2, b * UN + j
                    pool.wait_ge(h_done, k + 3)
                    pool.wait_ge(C_copied, k + 3)
                    pool.wait_ge(added, k + 1)
                    nc.gpsimd.tensor_tensor(prod[:, m], h[:, j % 4], bc(Cs[:, m, None, :], [P, DG, SQ]), ALU.mult).then_inc(prod_done, 1)


def slots(eng, step):
    pairs = SLOTS // 2
    for m in range(2):
        step(0, m)
    with eng.Fori(1, pairs - 1) as q:
        for m in range(2):
            step(q, m)
    for q in (pairs - 1, pairs):
        for m in range(2):
            step(q, m)


def neighbour(q, m, by):
    q, m = q + (m + by) // 2, (m + by) % 2
    if isinstance(q, int) and not 0 <= q < SLOTS // 2:
        return None
    return q, m


def experts(nc, s, I):
    sem = s.sem
    rows_in = [sem(f"slot_rows_in_{m}") for m in range(2)]
    xt_done, xt_copied = sem("slot_xT_done"), sem("slot_xT_copied")
    up_done, silu_done, g_done = sem("slot_up_done"), sem("slot_silu_done"), sem("slot_gated")
    gt_done, gt_copied, y_done, y_copied = sem("slot_gT_done"), sem("slot_gT_copied"), sem("slot_y_done"), sem("slot_y_copied")
    y_out = [sem(f"slot_y_out_{m}") for m in range(2)]
    bank = s.bank
    with ExitStack() as ctx:
        def sb(name, shape, dt=F32):
            return ctx.enter_context(nc.sbuf_tensor(name, shape, dt))

        xs = sb("slot_x", [P, 2, D])
        xsT = sb("slot_xT", [P, 2, P])
        sg = sb("slot_silu", [P, 2, 512])
        gg = sb("slot_g", [P, 2, 512])
        gT = sb("slot_gT", [P, 2, 512])
        ys = sb("slot_y", [P, 2, D])
        block = ctx.enter_context(nc.Block())
        G_BANK, Y_BANK = 6, 7

        @block.sync
        def _(sp):
            with sp.Fori(0, SLOTS // 2) as q:
                for m in range(2):
                    k = q * 2 + m
                    sp.wait_ge(xt_done, k + 1)
                    sp.dma_start(xs[:, m, :], s.rows_in[bass.ts(k, P), :]).then_inc(rows_in[m], 16)

        @block.gpsimd
        def _(pool):
            with pool.Fori(0, SLOTS // 2) as q:
                for m in range(2):
                    k = q * 2 + m
                    pool.wait_ge(y_copied, k + 2)
                    pool.dma_start(s.rows_out[bass.ts(k, P), :], ys[:, m, :]).then_inc(y_out[m], 16)
            for m in range(2):
                pool.wait_ge(y_out[m], 16 * (SLOTS // 2))

        @block.tensor
        def _(pe):
            pe.sem_inc(xt_done, 2)
            pe.sem_inc(y_done, 2)
            pe.sem_inc(up_done, 2)
            pe.sem_inc(gt_done, 2)
            pe.wait_ge(s.expert_w_in, 48)

            def expert_of(k):
                return pe.value_load(s.slot_e[0:1, bass.ts(k, 1)], min_val=0, max_val=7)

            def turn_rows(q, m):
                k = q * 2 + m
                pe.wait_ge(rows_in[m], (q + 1) * 16)
                pe.wait_ge(xt_copied, k + 1)
                nc.tensor.transpose(bank(m)[:, 0:P], xs[:, m, :], s.ident[:]).then_inc(xt_done, 1)

            def multiply_up(q, m):
                k = q * 2 + m
                e = expert_of(k)
                pe.wait_ge(xt_copied, k + 3)
                pe.wait_ge(g_done, k + 1)
                nc.tensor.matmul(bank(2 + m), xsT[:, m, :], s.w1[:, e, :], start=True, stop=True)
                nc.tensor.matmul(bank(4 + m), xsT[:, m, :], s.w3[:, e, :], start=True, stop=True).then_inc(up_done, 1)

            def turn_products(q, m):
                k = q * 2 + m
                pe.wait_ge(g_done, k + 3)
                pe.wait_ge(gt_copied, k + 1)
                for c in range(4):
                    last = nc.tensor.transpose(bank(G_BANK)[:, c * P:(c + 1) * P], gg[:, m, c * P:(c + 1) * P], s.ident[:])
                last.then_inc(gt_done, 1)

            def multiply_down(q, m):
                k = q * 2 + m
                e = expert_of(k)
                pe.wait_ge(gt_copied, k + 2)
                pe.wait_ge(y_copied, k + 1)
                for c in range(4):
                    last = nc.tensor.matmul(bank(Y_BANK)[:, 0:D], gT[:, m, c * P:(c + 1) * P], s.w2[:, e, c, :], start=(c == 0), stop=(c == 3))
                last.then_inc(y_done, 1)

            def step(q, m):
                for by, part in ((1, turn_rows), (0, multiply_up), (-1, turn_products), (-2, multiply_down)):
                    at = neighbour(q, m, by)
                    if at:
                        part(*at)

            turn_rows(0, 0)
            slots(pe, step)

        @block.scalar
        def _(act):
            act.sem_inc(xt_copied, 2)

            def copy_rows(q, m):
                k = q * 2 + m
                act.wait_ge(xt_done, k + 3)
                act.wait_ge(up_done, k + 1)
                nc.scalar.activation(xsT[:, m, :], bank(m)[:, 0:P], ACT.Copy).then_inc(xt_copied, 1)

            def silu(q, m):
                k = q * 2 + m
                act.wait_ge(g_done, k + 1)
                act.wait_ge(up_done, k + 3)
                nc.scalar.activation(sg[:, m], bank(2 + m), ACT.Silu).then_inc(silu_done, 1)

            def step(q, m):
                for by, part in ((1, copy_rows), (0, silu)):
                    at = neighbour(q, m, by)
                    if at:
                        part(*at)

            copy_rows(0, 0)
            slots(act, step)

        @block.vector
        def _(dve):
            dve.sem_inc(g_done, 2)
            dve.sem_inc(gt_copied, 1)
            dve.sem_inc(y_copied, 1)

            def gate(q, m):
                k = q * 2 + m
                dve.wait_ge(silu_done, k + 1)
                dve.wait_ge(gt_done, k + 1)
                nc.vector.tensor_tensor(gg[:, m], sg[:, m], bank(4 + m), ALU.mult).then_inc(g_done, 1)

            def copy_products(q, m):
                k = q * 2 + m
                dve.wait_ge(gt_done, k + 3)
                dve.wait_ge(y_done, k + 1)
                nc.vector.tensor_copy(gT[:, m], bank(G_BANK)).then_inc(gt_copied, 1)

            def copy_out(q, m):
                k = q * 2 + m
                dve.wait_ge(y_done, k + 3)
                if not isinstance(q, int) or q:
                    dve.wait_ge(y_out[m], q * 16)
                nc.vector.tensor_copy(ys[:, m], bank(Y_BANK)[:, 0:D]).then_inc(y_copied, 1)

            def step(q, m):
                for by, part in ((0, gate), (-1, copy_products), (-2, copy_out)):
                    at = neighbour(q, m, by)
                    if at:
                        part(*at)

            slots(dve, step)


def first_layer_out(nc, s, I):
    sem = s.sem
    w_in, gathered, o_done, dve_done = sem("out_w_loaded"), sem("rows_gathered"), sem("out_done"), s.tally.sem
    bank = s.bank
    with ExitStack() as ctx:
        def sb(name, shape, dt=F32):
            return ctx.enter_context(nc.sbuf_tensor(name, shape, dt))

        ow = sb("out_w_t", [P, DG, D])
        yr = sb("expert_rows", [P, 2, NT, D])
        block = ctx.enter_context(nc.Block())

        @block.sync
        def _(sp):
            sp.dma_start(ow[:], I["out_w_t"].rearrange("(g p) d -> p g d", p=P)).then_inc(w_in, 16)

        @block.gpsimd
        def _(pool):
            for i in range(NT):
                for k in range(2):
                    nc.gpsimd.indirect_dma_start(out=yr[:, k, i, :], out_offset=None, in_=s.rows_out,
                                                 in_offset=bass.IndirectOffsetOnAxis(ap=s.pos[:, k, i:i + 1], axis=0),
                                                 bounds_check=SLOTS * P - 1).then_inc(gathered, 16)

        @block.tensor
        def _(pe):
            pe.wait_ge(w_in, 16)
            for i in range(NT):
                for g in range(DG):
                    last = nc.tensor.matmul(bank(i // 4)[:, i % 4 * P:(i % 4 + 1) * P], s.u[:, g, i * P:(i + 1) * P], ow[:, g, :],
                                            start=(g == 0), stop=(g == DG - 1))
                if i % 4 == 3:
                    last.then_inc(o_done, 1)

        @block.vector
        def _(dve):
            t = s.tally

            def link(ins):
                dve.wait_ge(dve_done, t.by(ins))

            link(nc.vector.tensor_tensor(s.x[:], s.x[:], s.xn[:], ALU.add))
            for i in range(4):
                dve.wait_ge(o_done, i + 1)
                v = s.x[:, 4 * i:4 * i + 4, :]
                t.by(nc.vector.tensor_tensor(v, v, bank(i).rearrange("p (t d) -> p t d", t=4), ALU.add))
            dve.wait_ge(gathered, 32 * NT)
            for k in range(2):
                link(nc.vector.tensor_tensor(yr[:, k], yr[:, k], bc(s.wt[:, k, :, None], [P, NT, D]), ALU.mult))
                link(nc.vector.tensor_tensor(s.x[:], s.x[:], yr[:, k], ALU.add))


NH = 8
DH = D // NH
HG = 4
TPB = L // P
Q_PARTS = ((0, 0, 1), (0, 2, 1))
K_PARTS = ((0, 1, 0), (2, 0, 1))
SCALE = float(D) ** -0.5


def attention_operands(nc, s, I):
    sem = s.sem
    consts, dve_done = sem("l1_constants"), s.tally.sem
    var_ready, rstd_ready = sem("l1_var_ready"), sem("l1_rstd_ready")
    xb_ready, xq_ready, half_ready, pad_ready = sem("xb_ready"), sem("xq_ready"), sem("l1_half_ready"), sem("l1_padded")
    tr_done, tr_copied = sem("l1_transposed"), sem("l1_transposes_copied")
    logits_done, logits_copied, bias_ready = sem("logits_done"), sem("logits_copied"), sem("l1_biases")
    q_done, k_done, q_copied, k_copied = sem("q_done"), sem("k_done"), sem("q_copied"), sem("k_copied")
    v_done, v_read, qk_ready, s3_done = sem("v_done"), sem("v_read"), sem("next_key_products"), sem("next_key_scores_done")
    psi_done, turned, his, rest, mids, parts_ready = (
        sem("psi_done"), sem("turned"), sem("high_parts"), sem("rests"), sem("middle_parts"), sem("parts_ready"))
    parts_out = [sem(f"parts_out_{m}") for m in range(2)]
    bank = s.bank
    V_BANK, VNEXT_BANK, S3_BANK = 5, 6, 7
    with ExitStack() as ctx:
        def sb(name, shape, dt=F32):
            return ctx.enter_context(nc.sbuf_tensor(name, shape, dt))

        xq = sb("xq", [P, NT, D])
        norm_tmp = norm_tensors(sb, "l1_norm")
        half = sb("l1_half", [P, NT])
        xbT = sb("xbT", [P, T])
        xqT = sb("xqT", [P, T + 1])
        hw = sb("head_w", [P, 5, D])
        wg = sb("wg", [P, 8])
        hsel = sb("head_selector", [P, NH])
        turns = sb("turns", [P, 4, L])
        bv = sb("bv_row", [P, D])
        full = sb("operands", [P, 4, T + 1])
        vq = sb("q_plus_v", [P, T + 1])
        prod = sb("next_key_product", [P, 2, CH])
        t2 = sb("turn_work", [P, 2, CH])
        rem = sb("remainder", [P, 4, CH])
        part = sb("parts", [P, 2, 3 * 4, CH], BF16)
        bias2 = sb("l1_bias", [P, 2])
        corner = sb("last_token", [P, 2], BF16)
        block = ctx.enter_context(nc.Block())
        NCONST = 6

        @block.sync
        def _(sp):
            for dst, src in ((wg[:], I["L1_ffn_wg"]), (hw[:], I["head_w"]), (bv[:], I["rows"][3:4].squeeze(0).partition_broadcast(P)),
                             (hsel[:], I["head_selector"]), (corner[:], I["masks"][:, 4 * P:4 * P + 2]), (turns[:], I["turns"])):
                sp.dma_start(dst, src).then_inc(consts, 16)
            for c in range(NCH):
                sp.wait_ge(parts_ready, 2 * (c + 1))
                for h in range(NH):
                    sp.dma_start(s.parts[c // 2, h // HG, :, :, h % HG, c % 2 * CH:(c % 2 + 1) * CH],
                                 part[DH * h:DH * (h + 1), c % 2]).then_inc(parts_out[c % 2], 16)
            for m in range(2):
                sp.wait_ge(parts_out[m], NCH // 2 * 16 * NH)

        @block.gpsimd
        def _(pool):
            nc.gpsimd.memset(half[:], -0.5).then_inc(half_ready, 1)
            pool.wait_ge(half_ready, 1)
            reciprocal_roots(nc, pool, norm_tmp, half, var_ready, rstd_ready)
            for c in range(NCH):
                pool.wait_ge(mids, c + 1)
                if c >= 2:
                    pool.wait_ge(parts_out[c % 2], 16 * NH)
                nc.gpsimd.tensor_tensor(part[:, c % 2, 10:12], rem[:, 2:4], part[:, c % 2, 6:8], ALU.subtract).then_inc(parts_ready, 1)

        @block.vector
        def _(dve):
            t = s.tally

            def link(ins):
                dve.wait_ge(dve_done, t.by(ins))

            t.by(nc.vector.memset(vq[:, T:T + 1], 0.0))
            t.by(nc.vector.memset(full[:, 3, T:T + 1], 0.0))
            link(nc.vector.memset(xqT[:, T:T + 1], 0.0))
            dve.sem_inc(pad_ready, 1)
            t.by(nc.vector.tensor_tensor(bias2[:, 0:1], s.vec[:, 10:11], s.vec[:, 12:13], ALU.add))
            link(nc.vector.tensor_tensor(bias2[:, 1:2], s.vec[:, 10:11], s.vec[:, 13:14], ALU.add))
            dve.sem_inc(bias_ready, 1)
            two_norms(nc, dve, t, s.x, s.xb, xq, norm_tmp, None, var_ready, rstd_ready, xb_ready, xq_ready)
            dve.wait_ge(consts, 16 * NCONST)
            for c in range(NCH):
                cols = slice(c * CH, (c + 1) * CH)
                tiles = slice(4 * c, 4 * c + 4)
                dve.wait_ge(v_done, c + 1)
                for dst, y in ((s.vals, V_BANK), (s.v_next, VNEXT_BANK)):
                    last = t.by(nc.vector.tensor_tensor(dst[:, tiles], bank(y).rearrange("p (t d) -> p t d", t=4),
                                                        bc(bv[:, None, :], [P, 4, D]), ALU.add))
                dve.wait_ge(dve_done, last)
                dve.sem_inc(v_read, 1)
                dve.wait_ge(q_copied, 2 * (c + 1))
                dve.wait_ge(k_copied, min(c + 2, NCH))
                if c >= 2:
                    dve.wait_ge(s3_done, c - 1)
                nc.vector.tensor_tensor(prod[:, c % 2], full[:, 0, cols], full[:, 3, c * CH + 1:(c + 1) * CH + 1], ALU.mult).then_inc(qk_ready, 1)

            def turn(c):
                cols, cc = slice(c * CH, (c + 1) * CH), slice(c % 2 * CH, (c % 2 + 1) * CH)
                dve.wait_ge(psi_done, c + 1)
                for k in range(2):
                    y = 4 * (c % 2) + 2 * k
                    t.by(nc.vector.tensor_tensor(full[:, 1 + k, cols], bank(y), turns[:, 2 * k, cc], ALU.mult))
                    last = t.by(nc.vector.tensor_tensor(t2[:, k], bank(y + 1), turns[:, 2 * k + 1, cc], ALU.mult))
                dve.wait_ge(dve_done, last)
                link(nc.vector.tensor_tensor(full[:, 1:3, cols], full[:, 1:3, cols], t2[:], ALU.add))
                dve.sem_inc(turned, 1)

            def rests(c):
                dve.wait_ge(his, c + 1)
                if c:
                    dve.wait_ge(parts_ready, 2 * c)
                link(nc.vector.tensor_tensor(rem[:], full[:, :, c * CH:(c + 1) * CH], part[:, c % 2, 0:4], ALU.subtract))
                dve.sem_inc(rest, 1)

            def low(c):
                dve.wait_ge(mids, c + 1)
                nc.vector.tensor_tensor(part[:, c % 2, 8:10], rem[:, 0:2], part[:, c % 2, 4:6], ALU.subtract).then_inc(parts_ready, 1)

            turn(0)
            dve.wait_ge(s3_done, NCH)
            link(nc.vector.tensor_copy(s.s3[:].rearrange("p t h -> p (t h)"), bank(S3_BANK)[:, 0:NT * NH]))
            dve.sem_inc(v_read, 1)
            for b in range(B):
                i = (b + 1) * TPB - 1
                link(nc.vector.tensor_tensor(s.s3[:, i, :], s.s3[:, i, :], bc(corner[:, 0:1], [P, NH]), ALU.add))
            rests(0)
            for c in range(NCH):
                if c + 1 < NCH:
                    turn(c + 1)
                low(c)
                if c + 1 < NCH:
                    rests(c + 1)

        @block.scalar
        def _(act):
            for c in range(NCH):
                act.wait_ge(tr_done, c + 1)
                nc.scalar.activation(xbT[:, c * CH:(c + 1) * CH], bank(c), ACT.Copy).then_inc(tr_copied, 1)
            for c in range(NCH):
                act.wait_ge(tr_done, NCH + c + 1)
                nc.scalar.activation(xqT[:, c * CH:(c + 1) * CH], bank(4 + c), ACT.Identity,
                                     scale=s.vec[:, 8:9], bias=s.vec[:, 9:10]).then_inc(tr_copied, 1)
            act.wait_ge(bias_ready, 1)
            for c in range(NCH):
                cols = slice(c * CH, (c + 1) * CH)
                act.wait_ge(k_done, c + 1)
                nc.scalar.activation(full[:, 3, cols], bank(3 + c % 2), ACT.Identity, bias=s.vec[:, 11:12]).then_inc(k_copied, 1)
                act.wait_ge(q_done, c + 1)
                nc.scalar.activation(full[:, 0, cols], bank(1 + c % 2), ACT.Identity, bias=bias2[:, 0:1]).then_inc(q_copied, 1)
                nc.scalar.activation(vq[:, cols], bank(1 + c % 2), ACT.Identity, bias=bias2[:, 1:2]).then_inc(q_copied, 1)
            act.wait_ge(logits_done, 1)
            nc.scalar.activation(s.logits[:].rearrange("p t e -> p (t e)"), bank(0)[:, 0:8 * NT], ACT.Copy).then_inc(logits_copied, 1)

            def high(c):
                act.wait_ge(turned, c + 1)
                act.wait_ge(k_copied, NCH)
                act.wait_ge(q_copied, 2 * NCH)
                if c >= 2:
                    act.wait_ge(parts_out[c % 2], 16 * NH)
                nc.scalar.activation(part[:, c % 2, 0:4], full[:, :, c * CH:(c + 1) * CH], ACT.Copy).then_inc(his, 1)

            def middle(c):
                act.wait_ge(rest, c + 1)
                nc.scalar.activation(part[:, c % 2, 4:8], rem[:], ACT.Copy).then_inc(mids, 1)

            high(0)
            for c in range(NCH):
                middle(c)
                if c + 1 < NCH:
                    high(c + 1)

        @block.tensor
        def _(pe):
            for k, (src, ready) in enumerate(((s.xb, xb_ready), (xq, xq_ready))):
                for c in range(NCH):
                    pe.wait_ge(ready, c + 1)
                    for q in range(4):
                        last = nc.tensor.transpose(bank(4 * k + c)[:, q * P:(q + 1) * P], src[:, 4 * c + q, :], s.ident[:])
                    last.then_inc(tr_done, 1)
            pe.wait_ge(consts, 16 * NCONST)
            pe.wait_ge(pad_ready, 1)
            pe.wait_ge(tr_copied, 2 * NCH)
            for c in range(NCH):
                cols = slice(c * CH, (c + 1) * CH)
                if c >= 2:
                    pe.wait_ge(k_copied, c - 1)
                    pe.wait_ge(q_copied, 2 * (c - 1))
                nc.tensor.matmul(bank(3 + c % 2), hw[:, 1], xqT[:, cols], start=True, stop=True).then_inc(k_done, 1)
                nc.tensor.matmul(bank(1 + c % 2), hw[:, 0], xqT[:, cols], start=True, stop=True).then_inc(q_done, 1)
                if c:
                    pe.wait_ge(v_read, c)
                for q in range(4):
                    i = 4 * c + q
                    nc.tensor.matmul(bank(V_BANK)[:, q * P:(q + 1) * P], xqT[:, i * P:(i + 1) * P], hw[:, 2], start=True, stop=True)
                    last = nc.tensor.matmul(bank(VNEXT_BANK)[:, q * P:(q + 1) * P], xqT[:, i * P + 1:(i + 1) * P + 1], hw[:, 2], start=True, stop=True)
                last.then_inc(v_done, 1)
            for t in range(NT):
                last = nc.tensor.matmul(bank(0)[:, 8 * t:8 * t + 8], xbT[:, t * P:(t + 1) * P], wg[:], start=True, stop=True)
            last.then_inc(logits_done, 1)
            for c in range(NCH):
                pe.wait_ge(qk_ready, c + 1)
                for q in range(4):
                    i = 4 * c + q
                    last = nc.tensor.matmul(bank(S3_BANK)[:, NH * i:NH * (i + 1)], prod[:, c % 2, q * P:(q + 1) * P], hsel[:], start=True, stop=True)
                last.then_inc(s3_done, 1)
            pe.wait_ge(logits_copied, 1)
            pe.wait_ge(k_copied, NCH)
            pe.wait_ge(q_copied, 2 * NCH)
            for c in range(NCH):
                cols, nxt = slice(c * CH, (c + 1) * CH), slice(c * CH + 1, (c + 1) * CH + 1)
                if c == 1:
                    pe.wait_ge(v_read, NCH + 1)
                if c >= 2:
                    pe.wait_ge(turned, c - 1)
                for k in range(2):
                    y = 4 * (c % 2) + 2 * k
                    nc.tensor.matmul(bank(y), hw[:, 3], vq[:, (cols, nxt)[k]], start=True, stop=True)
                    last = nc.tensor.matmul(bank(y + 1), hw[:, 4], vq[:, (cols, nxt)[k]], start=True, stop=True)
                last.then_inc(psi_done, 1)


E = 8
CAPACITY = T // E
EPG = E // (2 * (B - 1))
UNITS = 2 * HG + 1
GROUPS = B * NH // HG
LOADS = 16 * 9


def attention(nc, s, I):
    sem = s.sem
    consts, ones_ready, v_copied = sem("attention_constants"), sem("ones_rows_ready"), sem("group_values_ready")
    route_in = sem("l1_route_constants")
    sin_in = [sem(f"sinusoids_in_{g}") for g in range(2)]
    first_in = [sem(f"stack_first_pass_{g}") for g in range(2)]
    second_in = [sem(f"stack_second_pass_{g}") for g in range(2)]
    max_in = [sem(f"max_rows_in_{g}") for g in range(2)]
    max_done, max_read = sem("max_scores_done"), sem("max_scores_read")
    mx_ready, split = sem("max_ready"), sem("max_split")
    score_done, exp_done, pv_done, pv2_done = sem("score_done"), sem("exp_done"), sem("pv_done"), sem("pv_diagonal_done")
    ctx_done, ctx_read, dve_done = sem("context_done"), sem("context_read"), sem("attention_dve")
    gap_ready, exps_ready, mask_ready, counted, counts_read = (
        sem("logit_gap_ready"), sem("logit_exps_ready"), sem("l1_mask_ready"), sem("l1_counted"), sem("l1_counts_read"))
    places_ready, scattered, moe_in, moe_out, gathered = (
        sem("l1_places_ready"), sem("l1_rows_scattered"), sem("moe_tiles_in"), sem("moe_tiles_out"), sem("moe_rows_gathered"))
    moe_turned, moe_xT, moe_done, moe_read, added = (
        sem("moe_rows_turned"), sem("moe_rows_turned_copied"), sem("moe_product_done"), sem("moe_product_read"), sem("moe_added"))
    bank = s.bank
    PV, RING, MAXRING, MOE = (0, 1), (2, 3, 4), (5, 6), 7
    with ExitStack() as ctx:
        def sb(name, shape, dt=F32):
            return ctx.enter_context(nc.sbuf_tensor(name, shape, dt))

        Q = sb("query_stacks", [99, 2, 2, 2, HG, L], BF16)
        K = sb("key_stacks", [99, 2, 2, HG, L], BF16)
        W = sb("exp_scores", [P, 2, HG, CH])
        W2 = sb("exp_diagonal", [P, 2, HG, P])
        V = sb("group_values", [P, TPB, HG, 32])
        xg = sb("moe_rows", [P, TPB, D])
        xgT = sb("moe_rows_turned", [P, P])
        we = sb("moe_w", [P, EPG, D])
        be = sb("moe_b", [1, EPG, D])
        ones = sb("ones_row", [1, P])
        before = sb("l1_before", [P, P])
        every = sb("l1_every", [P, P])
        exp_no = sb("l1_expert_no", [P, E])
        behind = sb("rows_behind", [P, NT])
        lmax = sb("logit_max", [P, NT])
        lg = sb("logit_gap", [P, NT, E])
        ex = sb("logit_exp", [P, NT, E])
        top = sb("l1_top", [P, NT, 8])
        idx = sb("l1_top_index", [P, NT, 8], U32)
        mask = sb("l1_mask", [P, NT, E])
        tot = sb("l1_totals", [P, E, NT])
        incl = sb("l1_inclusive", [P, E, NT])
        keep = sb("l1_keep", [P, E, NT])
        pos = sb("l1_pos", [P, NT, E])
        idf = sb("l1_top_index_f", [P, NT])
        loc = sb("l1_location", [P, NT])
        kept = sb("l1_kept", [P, NT])
        gates = sb("l1_gates", [P, NT])
        place = sb("l1_places", [P, 2, NT], U32)
        masks = sb("diagonal_masks", [P, 4 * P + 2], BF16)
        identb = sb("identity_bf16", [P, P], BF16)
        cm = sb("chunk_maxima", [P, TPB, HG, 3])
        mx = sb("row_maxima", [P, HG, TPB])
        mrest = sb("max_rest", [HG * TPB, P])
        mparts = sb("max_parts", [HG * TPB, 3, P], BF16)
        block = ctx.enter_context(nc.Block())

        def by_group(b, g, each, n):
            return b * (2 * each) + (g * each + n)

        STEP = TPB * UNITS
        assert EPG * CAPACITY == TPB * P
        MAXSTEP = STEP + 1
        FIRST, SECOND, FIRST_T, SECOND_T = (masks[:, q * P:(q + 1) * P] for q in range(4))

        @block.sync
        def _(sp):
            sp.dma_start(masks[:], I["masks"]).then_inc(consts, 16)
            sp.dma_start(identb[:], I["ident_bf"]).then_inc(consts, 16)
            for dst, src in ((before[:], I["before"]), (every[:], I["every"]), (exp_no[:], I["expert_numbers"]), (behind[:], I["rows_behind"])):
                sp.dma_start(dst, src).then_inc(route_in, 16)
            def load(b, g):
                if not (isinstance(b, int) and b == 0):
                    sp.wait_ge(ctx_done, b * 2 + g)
                parts = s.parts[b if isinstance(b, int) else bass.ts(b, 1), g]
                parts = parts if isinstance(b, int) else parts.squeeze(0)
                for ps, done in enumerate((first_in[g], second_in[g])):
                    for slot in range(3):
                        pq, pk, row = 4 * Q_PARTS[ps][slot], 4 * K_PARTS[ps][slot], 32 * slot
                        for dst, src in ((Q[row:row + DH, g, ps].rearrange("d f h c -> d f (h c)"),
                                          bc(parts[:, pq:pq + 1].rearrange("d f h c -> d f (h c)"), [DH, 2, HG * L])),
                                         (Q[row + DH:row + 2 * DH, g, ps], parts[:, pq + 1:pq + 3]),
                                         (K[row:row + DH, g, ps], parts[:, pk + 3])):
                            sp.dma_start(dst, src).then_inc(done, 16)

            def max_rows(b, g):
                sp.wait_ge(split, b * 2 + g + 2)
                for form in range(2):
                    for part in range(3):
                        sp.dma_start(Q[96 + part:97 + part, g, 0, form].rearrange("r h (t c) -> r (h t) c", t=TPB),
                                     mparts[:, part]).then_inc(max_in[g], 16)

            load(0, 0)
            load(0, 1)
            max_rows(0, 0)
            with sp.Fori(0, B - 1) as b:
                max_rows(b, 1)
                load(b + 1, 0)
                max_rows(b + 1, 0)
                load(b + 1, 1)
            max_rows(B - 1, 1)

        @block.gpsimd
        def _(pool):
            for g in range(2):
                for ps in range(2):
                    for slot in range(3):
                        pool.dma_start(K[32 * slot + DH:32 * slot + 2 * DH, g, ps],
                                       I["sinusoids"][64 * g:64 * g + 64, K_PARTS[ps][slot], :].rearrange("(h m) c -> m h c", h=HG)).then_inc(sin_in[g], 16)
            nc.gpsimd.memset(K[96:99, :, 0], 1.0).then_inc(ones_ready, 1)
            nc.gpsimd.memset(ones[:], 1.0).then_inc(ones_ready, 1)
            pool.wait_ge(ones_ready, 2)
            nc.gpsimd.memset(V[:], 0.0).then_inc(ones_ready, 1)
            pool.wait_ge(ones_ready, 3)
            nc.gpsimd.memset(V[:, :, :, DH:DH + 1], 1.0).then_inc(v_copied, 1)

            def copy_values(b, g):
                pool.wait_ge(ctx_done, b * 2 + g + 1)
                pool.wait_ge(v_copied, b * 2 + g + 1)
                nc.gpsimd.tensor_copy(V[:, :, :, 0:DH], s.vals[:, bass.ts(b, TPB), 64 * g:64 * (g + 1)].rearrange("p t (h d) -> p t h d", h=HG)
                                      ).then_inc(v_copied, 1)

            def moe_load(b, g):
                gi = b * 2 + g
                pool.dma_start(xg[:], s.rows2_in[bass.ts(gi, TPB * P)].rearrange("(t p) d -> p t d", p=P)).then_inc(moe_in, 16)
                pool.dma_start(we[:], I["moe_w"][:, bass.ts(gi, EPG)]).then_inc(moe_in, 16)
                pool.dma_start(be[:], I["L1_ffn_b"][None, bass.ts(gi, EPG)]).then_inc(moe_in, 16)

            def moe_store(b, g):
                gi = b * 2 + g
                pool.wait_ge(moe_read, gi * TPB + TPB + 1)
                pool.dma_start(s.rows2_out[bass.ts(gi, TPB * P)].rearrange("(t p) d -> p t d", p=P), xg[:]).then_inc(moe_out, 16)
                pool.wait_ge(moe_out, gi * 16 + 16)

            copy_values(0, 0)
            pool.wait_ge(places_ready, 1)
            for i in range(NT):
                nc.gpsimd.indirect_dma_start(out=s.rows2_in, out_offset=bass.IndirectOffsetOnAxis(ap=place[:, 0, i:i + 1], axis=0),
                                             in_=s.xb[:, i, :], in_offset=None, bounds_check=2 * T - 1).then_inc(scattered, 16)
            pool.wait_ge(scattered, 16 * NT)
            with pool.Fori(0, B - 1) as b:
                moe_load(b, 0)
                moe_store(b, 0)
                moe_load(b, 1)
                copy_values(b, 1)
                moe_store(b, 1)
                copy_values(b + 1, 0)
            for i in range(NT):
                nc.gpsimd.indirect_dma_start(out=s.xb[:, i, :], out_offset=None, in_=s.rows2_out,
                                             in_offset=bass.IndirectOffsetOnAxis(ap=place[:, 1, i:i + 1], axis=0),
                                             bounds_check=T - 1).then_inc(gathered, 16)
            copy_values(B - 1, 1)
            pool.wait_ge(gathered, 16 * NT)
            nc.gpsimd.tensor_tensor(s.xb[:], s.xb[:], bc(gates[:, :, None], [P, NT, D]), ALU.mult).then_inc(added, 1)
            pool.wait_ge(added, 1)
            nc.gpsimd.tensor_tensor(s.x[:], s.x[:], s.xb[:], ALU.add)

        @block.tensor
        def _(pe):
            pe.sem_inc(ctx_done, 1)
            pe.sem_inc(moe_done, 1)
            pe.sem_inc(pv_done, 2)
            pe.sem_inc(pv2_done, 2)
            pe.wait_ge(consts, 32)
            pe.wait_ge(sin_in[0], 96)
            pe.wait_ge(ones_ready, 3)
            pe.wait_ge(v_copied, 1)

            def max_unit(b, g, it, u):
                y = bank(MAXRING[(g * MAXSTEP + it * UNITS + u) % 2])
                pe.wait_ge(max_read, by_group(b, g, MAXSTEP, it * UNITS + u + 1))
                a, z = it * P, (it + 1) * P

                def product(h, form, lo, hi, at, start, stop):
                    return nc.tensor.matmul(y[:, lo - at:hi - at], Q[0:96, g, 0, form, h, a:z], K[0:96, g, 0, h, lo:hi], start=start, stop=stop)

                if u == 0:
                    for h in range(HG):
                        nc.tensor.matmul(y[:, h * P:(h + 1) * P], identb[:], SECOND, start=True, stop=False)
                        last = product(h, 1, a, z, a - h * P, False, True)
                    last.then_inc(max_done, 1)
                    return
                h, c = (u - 1) % HG, (u - 1) // HG
                lo, hi = c * CH, (c + 1) * CH
                if lo <= a < hi:
                    nc.tensor.matmul(y[:, a - lo:z - lo], identb[:], FIRST, start=True, stop=False)
                    last = product(h, 0, a, z, lo, False, True)
                if lo < min(a, hi):
                    last = product(h, 0, lo, min(a, hi), lo, True, True)
                if max(z, lo) < hi:
                    last = product(h, 1, max(z, lo), hi, lo, True, lo > z)
                    if lo <= z:
                        last = nc.tensor.matmul(y[:, z - lo:z - lo + 1], identb[:], masks[:, 4 * P:4 * P + 1], start=False, stop=True)
                last.then_inc(max_done, 1)

            def max_turned(b, g):
                pe.wait_ge(mx_ready, by_group(b, g, 1, 2))
                nc.tensor.transpose(bank(MAXRING[(g * MAXSTEP + STEP) % 2])[0:HG * TPB, 0:P], mx[:].rearrange("p h t -> p (h t)"), s.ident[:]).then_inc(max_done, 1)

            def score_unit(b, g, jt, u):
                y = bank(RING[u % 3])
                pe.wait_ge(exp_done, by_group(b, g, STEP, jt * UNITS + u + 1))
                a, z = jt * P, (jt + 1) * P

                def product(h, form, lo, hi, at, start, stop):
                    to = y[:, lo - at:hi - at]
                    nc.tensor.matmul(to, K[0:99, g, 0, h, a:z], Q[0:99, g, 0, form, h, lo:hi], start=start, stop=False)
                    return nc.tensor.matmul(to, K[0:96, g, 1, h, a:z], Q[0:96, g, 1, form, h, lo:hi], start=False, stop=stop)

                if u == 0:
                    for h in range(HG):
                        nc.tensor.matmul(y[:, h * P:(h + 1) * P], identb[:], SECOND_T, start=True, stop=False)
                        last = product(h, 1, a, z, a - h * P, False, True)
                    last.then_inc(score_done, 1)
                    return
                h, c = (u - 1) % HG, (u - 1) // HG
                lo, hi = c * CH, (c + 1) * CH
                if lo <= a < hi:
                    nc.tensor.matmul(y[:, a - lo:z - lo], identb[:], FIRST_T, start=True, stop=False)
                    last = product(h, 0, a, z, lo, False, True)
                if max(z, lo) < hi:
                    last = product(h, 0, max(z, lo), hi, lo, True, True)
                if lo < min(a, hi):
                    last = product(h, 1, lo, min(a, hi), lo, True, a > hi)
                    if a <= hi:
                        last = nc.tensor.matmul(y[:, a - 1 - lo:a - lo], identb[:], masks[:, 4 * P + 1:4 * P + 2], start=False, stop=True)
                last.then_inc(score_done, 1)

            def values(b, g, jt, c):
                pe.wait_ge(exp_done, by_group(b, g, STEP, jt * UNITS + 1 + HG * (c + 1) + 3))
                for h in range(HG):
                    last = nc.tensor.matmul(bank(PV[c])[32 * h:32 * h + 32, :], V[:, jt, h, :], W[:, c, h, :],
                                            start=(jt == 0), stop=(jt == TPB - 1))
                last.then_inc(pv_done, 1)

            def diagonal_values(g, jt):
                y, at = bank(PV[jt // 4]), jt % 4 * P
                for h in range(HG):
                    last = nc.tensor.matmul(y[32 * h:32 * h + 32, at:at + P], V[:, jt, h, :], W2[:, jt % 2, h, :], start=False, stop=False)
                last.then_inc(pv2_done, 1)

            def moe_turn(b, g, jt):
                if jt == 0:
                    pe.wait_ge(moe_in, by_group(b, g, 48, 48))
                pe.wait_ge(moe_read, by_group(b, g, TPB, jt + 1))
                nc.tensor.transpose(bank(MOE)[:, 0:P], xg[:, jt, :], s.ident[:]).then_inc(moe_turned, 1)

            def moe_multiply(b, g, jt):
                e = jt * P // CAPACITY
                pe.wait_ge(moe_xT, by_group(b, g, TPB, jt + 1))
                nc.tensor.matmul(bank(MOE)[:, P:2 * P], xgT[:], we[:, e, :], start=True, stop=False)
                nc.tensor.matmul(bank(MOE)[:, P:2 * P], ones[:], be[:, e, :], start=False, stop=True).then_inc(moe_done, 1)

            def scores_and_values(b, g, nb, ng, between, moe):
                for jt in range(TPB):
                    more = between[jt]
                    if jt == 1 and ng is not None:
                        pe.wait_ge(first_in[ng], LOADS * (nb + 1))
                    for u in range(UNITS):
                        score_unit(b, g, jt, u)
                        if moe and u == 1:
                            moe_turn(b, g, jt)
                        if moe and u == UNITS - 2:
                            moe_multiply(b, g, jt)
                        for it, v in more[u * len(more) // UNITS:(u + 1) * len(more) // UNITS]:
                            max_unit(nb, ng, it, v)
                        if u == HG and jt:
                            values(b, g, jt - 1, 1)
                        if u == HG and not jt:
                            pe.wait_ge(ctx_read, by_group(b, g, 2, 2))
                            pe.wait_ge(v_copied, by_group(b, g, 1, 2))
                    values(b, g, jt, 0)
                    diagonal_values(g, jt)
                values(b, g, TPB - 1, 1)
                pe.wait_ge(pv_done, by_group(b, g, 2 * TPB, 2 * TPB + 2))
                pe.wait_ge(pv2_done, by_group(b, g, TPB, TPB + 2))
                pe.sem_inc(ctx_done, 1)

            def maxima_alone(b, g):
                pe.wait_ge(first_in[g], LOADS * (b + 1))
                for it in range(TPB):
                    for u in range(UNITS):
                        max_unit(b, g, it, u)
                max_turned(b, g)

            def group(b, g, nb, ng, moe):
                pe.wait_ge(second_in[g], LOADS * (b + 1))
                pe.wait_ge(max_in[g], 96 * (b + 1))
                if nb is None:
                    scores_and_values(b, g, None, None, [[]] * TPB, moe)
                    return
                steps = [[], [0], [1], [2, 3], [4], [5], [6], [7]]
                scores_and_values(b, g, nb, ng, [[(it, u) for it in its for u in range(UNITS)] for its in steps], moe)
                max_turned(nb, ng)

            pe.wait_ge(route_in, 64)
            pe.wait_ge(mask_ready, 1)
            flat = mask[:].rearrange("p t e -> p (t e)")
            nc.tensor.matmul(bank(MOE)[:, 0:P], before[:], flat, start=True, stop=True)
            nc.tensor.matmul(bank(MOE)[:, P:2 * P], every[:], flat, start=True, stop=True).then_inc(counted, 1)
            maxima_alone(0, 0)
            pe.wait_ge(counts_read, 1)
            pe.wait_ge(sin_in[1], 96)
            with pe.Fori(0, B - 1) as b:
                group(b, 0, b, 1, True)
                group(b, 1, b + 1, 0, True)
            group(B - 1, 0, B - 1, 1, False)
            group(B - 1, 1, None, None, False)

        @block.scalar
        def _(act):
            act.sem_inc(exp_done, 3)
            act.sem_inc(moe_read, 1)
            act.wait_ge(gap_ready, 1)
            nc.scalar.activation(ex[:], lg[:], ACT.Exp).then_inc(exps_ready, 1)

            def group(b, g, moe):
                for jt in range(TPB):
                    for u in range(UNITS):
                        act.wait_ge(score_done, by_group(b, g, STEP, jt * UNITS + u + 1))
                        if u == 0:
                            act.wait_ge(pv2_done, by_group(b, g, TPB, jt + 1))
                            to = W2[:, jt % 2].rearrange("p h c -> p (h c)")
                        else:
                            h, c = (u - 1) % HG, (u - 1) // HG
                            if h == 0:
                                act.wait_ge(pv_done, by_group(b, g, 2 * TPB, jt * 2 + c + 1))
                            to = W[:, c, h, :]
                        nc.scalar.activation(to, bank(RING[u % 3]), ACT.Exp, scale=SCALE).then_inc(exp_done, 1)
                        if moe and u == 3:
                            act.wait_ge(moe_turned, by_group(b, g, TPB, jt + 1))
                            act.wait_ge(moe_done, by_group(b, g, TPB, jt + 1))
                            nc.scalar.activation(xgT[:], bank(MOE)[:, 0:P], ACT.Copy).then_inc(moe_xT, 1)
                    if moe:
                        act.wait_ge(moe_done, by_group(b, g, TPB, jt + 2))
                        nc.scalar.activation(xg[:, jt, :], bank(MOE)[:, P:2 * P], ACT.Copy).then_inc(moe_read, 1)

            with act.Fori(0, B - 1) as b:
                for g in range(2):
                    group(b, g, True)
            for g in range(2):
                group(B - 1, g, False)

        @block.vector
        def _(dve):
            dve.sem_inc(max_read, 2)
            dve.sem_inc(mx_ready, 1)
            dve.sem_inc(split, 1)
            dve.sem_inc(ctx_read, 2)

            LINKS = 4

            t = s.tally

            def link(ins):
                dve.wait_ge(t.sem, t.by(ins))

            def route():
                full = [P, NT, E]
                link(nc.vector.memset(keep[:], 1.0))
                t.by(nc.vector.memset(keep[:, :, 0:1], 0.0))
                link(nc.vector.reduce_max(lmax[:], s.logits[:], AX.X))
                nc.vector.tensor_tensor(lg[:], s.logits[:], bc(lmax[:, :, None], full), ALU.subtract).then_inc(gap_ready, 1)
                dve.wait_ge(exps_ready, 1)
                for i in range(NT):
                    last = t.by(nc.vector.max(top[:, i, :], ex[:, i, :]))
                dve.wait_ge(t.sem, last)
                for i in range(NT):
                    last = t.by(nc.vector.max_index(idx[:, i, :], top[:, i, :], ex[:, i, :]))
                dve.wait_ge(t.sem, last)
                link(nc.vector.tensor_copy(idf[:], idx[:, :, 0]))
                dve.wait_ge(route_in, 64)
                nc.vector.tensor_tensor(mask[:], bc(idf[:, :, None], full), bc(exp_no[:, None, :], full), ALU.is_equal).then_inc(mask_ready, 1)
                dve.wait_ge(mask_ready, 1)
                link(nc.vector.reduce_sum(lmax[:], ex[:], AX.X))
                link(nc.vector.reciprocal(lmax[:], lmax[:]))
                y = bank(MOE)
                count_before(nc, s, dve, link, mask, counted, tot, incl, keep, pos, y[:, 0:P], y[:, P:2 * P])
                dve.sem_inc(counts_read, 1)
                link(nc.vector.tensor_tensor(pos[:], pos[:], mask[:], ALU.mult))
                link(nc.vector.reduce_sum(loc[:], pos[:], AX.X))
                link(nc.vector.tensor_scalar(kept[:], loc[:], float(CAPACITY), None, ALU.is_lt))
                link(nc.vector.scalar_tensor_tensor(out=loc[:], in0=idf[:], scalar=float(CAPACITY), in1=loc[:], op0=ALU.mult, op1=ALU.add))
                link(nc.vector.tensor_tensor(gates[:], lmax[:], kept[:], ALU.mult))
                link(nc.vector.tensor_tensor(idf[:], loc[:], behind[:], ALU.subtract))
                link(nc.vector.tensor_tensor(idf[:], idf[:], kept[:], ALU.mult))
                link(nc.vector.tensor_tensor(place[:, 0], idf[:], behind[:], ALU.add))
                link(nc.vector.tensor_tensor(place[:, 1], loc[:], kept[:], ALU.mult))
                dve.sem_inc(places_ready, 1)

            def maxima(b, g):
                s3 = s.s3[:, bass.ts(b, TPB), HG * g:HG * (g + 1)]
                dve.wait_ge(mx_ready, by_group(b, g, 1, 1))
                for it in range(TPB):
                    for u in range(UNITS):
                        dve.wait_ge(max_done, by_group(b, g, MAXSTEP, it * UNITS + u + 1))
                        y = bank(MAXRING[(g * MAXSTEP + it * UNITS + u) % 2])
                        if u == 0:
                            nc.vector.reduce_max(cm[:, it, :, 2], y.rearrange("p (h c) -> p h c", h=HG), AX.X).then_inc(max_read, 1)
                        else:
                            h, c = (u - 1) % HG, (u - 1) // HG
                            nc.vector.reduce_max(cm[:, it, h, c:c + 1], y, AX.X).then_inc(max_read, 1)
                dve.wait_ge(max_read, by_group(b, g, MAXSTEP, STEP + 2))
                nc.vector.reduce_max(mx[:].rearrange("p h t -> p t h"), cm[:], AX.X).then_inc(dve_done, 1)
                dve.wait_ge(dve_done, by_group(b, g, LINKS, 1))
                mt = mx[:].rearrange("p h t -> p t h")
                nc.vector.tensor_tensor(mt, mt, s3, ALU.max).then_inc(mx_ready, 1)
                dve.wait_ge(mx_ready, by_group(b, g, 1, 2))
                nc.vector.tensor_tensor(s.next_gap[:, bass.ts(b, TPB), HG * g:HG * (g + 1)], s3, mt, ALU.subtract).then_inc(dve_done, 1)
                if g:
                    dve.wait_ge(max_in[0], 96 * (b + 1))
                elif not isinstance(b, int):
                    dve.wait_ge(max_in[1], 96 * b)
                turned = bank(MAXRING[(g * MAXSTEP + STEP) % 2])[0:HG * TPB, 0:P]
                dve.wait_ge(max_done, by_group(b, g, MAXSTEP, MAXSTEP))
                nc.vector.tensor_scalar(mparts[:, 0], turned, -1.0, None, ALU.mult).then_inc(dve_done, 1)
                dve.wait_ge(dve_done, by_group(b, g, LINKS, 3))
                nc.vector.scalar_tensor_tensor(out=mrest[:], in0=turned, scalar=-1.0, in1=mparts[:, 0],
                                               op0=ALU.mult, op1=ALU.subtract).then_inc(max_read, 1)
                dve.wait_ge(max_read, by_group(b, g, MAXSTEP, MAXSTEP + 2))
                nc.vector.tensor_copy(mparts[:, 1], mrest[:]).then_inc(dve_done, 1)
                dve.wait_ge(dve_done, by_group(b, g, LINKS, 4))
                nc.vector.tensor_tensor(mparts[:, 2], mrest[:], mparts[:, 1], ALU.subtract).then_inc(split, 1)

            def context(b, g):
                dve.wait_ge(ctx_done, by_group(b, g, 1, 2))
                nc.vector.tensor_copy(s.U[:, g, bass.ts(b * 2, CH)], bank(PV[0])).then_inc(ctx_read, 1)
                nc.vector.tensor_copy(s.U[:, g, bass.ts(b * 2 + 1, CH)], bank(PV[1])).then_inc(ctx_read, 1)

            route()
            maxima(0, 0)
            with dve.Fori(0, B - 1) as b:
                maxima(b, 1)
                context(b, 0)
                maxima(b + 1, 0)
                context(b, 1)
            maxima(B - 1, 1)
            context(B - 1, 0)
            context(B - 1, 1)


def second_layer_out(nc, s, I, out):
    sem = s.sem
    dve_done = s.tally.sem
    consts, e3_ready, ev_ready = sem("l1_out_constants"), sem("next_exp_ready"), sem("next_exp_values_ready")
    u_turned, u_read, ctx_ready, cT_done, cT_copied = (
        sem("context_turned"), sem("context_turned_read"), sem("token_context_ready"), sem("ctxT_done"), sem("ctxT_copied"))
    o_done, out_ready, out_sent, bo_added = sem("l1_o_done"), sem("out_ready"), sem("out_sent"), sem("bo_added")
    bank = s.bank
    U_BANKS, T_BANKS, O_BANKS = (0, 1, 2), (3, 4), (5, 6)
    NP = NT // 2
    with ExitStack() as ctx:
        def sb(name, shape, dt=F32):
            return ctx.enter_context(nc.sbuf_tensor(name, shape, dt))

        wo = sb("Wo", [P, D])
        bo = sb("bo_row", [P, D])
        e3 = sb("next_exp", [P, NT * NH])
        ev = sb("next_exp_v", [P, NT * NH, DH])
        num = sb("context_num", [P, 2, 2 * NH, DH])
        den = sb("context_den", [P, 2, 2 * NH])
        cT = sb("ctxT", [P, 2, 2 * P])
        block = ctx.enter_context(nc.Block())

        @block.sync
        def _(sp):
            for dst, src in ((wo[:], I["L1_attn_Wo"]), (bo[:], I["rows"][4:5].squeeze(0).partition_broadcast(P))):
                sp.dma_start(dst, src).then_inc(consts, 16)
            flat = out.rearrange("b (t p) d -> p (b t) d", p=P)
            for k in range(NP):
                sp.wait_ge(out_ready, k + 1)
                sp.dma_start(flat[:, 2 * k:2 * k + 2], s.x[:, 2 * k:2 * k + 2]).then_inc(out_sent, 16)
            sp.wait_ge(out_sent, 16 * NP)

        @block.gpsimd
        def _(pool):
            pool.wait_ge(consts, 32)
            nc.gpsimd.tensor_tensor(s.x[:], s.x[:], bc(bo[:, None, :], [P, NT, D]), ALU.add).then_inc(bo_added, 1)

        @block.tensor
        def _(pe):
            def turn_contexts(k):
                if k >= 3:
                    pe.wait_ge(u_read, k - 2)
                for i in range(2):
                    for g in range(2):
                        t = 2 * k + i
                        last = nc.tensor.transpose(bank(U_BANKS[k % 3])[:, (2 * i + g) * P:(2 * i + g + 1) * P], s.U[:, g, t * P:(t + 1) * P], s.ident[:])
                last.then_inc(u_turned, 1)

            def turn_back(k):
                pe.wait_ge(ctx_ready, k + 1)
                if k >= 2:
                    pe.wait_ge(cT_copied, k - 1)
                for i in range(2):
                    last = nc.tensor.transpose(bank(T_BANKS[k % 2])[:, i * P:(i + 1) * P],
                                               num[:, k % 2, NH * i:NH * (i + 1), :].rearrange("p h d -> p (h d)"), s.ident[:])
                last.then_inc(cT_done, 1)

            def output(k):
                pe.wait_ge(cT_copied, k + 1)
                if k >= 2:
                    pe.wait_ge(out_ready, k - 1)
                for i in range(2):
                    last = nc.tensor.matmul(bank(O_BANKS[k % 2])[:, i * P:(i + 1) * P], cT[:, k % 2, i * P:(i + 1) * P], wo[:], start=True, stop=True)
                last.then_inc(o_done, 1)

            for k in range(3):
                turn_contexts(k)
            pe.wait_ge(consts, 32)
            for k in range(NP):
                turn_back(k)
                if k:
                    output(k - 1)
                if k + 3 < NP:
                    turn_contexts(k + 3)
            output(NP - 1)

        @block.scalar
        def _(act):
            nc.scalar.activation(e3[:], s.next_gap[:].rearrange("p t h -> p (t h)"), ACT.Exp, scale=SCALE).then_inc(e3_ready, 1)
            for k in range(NP):
                act.wait_ge(cT_done, k + 1)
                if k >= 2:
                    act.wait_ge(o_done, k - 1)
                nc.scalar.activation(cT[:, k % 2], bank(T_BANKS[k % 2])[:, 0:2 * P], ACT.Copy).then_inc(cT_copied, 1)

        @block.vector
        def _(dve):
            t = s.tally

            def link(ins):
                dve.wait_ge(dve_done, t.by(ins))

            dve.wait_ge(e3_ready, 1)
            for b in range(B):
                hs = slice(b * TPB * NH, (b + 1) * TPB * NH)
                nc.vector.tensor_tensor(ev[:, hs], s.v_next[:].rearrange("p t (h d) -> p (t h) d", h=NH)[:, hs],
                                        bc(e3[:, hs, None], [P, TPB * NH, DH]), ALU.mult).then_inc(ev_ready, 1)

            def context(k):
                m = k % 2
                dve.wait_ge(ev_ready, B)
                dve.wait_ge(u_turned, k + 1)
                if k >= 2:
                    dve.wait_ge(cT_done, k - 1)
                y = bank(U_BANKS[k % 3]).rearrange("p (h d) -> p h d", d=32)
                hs = slice(2 * NH * k, 2 * NH * (k + 1))
                t.by(nc.vector.tensor_tensor(den[:, m], y[:, :, DH], e3[:, hs], ALU.add))
                link(nc.vector.tensor_tensor(num[:, m], y[:, :, 0:DH], ev[:, hs, :], ALU.add))
                dve.sem_inc(u_read, 1)
                link(nc.vector.reciprocal(den[:, m], den[:, m]))
                nc.vector.tensor_tensor(num[:, m], num[:, m], bc(den[:, m, :, None], [P, 2 * NH, DH]), ALU.mult).then_inc(ctx_ready, 1)

            def finish(k):
                dve.wait_ge(o_done, k + 1)
                dve.wait_ge(bo_added, 1)
                xs = s.x[:, 2 * k:2 * k + 2]
                nc.vector.tensor_tensor(xs, xs, bank(O_BANKS[k % 2])[:, 0:2 * P].rearrange("p (t d) -> p t d", t=2), ALU.add).then_inc(out_ready, 1)

            for k in range(NP):
                context(k)
                if k:
                    finish(k - 1)
            finish(NP - 1)


def build(nc, I, out):
    with ExitStack() as ctx:
        s = Shared()

        def sb(name, shape, dt=F32):
            return ctx.enter_context(nc.sbuf_tensor(name, shape, dt))

        s.sem = lambda name: ctx.enter_context(nc.semaphore(name))
        s.tally = Tally(s.sem("dve_steps"))
        banks = [ctx.enter_context(nc.psum_tensor(f"bank{i}", [P, CH], F32)) for i in range(8)]
        s.bank = lambda i: banks[i][:]
        s.rows_in = nc.dram_tensor("rows_by_expert", (SLOTS * P, D), F32, kind="Internal").ap()
        s.rows_out = nc.dram_tensor("expert_results", (SLOTS * P, D), F32, kind="Internal").ap()
        s.rows2_in = nc.dram_tensor("rows_by_second_expert", (2 * T, D), F32, kind="Internal").ap()
        s.rows2_out = nc.dram_tensor("second_expert_results", (T, D), F32, kind="Internal").ap()
        s.expert_w_in = s.sem("expert_weights_loaded")
        s.sel_in = s.sem("selectors_loaded")
        s.ident = sb("identity", [P, P])
        s.vec = sb("vectors_sb", [P, 24])
        s.x = sb("x", [P, NT, D])
        with ExitStack() as l0:
            def sb0(name, shape, dt=F32, c=l0):
                return c.enter_context(nc.sbuf_tensor(name, shape, dt))
            s.xn = sb0("xn", [P, NT, D])
            s.scores = sb0("scores", [P, NT, 8])
            s.wt = sb0("expert_weights_of_tokens", [P, 2, NT])
            s.pos = sb0("positions", [P, 2, NT], U32)
            s.slot_e = sb0("slot_expert", [P, SLOTS], I32)
            s.A = sb0("A", [P, DG, NS])
            s.zs = sb0("silu_z", [P, DG, T])
            s.u = sb0("u", [P, DG, T])
            s.delta = sb0("delta", [P, DG, T])
            s.du = sb0("delta_u", [P, DG, T])
            s.bc3 = sb0("bc_parts", [96, T], BF16)
            s.sel = sb0("selectors", [96, 2, NS, P], BF16)
            with ExitStack() as c:
                s.xnT = sb0("xnT", [P, T], c=c)
                s.gate_w = sb0("gate_w", [P, 8], c=c)
                s.taps = sb0("taps", [P, DG, KC], c=c)
                norms_and_projections(nc, s, I)
            with ExitStack() as c:
                s.w1 = sb0("w1", [P, 8, 512], c=c)
                s.w3 = sb0("w3", [P, 8, 512], c=c)
                s.w2 = sb0("w2", [P, 8, 4, P], c=c)
                selective_scan(nc, s, I)
                experts(nc, s, I)
            first_layer_out(nc, s, I)
        with ExitStack() as l1:
            def sb1(name, shape, dt=F32, c=l1):
                return c.enter_context(nc.sbuf_tensor(name, shape, dt))
            s.parts = nc.dram_tensor("operand_parts", (B, 2, DH, 3 * 4, HG, L), BF16, kind="Internal").ap()
            s.xb = sb1("xb", [P, NT, D])
            s.logits = sb1("logits", [P, NT, 8])
            s.vals = sb1("values", [P, NT, D])
            s.v_next = sb1("next_values", [P, NT, D])
            s.s3 = sb1("next_key_scores", [P, NT, NH])
            s.next_gap = sb1("next_key_gap", [P, NT, NH])
            s.U = sb1("contexts", [P, 2, T])
            attention_operands(nc, s, I)
            attention(nc, s, I)
            second_layer_out(nc, s, I, out)


BIG = -1e30


def constants():
    import numpy as np

    bf = mybir.dt.np(BF16)
    k, m = np.arange(P)[:, None], np.arange(P)[None, :]
    out = {"ident": np.eye(P, dtype=np.float32), "ident_bf": np.eye(P).astype(bf)}
    out["before"] = (k < m).astype(np.float32)
    out["every"] = np.ones((P, P), np.float32)
    sel = np.zeros((96, 2, NS, P), np.float32)
    for part in range(3):
        for which in range(2):
            for n in range(NS):
                sel[32 * part + NS * which + n, which, n, :] = 1.0
    out["selectors"] = sel.astype(bf)
    first = np.where(m > k, BIG, 0.0)
    second = np.where(m < k + 2, BIG, 0.0)
    corner = np.zeros((P, 2))
    corner[P - 1, 0] = BIG
    corner[0, 1] = BIG
    out["masks"] = np.concatenate([first, second, first.T, second.T, corner], 1).astype(bf)
    w = np.exp(np.arange(0, D, 2, dtype=np.float32) * np.float32(-np.log(10000.0) / D)).astype(np.float64)
    w = np.repeat(w, 2)[:, None]
    sign = np.where(np.arange(D) % 2 == 0, -1.0, 1.0)[:, None]
    i = np.arange(L)[None, :]
    turn = [np.cos((L - 1 - i) * w), sign * np.sin((L - 1 - i) * w), np.cos((i + 2) * w), -sign * np.sin((i + 2) * w)]
    out["turns"] = np.stack(turn, 1).astype(np.float32)
    table = np.where(sign < 0, np.sin(i * w), np.cos(i * w)).astype(np.float32)
    hi = table.astype(bf)
    mid = (table - hi.astype(np.float32)).astype(bf)
    lo = (table - hi.astype(np.float32) - mid.astype(np.float32)).astype(bf)
    out["sinusoids"] = np.stack([hi, mid, lo], 1)
    out["head_selector"] = (k // 16 == np.arange(D // 16)[None, :]).astype(np.float32)
    out["rows_behind"] = (T + k + P * np.arange(NT)[None, :]).astype(np.float32)
    slot = np.arange(NT * 2 + 8, dtype=np.float32)
    out["slot_numbers"] = np.broadcast_to(slot, (P, slot.size)).copy()
    out["expert_numbers"] = np.broadcast_to(np.arange(8, dtype=np.float32), (P, 8)).copy()
    return out


def layouts(v):
    import numpy as np

    a = {k: np.asarray(x) for k, x in v.items()}
    o = {k: a[k] for k in ("L0_attn_x", "L0_attn_A_log", "L1_attn_Wo", "L1_ffn_wg", "L1_ffn_b")}
    o["L0_attn_conv_w"] = a["L0_attn_conv_w"][:, 0, :]
    o["in_w_t"] = a["L0_attn_in_w"].T
    xw = a["L0_attn_xproj_w"].T
    o["xproj_t"] = xw[:, :R]
    o["xproj_bc_t"] = np.concatenate([xw[:, R:]] * 3, 1)
    o["dt_w_t"] = a["L0_attn_dt_w"].T
    o["out_w_t"] = a["L0_attn_out_w"].T
    o["gate_w_t"] = a["L0_ffn_gate_w"].T
    o["w1_t"] = a["L0_ffn_w1"].transpose(2, 0, 1)
    o["w3_t"] = a["L0_ffn_w3"].transpose(2, 0, 1)
    o["w2_t"] = a["L0_ffn_w2"].reshape(8, D, 4, P).transpose(3, 0, 2, 1)
    heads = D // 16

    def blocks(w):
        z = np.zeros((D, D), w.dtype)
        for h in range(heads):
            z[16 * h:16 * h + 16, 16 * h:16 * h + 16] = w
        return z

    wpt = a["L1_attn_Wp"].T
    swapped = wpt.reshape(16, 8, 2)[:, :, ::-1].reshape(16, 16)
    o["head_w"] = np.stack([blocks(a["L1_attn_Wq"]), blocks(a["L1_attn_Wk"]), blocks(a["L1_attn_Wv"]),
                            blocks(wpt), blocks(swapped)], 1)
    rep = lambda x: np.concatenate([x] * heads)
    two = lambda x: [x[:P], x[P:]]
    cols = [a["L0_attn_norm_g"], a["L0_attn_norm_b"], *two(a["L0_attn_conv_b"]), *two(a["L0_attn_dt_b"]), *two(a["L0_attn_D"]),
            a["L1_attn_ln_gamma"], a["L1_attn_ln_beta"], rep(a["L1_attn_bq"]), rep(a["L1_attn_bk"]),
            a["L1_attn_u_bias"].reshape(D), a["L1_attn_v_bias"].reshape(D)]
    cols += [np.zeros(P, np.float32)] * (24 - len(cols))
    o["vectors"] = np.stack(cols, 1)
    o["rows"] = np.stack([rep(a["L1_attn_bq"]), a["L1_attn_u_bias"].reshape(D), rep(a["L1_attn_bk"]), rep(a["L1_attn_bv"]),
                          a["L1_attn_bo"]], 0)
    o["moe_w"] = a["L1_ffn_W"].transpose(2, 0, 1)
    o.update(constants())
    return {k: np.ascontiguousarray(x) for k, x in o.items()}


def kernel(**inputs):
    import concourse.bacc as bacc
    from concourse.bass_utils import run_bass_kernel_spmd

    nc = bacc.Bacc("TRN2", target_bir_lowering=False, num_devices=1)
    arrays = layouts(inputs)
    aps = {k: nc.dram_tensor("in_" + k, x.shape, mybir.dt.from_np(x.dtype), kind="ExternalInput").ap() for k, x in arrays.items()}
    out = nc.dram_tensor("out", (B, L, D), F32, kind="ExternalOutput").ap()
    build(nc, aps, out)
    r = run_bass_kernel_spmd(nc, [{"in_" + k: x for k, x in arrays.items()}], core_ids=[0])
    return r.results[0]["out"]
```

```python
from contextlib import ExitStack

import concourse.bass as bass
from concourse import mybir

F32 = mybir.dt.float32
BF16 = mybir.dt.bfloat16
I32 = mybir.dt.int32
U32 = mybir.dt.uint32
ALU = mybir.AluOpType
ACT = mybir.ActivationFunctionType
AX = mybir.AxisListType

P = 128
B, L, D = 2, 1024, 128
T = B * L
NT = T // P
DG = 2
NS = 16
R = 64
KC = 4
CH = 512
NCH = T // CH
TPS = L // P
EPS = 1e-5


class Tally:

    def __init__(self, sem):
        self.sem, self.n = sem, 0

    def by(self, ins):
        ins.then_inc(self.sem, 1)
        self.n += 1
        return self.n


def bc(ap, shape):
    return ap.to_broadcast(shape)


class Shared:
    pass


NQ = 4
SLOTS = 2 * T // P + 8


def two_norms(nc, dve, t, src, mid, dst, tmp, have, var_ready, rstd_ready, mid_ready, dst_ready):
    stats, mv, ve, rstd = tmp

    def link(ins):
        dve.wait_ge(dve_done, t.by(ins))

    dve_done = t.sem

    def statistics(x, k, q):
        for i in range(NQ * q, NQ * (q + 1)):
            last = t.by(nc.vector.bn_stats(stats[:, k, i, :], x[:, i, :]))
        dve.wait_ge(dve_done, last)
        for i in range(NQ * q, NQ * (q + 1)):
            last = t.by(nc.vector.bn_aggr(mv[:, k, i, :], stats[:, k, i, :]))
        dve.wait_ge(dve_done, last)
        nc.vector.tensor_scalar(ve[:, k, NQ * q:NQ * (q + 1)], mv[:, k, NQ * q:NQ * (q + 1), 1], EPS, None, ALU.add).then_inc(var_ready, 1)

    def scale(x, y, k, q, ready):
        dve.wait_ge(rstd_ready, k * NT // NQ + q + 1)
        for i in range(NQ * q, NQ * (q + 1)):
            last = t.by(nc.vector.tensor_scalar(y[:, i, :], x[:, i, :], mv[:, k, i, 0:1], rstd[:, k, i:i + 1], ALU.subtract, ALU.mult))
        dve.wait_ge(dve_done, last)
        dve.sem_inc(ready, 1)

    for q in range(NT // NQ):
        if have:
            dve.wait_ge(have[q], 16)
        statistics(src, 0, q)
    for q in range(NT // NQ):
        scale(src, mid, 0, q, mid_ready)
        statistics(mid, 1, q)
    for q in range(NT // NQ):
        scale(mid, dst, 1, q, dst_ready)


def reciprocal_roots(nc, pool, tmp, half, var_ready, rstd_ready):
    ve, rstd = tmp[2:]
    for k in range(2):
        for q in range(NT // NQ):
            pool.wait_ge(var_ready, k * NT // NQ + q + 1)
            cols = slice(NQ * q, NQ * (q + 1))
            nc.gpsimd.tensor_tensor(rstd[:, k, cols], ve[:, k, cols], half[:, 0:NQ], ALU.pow).then_inc(rstd_ready, 1)


def norm_tensors(sb, name):
    return (sb(name + "_stats", [P, 2, NT, 6]), sb(name + "_mean_var", [P, 2, NT, 2]), sb(name + "_var_eps", [P, 2, NT]),
            sb(name + "_rstd", [P, 2, NT]))


def count_before(nc, s, dve, link, mask, counted, tot, incl, keep, pos, rank_bank, total_bank, E=8):
    dve.wait_ge(counted, 1)
    link(nc.vector.tensor_copy(tot[:], total_bank.rearrange("p (t e) -> p e t", e=E)))
    link(nc.vector.tensor_tensor_scan(incl[:].rearrange("p e t -> p (e t)"), keep[:].rearrange("p e t -> p (e t)"),
                                      tot[:].rearrange("p e t -> p (e t)"), 0.0, ALU.mult, ALU.add))
    link(nc.vector.tensor_tensor(tot[:], incl[:], tot[:], ALU.subtract))
    link(nc.vector.tensor_tensor(pos[:], rank_bank.rearrange("p (t e) -> p t e", e=E), tot[:].rearrange("p e t -> p t e"), ALU.add))


def norms_and_projections(nc, s, I):
    sem = s.sem
    s.quarter_in = [sem(f"quarter_loaded_{q}") for q in range(NT // NQ)]
    x_in, w_in, ident_in, route_in = s.quarter_in, sem("weights_loaded"), sem("identity_loaded"), sem("route_constants")
    dve_done, act_done, pool_done = s.tally.sem, sem("a_act"), sem("a_pool")
    var_ready, rstd_ready = sem("var_ready"), sem("rstd_ready")
    xn_ready, xa_ready = sem("xn_ready"), sem("xa_ready")
    tr_done, tr_copied = sem("transposes_done"), sem("transposes_copied")
    proj_done, proj_copied = sem("in_proj_done"), sem("in_proj_copied")
    conv_done, u_ready = sem("conv_done"), sem("u_ready")
    score_done, scores_copied = sem("scores_done"), sem("scores_copied")
    dbc_done, draw_copied, bc_copied, bc_split = sem("dbc_done"), sem("draw_copied"), sem("bc_copied"), sem("bc_split")
    dt_done, relu_done, abs_done, exp_done, one_done, rest_done, ln_done, given_back, delta_ready = (
        sem("dt_done"), sem("softplus_relu"), sem("softplus_abs"), sem("softplus_exp"), sem("softplus_one"),
        sem("softplus_rest"), sem("softplus_ln"), sem("softplus_given_back"), sem("delta_ready"))
    pads_ready = sem("pads_ready")
    diff_ready, e2_ready, mask_ready, counted, counts_read = (
        sem("gap_ready"), sem("gap_exp"), sem("mask_ready"), sem("counted"), sem("counts_read"))
    rows_placed = sem("rows_and_places_ready")
    zeroed_2 = sem("second_rows_zeroed")
    pos_ready, zero_ready, zeroed, scattered = sem("positions_ready"), sem("zeros_ready"), sem("rows_zeroed"), sem("rows_scattered")
    bank = s.bank
    with ExitStack() as ctx:
        def sb(name, shape, dt=F32):
            return ctx.enter_context(nc.sbuf_tensor(name, shape, dt))

        xa = sb("xa", [P, NT, D])
        norm_tmp = norm_tensors(sb, "norm")
        half = sb("minus_half", [P, NT])
        xaT = sb("xaT", [P, T])
        xp = sb("x_padded", [P, DG, B, L + KC - 1])
        draw = sb("delta_low_rank", [R, T])
        in_w = sb("in_w_t", [P, 4 * P])
        xw = sb("xproj_w_t", [P, DG, R])
        xbc = sb("xproj_bc_t", [P, DG, 96])
        dtw = sb("dt_w_t", [R, DG * P])
        bcr = sb("bc_rest", [96, T])
        bcm = sb("bc_middle", [96, T], BF16)
        bcl = sb("bc_low", [96, T], BF16)
        before = sb("before", [P, P])
        every = sb("every", [P, P])
        slot_no = sb("slot_no", [P, SLOTS])
        exp_no = sb("expert_no", [P, 8])
        top = sb("top", [P, NT, 8])
        idx = sb("top_index", [P, NT, 8], U32)
        idf = sb("top_index_f", [P, NT, 2])
        gap = sb("gap", [P, NT])
        one = sb("one_hot", [P, 2, NT, 8])
        mask = sb("mask", [P, NT, 8])
        tot = sb("totals", [P, 8, NT])
        incl = sb("inclusive", [P, 8, NT])
        keep = sb("keep", [P, 8, NT])
        pos = sb("pos", [P, NT, 8])
        picked = sb("picked", [P, NT, 8])
        posf = sb("pos_f", [P, 2, NT])
        tiles = sb("expert_tiles", [P, 8])
        tiles_i = sb("expert_tiles_i", [P, 8], I32)
        ends = sb("expert_ends", [P, 8])
        ones8 = sb("ones8", [P, 8])
        past = sb("slots_past", [P, SLOTS, 8])
        slot_f = sb("slot_expert_f", [P, SLOTS])
        zeros = sb("zeros", [P, 5 * (D + 1)])
        xe = sb("rows_and_places", [P, 2, NT, D + 1])
        back = sb("result_places", [P, 2, NT])
        spe = xp[:].rearrange("p g b l -> p (g b l)")[:, 0:DG * T].rearrange("p (g t) -> p g t", g=DG)
        spw = s.du
        block = ctx.enter_context(nc.Block())

        NW = 8
        COUNT_BANK = 7

        @block.sync
        def _(sp):
            for q in range(NT // NQ):
                b, t0 = q // (TPS // NQ), q % (TPS // NQ) * NQ
                sp.dma_start(s.x[:, NQ * q:NQ * (q + 1)],
                             I["L0_attn_x"][b, t0 * P:(t0 + NQ) * P].rearrange("(t p) d -> p t d", p=P)).then_inc(x_in[q], 16)
            sp.dma_start(s.ident[:], I["ident"]).then_inc(ident_in, 16)
            for dst, src in ((s.gate_w[:], I["gate_w_t"]), (in_w[:], I["in_w_t"]), (s.vec[:], I["vectors"]),
                             (s.A[:], I["L0_attn_A_log"].rearrange("(g p) n -> p g n", p=P)),
                             (s.taps[:], I["L0_attn_conv_w"].rearrange("(g p) k -> p g k", p=P)),
                             (xw[:], I["xproj_t"].rearrange("(g p) r -> p g r", p=P)),
                             (xbc[:], I["xproj_bc_t"].rearrange("(g p) r -> p g r", p=P)),
                             (dtw[:], I["dt_w_t"])):
                sp.dma_start(dst, src).then_inc(w_in, 16)
            for dst, src in ((before[:], I["before"]), (every[:], I["every"]), (slot_no[:], I["slot_numbers"]), (exp_no[:], I["expert_numbers"]),
                             (back[:], I["result_places"])):
                sp.dma_start(dst, src).then_inc(route_in, 16)
            sp.wait_ge(zero_ready, 1)
            flat = s.rows_in.rearrange("(c p q) d -> c p (q d)", p=P, q=5)
            for c in range(SLOTS // 5):
                sp.dma_start(flat[c], zeros[:]).then_inc(zeroed, 16)
            sp.dma_start(s.sel[:], I["selectors"]).then_inc(s.sel_in, 16)
            flat = s.rows2_in[0:T].rearrange("(c p q) d -> c p (q d)", p=P, q=4)
            for c in range(NT // 4):
                sp.dma_start(flat[c], zeros[:, 0:4 * D]).then_inc(zeroed_2, 16)
            sp.wait_ge(zeroed_2, 16 * (NT // 4))

        def delta_u(pool, i):
            g, cols = i // NCH, slice(i % NCH * CH, (i % NCH + 1) * CH)
            pool.wait_ge(delta_ready, i + 1)
            nc.gpsimd.tensor_tensor(s.du[:, g, cols], s.delta[:, g, cols], s.u[:, g, cols], ALU.mult)

        @block.gpsimd
        def _(pool):
            t = Tally(pool_done)

            def link(ins):
                pool.wait_ge(pool_done, t.by(ins))

            link(nc.gpsimd.memset(half[:], -0.5))
            link(nc.gpsimd.memset(zeros[:], 0.0))
            pool.sem_inc(zero_ready, 1)
            link(nc.gpsimd.memset(xp[:, :, :, 0:KC - 1], 0.0))
            pool.sem_inc(pads_ready, 1)
            reciprocal_roots(nc, pool, norm_tmp, half, var_ready, rstd_ready)
            pool.wait_ge(pos_ready, 1)
            pool.wait_ge(zeroed, 16 * (SLOTS // 5))
            pool.wait_ge(rows_placed, 3)
            for i in range(NT):
                for k in range(2):
                    nc.gpsimd.indirect_dma_start(out=s.rows_in, out_offset=bass.IndirectOffsetOnAxis(ap=s.pos[:, k, i:i + 1], axis=0),
                                                 in_=xe[:, k, i, :], in_offset=None,
                                                 bounds_check=SLOTS * P - 1).then_inc(scattered, 16)
            for i in range(DG * NCH):
                delta_u(pool, i)
            pool.wait_ge(scattered, 32 * NT)

        @block.vector
        def _(dve):
            t = s.tally

            def link(ins):
                dve.wait_ge(dve_done, t.by(ins))

            two_norms(nc, dve, t, s.x, s.xn, xa, norm_tmp, x_in, var_ready, rstd_ready, xn_ready, xa_ready)

            full = [P, NT, 8]
            t.by(nc.vector.memset(ones8[:], 1.0))
            link(nc.vector.memset(keep[:], 1.0))
            t.by(nc.vector.memset(keep[:, :, 0:1], 0.0))
            dve.wait_ge(scores_copied, 1)
            for i in range(NT):
                last = t.by(nc.vector.max(top[:, i, :], s.scores[:, i, :]))
            dve.wait_ge(dve_done, last)
            for i in range(NT):
                last = t.by(nc.vector.max_index(idx[:, i, :], top[:, i, :], s.scores[:, i, :]))
            nc.vector.tensor_tensor(gap[:], top[:, :, 1], top[:, :, 0], ALU.subtract).then_inc(diff_ready, 1)
            dve.wait_ge(dve_done, last)
            dve.wait_ge(route_in, 80)
            link(nc.vector.tensor_copy(xe[:, :, :, D], back[:]))
            dve.sem_inc(rows_placed, 1)
            link(nc.vector.tensor_copy(idf[:], idx[:, :, 0:2]))
            for k in range(2):
                last = t.by(nc.vector.tensor_tensor(one[:, k], bc(idf[:, :, k:k + 1], full), bc(exp_no[:, None, :], full), ALU.is_equal))
            dve.wait_ge(dve_done, last)
            nc.vector.tensor_tensor(mask[:], one[:, 0], one[:, 1], ALU.add).then_inc(mask_ready, 1)

            def convolve(g):
                dve.wait_ge(proj_copied, 4 * (g + 1))
                dve.wait_ge(pads_ready, 1)
                out = s.u[:, g].rearrange("p (b l) -> p b l", b=B)
                link(nc.vector.tensor_scalar(out, xp[:, g, :, 0:L], s.taps[:, g, 0:1], None, ALU.mult))
                for k in range(1, KC):
                    link(nc.vector.scalar_tensor_tensor(out=out, in0=xp[:, g, :, k:k + L], scalar=s.taps[:, g, k:k + 1],
                                                        in1=out, op0=ALU.mult, op1=ALU.add))
                dve.sem_inc(conv_done, 1)

            convolve(0)
            y = bank(COUNT_BANK)
            count_before(nc, s, dve, link, mask, counted, tot, incl, keep, pos, y[:, 0:P], y[:, P:2 * P])
            dve.sem_inc(counts_read, 1)
            link(nc.vector.tensor_scalar(tiles_i[:], incl[:, :, NT - 1], float(P - 1), None, ALU.add))
            link(nc.vector.tensor_single_scalar(tiles_i[:], tiles_i[:], 7, ALU.arith_shift_right))
            link(nc.vector.tensor_copy(tiles[:], tiles_i[:]))
            link(nc.vector.tensor_tensor_scan(ends[:], ones8[:], tiles[:], 0.0, ALU.mult, ALU.add))
            link(nc.vector.tensor_tensor(tiles[:], ends[:], tiles[:], ALU.subtract))
            link(nc.vector.tensor_scalar(tiles[:], tiles[:], float(P), None, ALU.mult))
            link(nc.vector.tensor_tensor(pos[:], pos[:], bc(tiles[:, None, :], full), ALU.add))
            for k in range(2):
                link(nc.vector.tensor_tensor(picked[:], pos[:], one[:, k], ALU.mult))
                link(nc.vector.reduce_sum(posf[:, k], picked[:], AX.X))
            link(nc.vector.tensor_copy(s.pos[:], posf[:]))
            dve.sem_inc(pos_ready, 1)
            convolve(1)
            wide = [P, SLOTS, 8]
            link(nc.vector.tensor_tensor(past[:], bc(slot_no[:, :, None], wide), bc(ends[:, None, :], wide), ALU.is_ge))
            link(nc.vector.reduce_sum(slot_f[:], past[:], AX.X))
            link(nc.vector.tensor_scalar(s.slot_e[:], slot_f[:], 7.0, None, ALU.min))
            for c in range(NCH):
                cols = slice(c * CH, (c + 1) * CH)
                dve.wait_ge(bc_copied, c + 1)
                link(nc.vector.tensor_tensor(bcr[:, cols], bank(4 + c % 2)[0:96, :], s.bc3[:, cols], ALU.subtract))
                dve.sem_inc(bc_split, 1)
                link(nc.vector.tensor_copy(bcm[:, cols], bcr[:, cols]))
                link(nc.vector.tensor_tensor(bcl[64:96, cols], bcr[64:96, cols], bcm[64:96, cols], ALU.subtract))
                nc.vector.tensor_copy(s.bc3[32:64, cols], bcm[32:64, cols])
                link(nc.vector.tensor_copy(s.bc3[64:96, cols], bcl[64:96, cols]))
            dve.wait_ge(e2_ready, 1)
            link(nc.vector.tensor_scalar(gap[:], s.wt[:, 1], 1.0, None, ALU.add))
            link(nc.vector.reciprocal(s.wt[:, 0], gap[:]))
            link(nc.vector.tensor_tensor(s.wt[:, 1], s.wt[:, 1], s.wt[:, 0], ALU.mult))
            n = DG * NCH

            def place(i):
                return i // NCH, slice(i % NCH * CH, (i % NCH + 1) * CH)

            for i in range(n):
                g, cols = place(i)
                dve.wait_ge(dt_done, i + 1)
                nc.vector.tensor_scalar(s.delta[:, g, cols], bank(i % 4), s.vec[:, 4 + g:5 + g], 0.0, ALU.add, ALU.max).then_inc(relu_done, 1)

            def give_back(i):
                g, cols = place(i)
                dve.wait_ge(rest_done, i + 1)
                dve.wait_ge(relu_done, i + 1)
                nc.vector.tensor_tensor(s.delta[:, g, cols], s.delta[:, g, cols], spe[:, g, cols], ALU.subtract).then_inc(given_back, 1)

            for i in range(n):
                g, cols = place(i)
                dve.wait_ge(exp_done, i + 1)
                nc.vector.tensor_scalar(spw[:, g, cols], spe[:, g, cols], 1.0, None, ALU.add).then_inc(one_done, 1)
                dve.wait_ge(one_done, i + 1)
                nc.vector.scalar_tensor_tensor(out=spe[:, g, cols], in0=spw[:, g, cols], scalar=-1.0, in1=spe[:, g, cols],
                                               op0=ALU.add, op1=ALU.subtract).then_inc(rest_done, 1)
                if i:
                    give_back(i - 1)
            give_back(n - 1)
            for i in range(n):
                g, cols = place(i)
                dve.wait_ge(ln_done, i + 1)
                dve.wait_ge(given_back, i + 1)
                nc.vector.tensor_tensor(s.delta[:, g, cols], s.delta[:, g, cols], spw[:, g, cols], ALU.add).then_inc(delta_ready, 1)

        @block.scalar
        def _(act):
            a = Tally(act_done)
            for c in range(NCH):
                act.wait_ge(tr_done, c + 1)
                nc.scalar.activation(s.xnT[:, c * CH:(c + 1) * CH], bank(c), ACT.Copy).then_inc(tr_copied, 1)
            for k in range(2):
                act.wait_ge(xn_ready, NCH)
                nc.scalar.activation(xe[:, k, :, 0:D], s.xn[:], ACT.Copy).then_inc(rows_placed, 1)
            act.wait_ge(score_done, 1)
            nc.scalar.activation(s.scores[:].rearrange("p t e -> p (t e)"), bank(0)[:, 0:8 * NT], ACT.Copy).then_inc(scores_copied, 1)
            act.wait_ge(w_in, 16 * NW)
            for c in range(NCH):
                act.wait_ge(tr_done, NCH + c + 1)
                nc.scalar.activation(xaT[:, c * CH:(c + 1) * CH], bank(4 + c), ACT.Identity,
                                     scale=s.vec[:, 0:1], bias=s.vec[:, 1:2]).then_inc(tr_copied, 1)
            for i in range(2 * DG * NCH):
                q, c = i // NCH, i % NCH
                act.wait_ge(proj_done, i + 1)
                if q < DG:
                    b, l0 = c // (NCH // B), c % (NCH // B) * CH
                    nc.scalar.activation(xp[:, q, b, KC - 1 + l0:KC - 1 + l0 + CH], bank(i % 4), ACT.Copy).then_inc(proj_copied, 1)
                else:
                    nc.scalar.activation(s.zs[:, q - DG, c * CH:(c + 1) * CH], bank(i % 4), ACT.Silu).then_inc(proj_copied, 1)
            for g in range(DG):
                act.wait_ge(conv_done, g + 1)
                nc.scalar.activation(s.u[:, g], s.u[:, g], ACT.Silu, bias=s.vec[:, 2 + g:3 + g]).then_inc(u_ready, 1)
            for c in range(NCH):
                cols = slice(c * CH, (c + 1) * CH)
                act.wait_ge(dbc_done, 2 * c + 1)
                nc.scalar.activation(draw[:, cols], bank(6 + c % 2)[0:R, :], ACT.Copy).then_inc(draw_copied, 1)
                act.wait_ge(dbc_done, 2 * c + 2)
                nc.scalar.activation(s.bc3[:, cols], bank(4 + c % 2)[0:96, :], ACT.Copy).then_inc(bc_copied, 1)
            act.wait_ge(diff_ready, 1)
            nc.scalar.activation(s.wt[:, 1], gap[:], ACT.Exp).then_inc(e2_ready, 1)
            a.by(nc.scalar.activation(s.A[:], s.A[:], ACT.Exp))
            act.wait_ge(act_done, a.n)
            nc.scalar.mul(s.A[:], s.A[:], -1.0)
            for i in range(DG * NCH):
                g, cols = i // NCH, slice(i % NCH * CH, (i % NCH + 1) * CH)
                act.wait_ge(dt_done, i + 1)
                act.wait_ge(relu_done, i + 1)
                nc.scalar.activation(spe[:, g, cols], bank(i % 4), ACT.Abs, bias=s.vec[:, 4 + g:5 + g]).then_inc(abs_done, 1)
            for i in range(DG * NCH):
                g, cols = i // NCH, slice(i % NCH * CH, (i % NCH + 1) * CH)
                act.wait_ge(abs_done, i + 1)
                nc.scalar.activation(spe[:, g, cols], spe[:, g, cols], ACT.Exp, scale=-1.0).then_inc(exp_done, 1)
            for i in range(DG * NCH):
                g, cols = i // NCH, slice(i % NCH * CH, (i % NCH + 1) * CH)
                act.wait_ge(rest_done, i + 1)
                nc.scalar.activation(spw[:, g, cols], spw[:, g, cols], ACT.Ln).then_inc(ln_done, 1)

        @block.tensor
        def _(pe):
            pe.wait_ge(ident_in, 16)

            def turn(src, k, ready):
                for c in range(NCH):
                    pe.wait_ge(ready, c + 1)
                    for q in range(4):
                        last = nc.tensor.transpose(bank(4 * k + c)[:, q * P:(q + 1) * P], src[:, 4 * c + q, :], s.ident[:])
                    last.then_inc(tr_done, 1)

            turn(s.xn, 0, xn_ready)
            pe.wait_ge(w_in, 16 * NW)
            pe.wait_ge(tr_copied, NCH)
            for t in range(NT):
                last = nc.tensor.matmul(bank(0)[:, 8 * t:8 * t + 8], s.xnT[:, t * P:(t + 1) * P], s.gate_w[:], start=True, stop=True)
            last.then_inc(score_done, 1)
            turn(xa, 1, xa_ready)
            pe.wait_ge(scores_copied, 1)
            for i in range(2 * DG * NCH):
                q, c = i // NCH, i % NCH
                pe.wait_ge(tr_copied, NCH + c + 1 if q == 0 else 2 * NCH)
                if i >= 4:
                    pe.wait_ge(proj_copied, i - 3)
                nc.tensor.matmul(bank(i % 4), in_w[:, q * P:(q + 1) * P], xaT[:, c * CH:(c + 1) * CH],
                                 start=True, stop=True).then_inc(proj_done, 1)
                if i == DG * NCH - 1:
                    pe.wait_ge(route_in, 80)
                    pe.wait_ge(mask_ready, 1)
                    pe.wait_ge(tr_copied, 2 * NCH)
                    flat = mask[:].rearrange("p t e -> p (t e)")
                    nc.tensor.matmul(bank(COUNT_BANK)[:, 0:P], before[:], flat, start=True, stop=True)
                    nc.tensor.matmul(bank(COUNT_BANK)[:, P:2 * P], every[:], flat, start=True, stop=True).then_inc(counted, 1)
            pe.wait_ge(counts_read, 1)
            for c in range(NCH):
                cols = slice(c * CH, (c + 1) * CH)
                pe.wait_ge(u_ready, DG)
                if c >= 2:
                    pe.wait_ge(draw_copied, c - 1)
                    pe.wait_ge(bc_split, c - 1)
                for g in range(DG):
                    last = nc.tensor.matmul(bank(6 + c % 2)[0:R, :], xw[:, g, :], s.u[:, g, cols], start=(g == 0), stop=(g == DG - 1))
                last.then_inc(dbc_done, 1)
                for g in range(DG):
                    last = nc.tensor.matmul(bank(4 + c % 2)[0:96, :], xbc[:, g, :], s.u[:, g, cols], start=(g == 0), stop=(g == DG - 1))
                last.then_inc(dbc_done, 1)
            pe.wait_ge(proj_copied, 2 * DG * NCH)
            for i in range(DG * NCH):
                g, c = i // NCH, i % NCH
                if i < NCH:
                    pe.wait_ge(draw_copied, c + 1)
                else:
                    pe.wait_ge(abs_done, i - 3)
                nc.tensor.matmul(bank(i % 4), dtw[:, g * P:(g + 1) * P], draw[:, c * CH:(c + 1) * CH],
                                 start=True, stop=True).then_inc(dt_done, 1)


UN = 2 * NS


def selective_scan(nc, s, I):
    sem = s.sem
    B_ready, C_ready, C_copied = sem("B_spread"), sem("C_spread"), sem("C_copied")
    dA_ready, dbu_done, h_done = sem("dA_ready"), sem("dBu_done"), sem("h_done")
    prod_done, added, y_read, gated = sem("product_done"), sem("product_added"), sem("y_read"), sem("y_gated")
    bank = s.bank
    with ExitStack() as ctx:
        def sb(name, shape, dt=F32):
            return ctx.enter_context(nc.sbuf_tensor(name, shape, dt))

        sel = s.sel
        dA = sb("dA", [P, 2, DG, L])
        h = sb("h", [P, 2, DG, L])
        prod = sb("products", [P, DG, L])
        Cs = sb("C_in_sbuf", [P, 2, L])
        block = ctx.enter_context(nc.Block())
        Bb, Cb, Yb = (0, 1), (2, 3), ((4, 5), (6, 7))

        def half_of(b, half):
            return bass.ts(b * 2 + half, CH)

        @block.sync
        def _(sp):
            for dst, src in ((s.w1[:], I["w1_t"]), (s.w3[:], I["w3_t"]), (s.w2[:], I["w2_t"])):
                sp.dma_start(dst, src).then_inc(s.expert_w_in, 16)

        @block.tensor
        def _(pe):
            pe.sem_inc(added, 2)
            pe.wait_ge(s.sel_in, 16)
            with pe.Fori(0, B) as b:
                def spread(n):
                    for half in range(2):
                        k = b * UN + 2 * n + half
                        pe.wait_ge(dbu_done, k + 1)
                        nc.tensor.matmul(bank(Bb[half]), sel[:, 0, n, :], s.bc3[:, half_of(b, half)], start=True, stop=True).then_inc(B_ready, 1)
                    for half in range(2):
                        k = b * UN + 2 * n + half
                        pe.wait_ge(C_copied, k + 1)
                        nc.tensor.matmul(bank(Cb[half]), sel[:, 1, n, :], s.bc3[:, half_of(b, half)], start=True, stop=True).then_inc(C_ready, 1)

                def add_up(n, g):
                    if n == 0:
                        pe.wait_ge(y_read, b * DG + g + 1)
                    pe.wait_ge(prod_done, b * UN + 2 * n + g + 5)
                    for half in range(2):
                        last = nc.tensor.matmul(bank(Yb[g][half]), s.ident[:], prod[:, g, half * CH:(half + 1) * CH],
                                                start=(n == 0), stop=(n == NS - 1))
                    last.then_inc(added, 1)

                spread(0)
                for n in range(NS):
                    if n:
                        add_up(n - 1, 0)
                    if n + 1 < NS:
                        spread(n + 1)
                    if n:
                        add_up(n - 1, 1)
                for g in range(DG):
                    add_up(NS - 1, g)

        @block.scalar
        def _(act):
            act.sem_inc(C_copied, 2)
            with act.Fori(0, B) as b:
                for n in range(NS):
                    m, k = n % 2, b * UN + 2 * n
                    act.wait_ge(prod_done, k + 2)
                    act.wait_ge(h_done, k + 2)
                    for half in range(2):
                        act.wait_ge(C_ready, k + half + 1)
                        nc.scalar.activation(Cs[:, m, half * CH:(half + 1) * CH], bank(Cb[half]), ACT.Copy).then_inc(C_copied, 1)
                    for g in range(DG):
                        nc.scalar.activation(dA[:, m, g, :], s.delta[:, g, bass.ts(b, L)], ACT.Exp, scale=s.A[:, g, n:n + 1]).then_inc(dA_ready, 1)

        @block.vector
        def _(dve):
            dve.sem_inc(dbu_done, 2)
            dve.sem_inc(h_done, 4)
            dve.sem_inc(y_read, DG)
            with dve.Fori(0, B) as b:
                for n in range(NS):
                    m, k = n % 2, b * UN + 2 * n
                    dve.wait_ge(prod_done, k + 2)
                    for half in range(2):
                        dve.wait_ge(B_ready, k + half + 1)
                        nc.vector.tensor_tensor(h[:, m, :, half * CH:(half + 1) * CH], s.du[:, :, half_of(b, half)],
                                                bc(bank(Bb[half])[:, None, :], [P, DG, CH]), ALU.mult).then_inc(dbu_done, 1)
                    dve.wait_ge(dbu_done, k + 4)
                    for g in range(DG):
                        dve.wait_ge(dA_ready, k + g + 1)
                        nc.vector.tensor_tensor_scan(h[:, m, g, :], dA[:, m, g, :], h[:, m, g, :], 0.0, ALU.mult, ALU.add).then_inc(h_done, 1)
                for g in range(DG):
                    dve.wait_ge(added, b * UN + UN + g + 1)
                    for half in range(2):
                        last = nc.vector.scalar_tensor_tensor(out=h[:, 0, g, half * CH:(half + 1) * CH], in0=s.u[:, g, half_of(b, half)],
                                                              scalar=s.vec[:, 6 + g:7 + g], in1=bank(Yb[g][half]), op0=ALU.mult, op1=ALU.add)
                    last.then_inc(y_read, 1)
                    dve.wait_ge(y_read, b * DG + g + 3)
                    nc.vector.tensor_tensor(s.u[:, g, bass.ts(b, L)], h[:, 0, g], s.zs[:, g, bass.ts(b, L)], ALU.mult).then_inc(gated, 1)
                dve.wait_ge(gated, b * DG + DG)

        @block.gpsimd
        def _(pool):
            pool.sem_inc(prod_done, 4)
            with pool.Fori(0, B) as b:
                for n in range(NS):
                    m = n % 2
                    for g in range(DG):
                        k = b * UN + 2 * n + g
                        pool.wait_ge(h_done, k + 5)
                        if g == 0:
                            pool.wait_ge(C_copied, k + 4)
                        pool.wait_ge(added, k + 1)
                        nc.gpsimd.tensor_tensor(prod[:, g], h[:, m, g], Cs[:, m], ALU.mult).then_inc(prod_done, 1)


def slots(eng, step):
    pairs = SLOTS // 2
    for m in range(2):
        step(0, m)
    with eng.Fori(0, pairs // 2 - 1) as r:
        for j in range(4):
            step(r * 2 + (1 + j // 2), j % 2)
    for q in (pairs - 1, pairs):
        for m in range(2):
            step(q, m)


def neighbour(q, m, by):
    q, m = q + (m + by) // 2, (m + by) % 2
    if isinstance(q, int) and not 0 <= q < SLOTS // 2:
        return None
    return q, m


def experts(nc, s, I):
    sem = s.sem
    rows_in = [sem(f"slot_rows_in_{m}") for m in range(2)]
    place_read, none_done, to_ready, stores_begun = sem("slot_places_read"), sem("slot_unplaced"), sem("slot_result_places_ready"), sem("slot_stores_begun")
    xt_done, xt_copied = sem("slot_xT_done"), sem("slot_xT_copied")
    up_done, silu_done, g_done = sem("slot_up_done"), sem("slot_silu_done"), sem("slot_gated")
    gt_done, gt_copied, y_done, y_copied = sem("slot_gT_done"), sem("slot_gT_copied"), sem("slot_y_done"), sem("slot_y_copied")
    y_out = [sem(f"slot_y_out_{m}") for m in range(2)]
    bank = s.bank
    with ExitStack() as ctx:
        def sb(name, shape, dt=F32):
            return ctx.enter_context(nc.sbuf_tensor(name, shape, dt))

        xs = sb("slot_x", [P, 2, D + 1])
        place = sb("slot_places", [P, SLOTS])
        unused = sb("unused_places", [P, SLOTS])
        none = sb("no_place", [P, 2])
        to = sb("slot_result_places", [P, 2], U32)
        xsT = sb("slot_xT", [P, 2, P])
        sg = sb("slot_silu", [P, 2, 512])
        gg = sb("slot_g", [P, 2, 512])
        gT = sb("slot_gT", [P, 2, 512])
        ys = sb("slot_y", [P, 2, D])
        block = ctx.enter_context(nc.Block())
        G_BANK, Y_BANK = 6, 7

        @block.sync
        def _(sp):
            sp.dma_start(unused[:], I["unused_places"]).then_inc(s.expert_w_in, 16)
            with sp.Fori(0, SLOTS // 2) as q:
                for m in range(2):
                    k = q * 2 + m
                    sp.wait_ge(xt_done, k + 1)
                    sp.wait_ge(place_read, k + 1)
                    sp.dma_start(xs[:, m, :], s.rows_in[bass.ts(k, P), :]).then_inc(rows_in[m], 16)

        @block.gpsimd
        def _(pool):
            nc.gpsimd.tensor_tensor(s.x[:], s.x[:], s.xn[:], ALU.add).then_inc(stores_begun, 1)
            with pool.Fori(0, SLOTS // 2) as q:
                for m in range(2):
                    k = q * 2 + m
                    pool.wait_ge(y_copied, k + 2)
                    pool.wait_ge(to_ready, k + 1)
                    pool.sem_inc(stores_begun, 1)
                    nc.gpsimd.indirect_dma_start(out=s.rows_out, out_offset=bass.IndirectOffsetOnAxis(ap=to[:, m:m + 1], axis=0),
                                                 in_=ys[:, m, :], in_offset=None, bounds_check=2 * T + SLOTS * P).then_inc(y_out[m], 16)
            for m in range(2):
                pool.wait_ge(y_out[m], 16 * (SLOTS // 2))

        @block.tensor
        def _(pe):
            pe.sem_inc(xt_done, 2)
            pe.sem_inc(y_done, 2)
            pe.sem_inc(up_done, 2)
            pe.sem_inc(gt_done, 2)
            pe.wait_ge(s.expert_w_in, 64)

            def expert_of(k):
                return pe.value_load(s.slot_e[0:1, bass.ts(k, 1)], min_val=0, max_val=7)

            def turn_rows(q, m):
                k = q * 2 + m
                pe.wait_ge(rows_in[m], (q + 1) * 16)
                pe.wait_ge(xt_copied, k + 1)
                nc.tensor.transpose(bank(m)[:, 0:P], xs[:, m, 0:D], s.ident[:]).then_inc(xt_done, 1)

            def multiply_up(q, m):
                k = q * 2 + m
                e = expert_of(k)
                pe.wait_ge(xt_copied, k + 3)
                pe.wait_ge(g_done, k + 1)
                nc.tensor.matmul(bank(2 + m), xsT[:, m, :], s.w1[:, e, :], start=True, stop=True)
                nc.tensor.matmul(bank(4 + m), xsT[:, m, :], s.w3[:, e, :], start=True, stop=True).then_inc(up_done, 1)

            def turn_products(q, m):
                k = q * 2 + m
                pe.wait_ge(g_done, k + 3)
                pe.wait_ge(gt_copied, k + 1)
                for c in range(4):
                    last = nc.tensor.transpose(bank(G_BANK)[:, c * P:(c + 1) * P], gg[:, m, c * P:(c + 1) * P], s.ident[:])
                last.then_inc(gt_done, 1)

            def multiply_down(q, m):
                k = q * 2 + m
                e = expert_of(k)
                pe.wait_ge(gt_copied, k + 2)
                pe.wait_ge(y_copied, k + 1)
                for c in range(4):
                    last = nc.tensor.matmul(bank(Y_BANK)[:, 0:D], gT[:, m, c * P:(c + 1) * P], s.w2[:, e, c, :], start=(c == 0), stop=(c == 3))
                last.then_inc(y_done, 1)

            def step(q, m):
                for by, part in ((1, turn_rows), (0, multiply_up), (-1, turn_products), (-2, multiply_down)):
                    at = neighbour(q, m, by)
                    if at:
                        part(*at)

            turn_rows(0, 0)
            slots(pe, step)

        @block.scalar
        def _(act):
            act.sem_inc(xt_copied, 2)

            def copy_rows(q, m):
                k = q * 2 + m
                act.wait_ge(xt_done, k + 3)
                act.wait_ge(up_done, k + 1)
                nc.scalar.activation(xsT[:, m, :], bank(m)[:, 0:P], ACT.Copy).then_inc(xt_copied, 1)

            def silu(q, m):
                k = q * 2 + m
                act.wait_ge(g_done, k + 1)
                act.wait_ge(up_done, k + 3)
                nc.scalar.activation(sg[:, m], bank(2 + m), ACT.Silu).then_inc(silu_done, 1)

            def step(q, m):
                for by, part in ((1, copy_rows), (0, silu)):
                    at = neighbour(q, m, by)
                    if at:
                        part(*at)

            copy_rows(0, 0)
            slots(act, step)

        @block.vector
        def _(dve):
            dve.sem_inc(g_done, 2)
            dve.sem_inc(gt_copied, 1)
            dve.sem_inc(y_copied, 1)
            dve.sem_inc(place_read, 2)

            def gate(q, m):
                k = q * 2 + m
                dve.wait_ge(silu_done, k + 1)
                dve.wait_ge(gt_done, k + 1)
                nc.vector.tensor_tensor(gg[:, m], sg[:, m], bank(4 + m), ALU.mult).then_inc(g_done, 1)

            def copy_products(q, m):
                k = q * 2 + m
                dve.wait_ge(gt_done, k + 3)
                dve.wait_ge(y_done, k + 1)
                nc.vector.tensor_copy(gT[:, m], bank(G_BANK)).then_inc(gt_copied, 1)

            def read_places(q, m):
                k = q * 2 + m
                dve.wait_ge(rows_in[m], (q + 1) * 16)
                nc.vector.tensor_scalar(place[:, bass.ts(k, 1)], xs[:, m, D:D + 1], 0.0, None, ALU.add).then_inc(place_read, 1)

            def copy_out(q, m):
                k = q * 2 + m
                dve.wait_ge(y_done, k + 3)
                if not isinstance(q, int) or q:
                    dve.wait_ge(y_out[m], q * 16)
                nc.vector.tensor_copy(ys[:, m], bank(Y_BANK)[:, 0:D]).then_inc(y_copied, 1)
                dve.wait_ge(place_read, k + 3)
                nc.vector.scalar_tensor_tensor(out=none[:, m:m + 1], in0=place[:, bass.ts(k, 1)], scalar=0.0,
                                               in1=unused[:, bass.ts(k, 1)], op0=ALU.is_equal, op1=ALU.mult).then_inc(none_done, 1)
                dve.wait_ge(none_done, k + 1)
                nc.vector.tensor_tensor(to[:, m:m + 1], none[:, m:m + 1], place[:, bass.ts(k, 1)], ALU.add).then_inc(to_ready, 1)

            def step(q, m):
                for by, part in ((1, read_places), (0, gate), (-1, copy_products), (-2, copy_out)):
                    at = neighbour(q, m, by)
                    if at:
                        part(*at)

            dve.wait_ge(s.expert_w_in, 64)
            read_places(0, 0)
            slots(dve, step)


def first_layer_out(nc, s, I):
    sem = s.sem
    w_in, o_done, dve_done = sem("out_w_loaded"), sem("out_done"), s.tally.sem
    rows_back = s.quarter_in
    bank = s.bank
    with ExitStack() as ctx:
        def sb(name, shape, dt=F32):
            return ctx.enter_context(nc.sbuf_tensor(name, shape, dt))

        ow = sb("out_w_t", [P, DG, D])
        yr = sb("expert_rows", [P, 2, NT, D])
        block = ctx.enter_context(nc.Block())

        @block.sync
        def _(sp):
            sp.dma_start(ow[:], I["out_w_t"].rearrange("(g p) d -> p g d", p=P)).then_inc(w_in, 16)
            for q in range(4):
                for k in range(2):
                    first = 1 + k * T + 4 * q * P
                    sp.dma_start(yr[:, k, 4 * q:4 * q + 4], s.rows_out[first:first + 4 * P].rearrange("(t p) d -> p t d", p=P)).then_inc(rows_back[q], 16)

        @block.tensor
        def _(pe):
            pe.wait_ge(w_in, 16)
            for i in range(NT):
                for g in range(DG):
                    last = nc.tensor.matmul(bank(i // 4)[:, i % 4 * P:(i % 4 + 1) * P], s.u[:, g, i * P:(i + 1) * P], ow[:, g, :],
                                            start=(g == 0), stop=(g == DG - 1))
                if i % 4 == 3:
                    last.then_inc(o_done, 1)

        @block.vector
        def _(dve):
            t = s.tally

            def link(ins):
                dve.wait_ge(dve_done, t.by(ins))

            for i in range(4):
                dve.wait_ge(o_done, i + 1)
                v = s.x[:, 4 * i:4 * i + 4, :]
                t.by(nc.vector.tensor_tensor(v, v, bank(i).rearrange("p (t d) -> p t d", t=4), ALU.add))
            for k in range(8):
                q, k = k // 2, k % 2
                dve.wait_ge(rows_back[q], 16 + 32)
                dve.wait_ge(dve_done, t.n)
                for i in range(4 * q, 4 * q + 4):
                    t.by(nc.vector.scalar_tensor_tensor(out=s.x[:, i, :], in0=yr[:, k, i, :], scalar=s.wt[:, k, i:i + 1],
                                                        in1=s.x[:, i, :], op0=ALU.mult, op1=ALU.add))
            dve.wait_ge(dve_done, t.n)


NH = 8
DH = D // NH
HG = 4
TPB = L // P
Q_PARTS = ((0, 0, 1), (0, 2, 1))
K_PARTS = ((0, 1, 0), (2, 0, 1))
SCALE = float(D) ** -0.5


def attention_operands(nc, s, I):
    sem = s.sem
    consts, dve_done = sem("l1_constants"), s.tally.sem
    var_ready, rstd_ready = sem("l1_var_ready"), sem("l1_rstd_ready")
    xb_ready, xq_ready, half_ready, pad_ready = sem("xb_ready"), sem("xq_ready"), sem("l1_half_ready"), sem("l1_padded")
    tr_done, tr_copied = sem("l1_transposed"), sem("l1_transposes_copied")
    logits_done, logits_copied, bias_ready = sem("logits_done"), sem("logits_copied"), sem("l1_biases")
    q_done, k_done, q_copied, k_copied = sem("q_done"), sem("k_done"), sem("q_copied"), sem("k_copied")
    v_done, v_read, qk_ready, s3_done = sem("v_done"), sem("v_read"), sem("next_key_products"), sem("next_key_scores_done")
    psi_done, turned, his, rest, mids, parts_ready = (
        sem("psi_done"), sem("turned"), sem("high_parts"), sem("rests"), sem("middle_parts"), sem("parts_ready"))
    parts_out = [sem(f"parts_out_{m}") for m in range(2)]
    bank = s.bank
    V_BANK, VNEXT_BANK, S3_BANK = 5, 6, 7
    with ExitStack() as ctx:
        def sb(name, shape, dt=F32):
            return ctx.enter_context(nc.sbuf_tensor(name, shape, dt))

        xq = sb("xq", [P, NT, D])
        norm_tmp = norm_tensors(sb, "l1_norm")
        half = sb("l1_half", [P, NT])
        xbT = sb("xbT", [P, T])
        xqT = sb("xqT", [P, T + 1])
        hw = sb("head_w", [P, 5, D])
        wg = sb("wg", [P, 8])
        hsel = sb("head_selector", [P, NH])
        turns = sb("turns", [P, 4, L])
        bv = sb("bv_row", [P, D])
        full = sb("operands", [P, 4, T + 1])
        vq = sb("q_plus_v", [P, T + 1])
        prod = sb("next_key_product", [P, 2, CH])
        t2 = sb("turn_work", [P, 2, CH])
        rem = sb("remainder", [P, 4, CH])
        part = sb("parts", [P, 2, 3 * 4, CH], BF16)
        bias2 = sb("l1_bias", [P, 2])
        corner = sb("last_token", [P, 2], BF16)
        block = ctx.enter_context(nc.Block())
        NCONST = 6

        @block.sync
        def _(sp):
            for dst, src in ((wg[:], I["L1_ffn_wg"]), (hw[:], I["head_w"]), (bv[:], I["rows"][3:4].squeeze(0).partition_broadcast(P)),
                             (hsel[:], I["head_selector"]), (corner[:], I["masks"][:, 4 * P:4 * P + 2]), (turns[:], I["turns"])):
                sp.dma_start(dst, src).then_inc(consts, 16)
            for c in range(NCH):
                sp.wait_ge(parts_ready, 2 * (c + 1))
                for h in range(NH):
                    sp.dma_start(s.parts[c // 2, h // HG, :, :, h % HG, c % 2 * CH:(c % 2 + 1) * CH],
                                 part[DH * h:DH * (h + 1), c % 2]).then_inc(parts_out[c % 2], 16)
            for m in range(2):
                sp.wait_ge(parts_out[m], NCH // 2 * 16 * NH)

        @block.gpsimd
        def _(pool):
            nc.gpsimd.memset(half[:], -0.5).then_inc(half_ready, 1)
            pool.wait_ge(half_ready, 1)
            reciprocal_roots(nc, pool, norm_tmp, half, var_ready, rstd_ready)
            for c in range(NCH):
                pool.wait_ge(mids, c + 1)
                if c >= 2:
                    pool.wait_ge(parts_out[c % 2], 16 * NH)
                nc.gpsimd.tensor_tensor(part[:, c % 2, 10:12], rem[:, 2:4], part[:, c % 2, 6:8], ALU.subtract).then_inc(parts_ready, 1)

        @block.vector
        def _(dve):
            t = s.tally

            def link(ins):
                dve.wait_ge(dve_done, t.by(ins))

            t.by(nc.vector.memset(vq[:, T:T + 1], 0.0))
            t.by(nc.vector.memset(full[:, 3, T:T + 1], 0.0))
            link(nc.vector.memset(xqT[:, T:T + 1], 0.0))
            dve.sem_inc(pad_ready, 1)
            t.by(nc.vector.tensor_tensor(bias2[:, 0:1], s.vec[:, 10:11], s.vec[:, 12:13], ALU.add))
            link(nc.vector.tensor_tensor(bias2[:, 1:2], s.vec[:, 10:11], s.vec[:, 13:14], ALU.add))
            dve.sem_inc(bias_ready, 1)
            two_norms(nc, dve, t, s.x, s.xb, xq, norm_tmp, None, var_ready, rstd_ready, xb_ready, xq_ready)
            dve.wait_ge(consts, 16 * NCONST)
            for c in range(NCH):
                cols = slice(c * CH, (c + 1) * CH)
                tiles = slice(4 * c, 4 * c + 4)
                dve.wait_ge(v_done, c + 1)
                for dst, y in ((s.vals, V_BANK), (s.v_next, VNEXT_BANK)):
                    last = t.by(nc.vector.tensor_tensor(dst[:, tiles], bank(y).rearrange("p (t d) -> p t d", t=4),
                                                        bc(bv[:, None, :], [P, 4, D]), ALU.add))
                dve.wait_ge(dve_done, last)
                dve.sem_inc(v_read, 1)
                dve.wait_ge(q_copied, 2 * (c + 1))
                dve.wait_ge(k_copied, min(c + 2, NCH))
                if c >= 2:
                    dve.wait_ge(s3_done, c - 1)
                nc.vector.tensor_tensor(prod[:, c % 2], full[:, 0, cols], full[:, 3, c * CH + 1:(c + 1) * CH + 1], ALU.mult).then_inc(qk_ready, 1)

            def turn(c):
                cols, cc = slice(c * CH, (c + 1) * CH), slice(c % 2 * CH, (c % 2 + 1) * CH)
                dve.wait_ge(psi_done, c + 1)
                for k in range(2):
                    y = 4 * (c % 2) + 2 * k
                    t.by(nc.vector.tensor_tensor(full[:, 1 + k, cols], bank(y), turns[:, 2 * k, cc], ALU.mult))
                    last = t.by(nc.vector.tensor_tensor(t2[:, k], bank(y + 1), turns[:, 2 * k + 1, cc], ALU.mult))
                dve.wait_ge(dve_done, last)
                link(nc.vector.tensor_tensor(full[:, 1:3, cols], full[:, 1:3, cols], t2[:], ALU.add))
                dve.sem_inc(turned, 1)

            def rests(c):
                dve.wait_ge(his, c + 1)
                if c:
                    dve.wait_ge(parts_ready, 2 * c)
                link(nc.vector.tensor_tensor(rem[:], full[:, :, c * CH:(c + 1) * CH], part[:, c % 2, 0:4], ALU.subtract))
                dve.sem_inc(rest, 1)

            def low(c):
                dve.wait_ge(mids, c + 1)
                nc.vector.tensor_tensor(part[:, c % 2, 8:10], rem[:, 0:2], part[:, c % 2, 4:6], ALU.subtract).then_inc(parts_ready, 1)

            turn(0)
            dve.wait_ge(s3_done, NCH)
            link(nc.vector.tensor_copy(s.s3[:].rearrange("p t h -> p (t h)"), bank(S3_BANK)[:, 0:NT * NH]))
            dve.sem_inc(v_read, 1)
            for b in range(B):
                i = (b + 1) * TPB - 1
                link(nc.vector.tensor_tensor(s.s3[:, i, :], s.s3[:, i, :], bc(corner[:, 0:1], [P, NH]), ALU.add))
            rests(0)
            for c in range(NCH):
                if c + 1 < NCH:
                    turn(c + 1)
                low(c)
                if c + 1 < NCH:
                    rests(c + 1)

        @block.scalar
        def _(act):
            for c in range(NCH):
                act.wait_ge(tr_done, c + 1)
                nc.scalar.activation(xbT[:, c * CH:(c + 1) * CH], bank(c), ACT.Copy).then_inc(tr_copied, 1)
            for c in range(NCH):
                act.wait_ge(tr_done, NCH + c + 1)
                nc.scalar.activation(xqT[:, c * CH:(c + 1) * CH], bank(4 + c), ACT.Identity,
                                     scale=s.vec[:, 8:9], bias=s.vec[:, 9:10]).then_inc(tr_copied, 1)
            act.wait_ge(bias_ready, 1)
            for c in range(NCH):
                cols = slice(c * CH, (c + 1) * CH)
                act.wait_ge(k_done, c + 1)
                nc.scalar.activation(full[:, 3, cols], bank(3 + c % 2), ACT.Identity, bias=s.vec[:, 11:12]).then_inc(k_copied, 1)
                act.wait_ge(q_done, c + 1)
                nc.scalar.activation(full[:, 0, cols], bank(1 + c % 2), ACT.Identity, bias=bias2[:, 0:1]).then_inc(q_copied, 1)
                nc.scalar.activation(vq[:, cols], bank(1 + c % 2), ACT.Identity, bias=bias2[:, 1:2]).then_inc(q_copied, 1)
            act.wait_ge(logits_done, 1)
            nc.scalar.activation(s.logits[:].rearrange("p t e -> p (t e)"), bank(0)[:, 0:8 * NT], ACT.Copy).then_inc(logits_copied, 1)

            def high(c):
                act.wait_ge(turned, c + 1)
                act.wait_ge(k_copied, NCH)
                act.wait_ge(q_copied, 2 * NCH)
                if c >= 2:
                    act.wait_ge(parts_out[c % 2], 16 * NH)
                nc.scalar.activation(part[:, c % 2, 0:4], full[:, :, c * CH:(c + 1) * CH], ACT.Copy).then_inc(his, 1)

            def middle(c):
                act.wait_ge(rest, c + 1)
                nc.scalar.activation(part[:, c % 2, 4:8], rem[:], ACT.Copy).then_inc(mids, 1)

            high(0)
            for c in range(NCH):
                middle(c)
                if c + 1 < NCH:
                    high(c + 1)

        @block.tensor
        def _(pe):
            for k, (src, ready) in enumerate(((s.xb, xb_ready), (xq, xq_ready))):
                for c in range(NCH):
                    pe.wait_ge(ready, c + 1)
                    for q in range(4):
                        last = nc.tensor.transpose(bank(4 * k + c)[:, q * P:(q + 1) * P], src[:, 4 * c + q, :], s.ident[:])
                    last.then_inc(tr_done, 1)
            pe.wait_ge(consts, 16 * NCONST)
            pe.wait_ge(pad_ready, 1)
            pe.wait_ge(tr_copied, 2 * NCH)
            for c in range(NCH):
                cols = slice(c * CH, (c + 1) * CH)
                if c >= 2:
                    pe.wait_ge(k_copied, c - 1)
                    pe.wait_ge(q_copied, 2 * (c - 1))
                nc.tensor.matmul(bank(3 + c % 2), hw[:, 1], xqT[:, cols], start=True, stop=True).then_inc(k_done, 1)
                nc.tensor.matmul(bank(1 + c % 2), hw[:, 0], xqT[:, cols], start=True, stop=True).then_inc(q_done, 1)
                if c:
                    pe.wait_ge(v_read, c)
                for q in range(4):
                    i = 4 * c + q
                    nc.tensor.matmul(bank(V_BANK)[:, q * P:(q + 1) * P], xqT[:, i * P:(i + 1) * P], hw[:, 2], start=True, stop=True)
                    last = nc.tensor.matmul(bank(VNEXT_BANK)[:, q * P:(q + 1) * P], xqT[:, i * P + 1:(i + 1) * P + 1], hw[:, 2], start=True, stop=True)
                last.then_inc(v_done, 1)
            for t in range(NT):
                last = nc.tensor.matmul(bank(0)[:, 8 * t:8 * t + 8], xbT[:, t * P:(t + 1) * P], wg[:], start=True, stop=True)
            last.then_inc(logits_done, 1)
            for c in range(NCH):
                pe.wait_ge(qk_ready, c + 1)
                for q in range(4):
                    i = 4 * c + q
                    last = nc.tensor.matmul(bank(S3_BANK)[:, NH * i:NH * (i + 1)], prod[:, c % 2, q * P:(q + 1) * P], hsel[:], start=True, stop=True)
                last.then_inc(s3_done, 1)
            pe.wait_ge(logits_copied, 1)
            pe.wait_ge(k_copied, NCH)
            pe.wait_ge(q_copied, 2 * NCH)
            for c in range(NCH):
                cols, nxt = slice(c * CH, (c + 1) * CH), slice(c * CH + 1, (c + 1) * CH + 1)
                if c == 1:
                    pe.wait_ge(v_read, NCH + 1)
                if c >= 2:
                    pe.wait_ge(turned, c - 1)
                for k in range(2):
                    y = 4 * (c % 2) + 2 * k
                    nc.tensor.matmul(bank(y), hw[:, 3], vq[:, (cols, nxt)[k]], start=True, stop=True)
                    last = nc.tensor.matmul(bank(y + 1), hw[:, 4], vq[:, (cols, nxt)[k]], start=True, stop=True)
                last.then_inc(psi_done, 1)


E = 8
CAPACITY = T // E
EPG = E // B
UNITS = 2 * HG + 1
GROUPS = B * NH // HG
LOADS = 16 * 9


def attention(nc, s, I):
    sem = s.sem
    consts, ones_ready, v_copied = sem("attention_constants"), sem("ones_rows_ready"), sem("group_values_ready")
    route_in = sem("l1_route_constants")
    moe_in = [sem(f"moe_tiles_in_{m}") for m in range(2)]
    sin_in = [sem(f"sinusoids_in_{g}") for g in range(2)]
    first_in = [sem(f"stack_first_pass_{g}") for g in range(2)]
    second_in = [sem(f"stack_second_pass_{g}") for g in range(2)]
    max_in = [sem(f"max_rows_in_{g}") for g in range(2)]
    max_done, max_read = sem("max_scores_done"), sem("max_scores_read")
    mx_ready, split = sem("max_ready"), sem("max_split")
    score_done, exp_done, pv_done, pv2_done = sem("score_done"), sem("exp_done"), sem("pv_done"), sem("pv_diagonal_done")
    ctx_done, ctx_read, dve_done = sem("context_done"), sem("context_read"), sem("attention_dve")
    next_ready = sem("next_key_exps_ready")
    gap_ready, exps_ready, mask_ready, counted, counts_read = (
        sem("logit_gap_ready"), sem("logit_exps_ready"), sem("l1_mask_ready"), sem("l1_counted"), sem("l1_counts_read"))
    places_ready, scattered, moe_out, gathered = (
        sem("l1_places_ready"), sem("l1_rows_scattered"), sem("moe_tiles_out"), sem("moe_rows_gathered"))
    moe_turned, moe_xT, moe_done, moe_read, added = (
        sem("moe_rows_turned"), sem("moe_rows_turned_copied"), sem("moe_product_done"), sem("moe_product_read"), sem("moe_added"))
    bank = s.bank
    PV, RING, MAXRING, MOE = (0, 1), (2, 3, 4), (5, 6), 7
    with ExitStack() as ctx:
        def sb(name, shape, dt=F32):
            return ctx.enter_context(nc.sbuf_tensor(name, shape, dt))

        Q = sb("query_stacks", [99, 2, 2, 2, HG, L], BF16)
        K = sb("key_stacks", [99, 2, 2, HG, L], BF16)
        W = sb("exp_scores", [P, 2, HG, CH])
        W2 = sb("exp_diagonal", [P, 2, HG, P])
        V = sb("group_values", [P, TPB, HG, 32])
        xg = sb("moe_rows", [P, 2, TPB, D])
        xgT = sb("moe_rows_turned", [P, P])
        we = sb("moe_w", [P, 2, EPG, D])
        be = sb("moe_b", [1, 2, EPG, D])
        ones = sb("ones_row", [1, P])
        before = sb("l1_before", [P, P])
        every = sb("l1_every", [P, P])
        exp_no = sb("l1_expert_no", [P, E])
        bo = sb("bo_row", [P, D])
        behind = sb("rows_behind", [P, NT])
        lmax = sb("logit_max", [P, NT])
        lg = sb("logit_gap", [P, NT, E])
        ex = sb("logit_exp", [P, NT, E])
        top = sb("l1_top", [P, NT, 8])
        idx = sb("l1_top_index", [P, NT, 8], U32)
        mask = sb("l1_mask", [P, NT, E])
        tot = sb("l1_totals", [P, E, NT])
        incl = sb("l1_inclusive", [P, E, NT])
        keep = sb("l1_keep", [P, E, NT])
        pos = sb("l1_pos", [P, NT, E])
        idf = sb("l1_top_index_f", [P, NT])
        loc = sb("l1_location", [P, NT])
        kept = sb("l1_kept", [P, NT])
        gates = sb("l1_gates", [P, NT])
        place = sb("l1_places", [P, 2, NT], U32)
        masks = sb("diagonal_masks", [P, 4 * P + 2], BF16)
        identb = sb("identity_bf16", [P, P], BF16)
        cm = sb("chunk_maxima", [P, TPB, HG, 3])
        mx = sb("row_maxima", [P, HG, TPB])
        mrest = sb("max_rest", [HG * TPB, P])
        mparts = sb("max_parts", [HG * TPB, 3, P], BF16)
        block = ctx.enter_context(nc.Block())

        def by_group(b, g, each, n):
            return b * (2 * each) + (g * each + n)

        STEP = TPB * UNITS
        assert EPG * CAPACITY == TPB * P
        MAXSTEP = STEP + 1
        FIRST, SECOND, FIRST_T, SECOND_T = (masks[:, q * P:(q + 1) * P] for q in range(4))

        @block.sync
        def _(sp):
            sp.dma_start(masks[:], I["masks"]).then_inc(consts, 16)
            sp.dma_start(identb[:], I["ident_bf"]).then_inc(consts, 16)
            for dst, src in ((before[:], I["before"]), (every[:], I["every"]), (exp_no[:], I["expert_numbers"]), (behind[:], I["rows_behind"]),
                             (bo[:], I["rows"][4:5].squeeze(0).partition_broadcast(P))):
                sp.dma_start(dst, src).then_inc(route_in, 16)
            def load(b, g):
                if not (isinstance(b, int) and b == 0):
                    sp.wait_ge(ctx_done, b * 2 + g)
                parts = s.parts[b if isinstance(b, int) else bass.ts(b, 1), g]
                parts = parts if isinstance(b, int) else parts.squeeze(0)
                for ps, done in enumerate((first_in[g], second_in[g])):
                    for slot in range(3):
                        pq, pk, row = 4 * Q_PARTS[ps][slot], 4 * K_PARTS[ps][slot], 32 * slot
                        for dst, src in ((Q[row:row + DH, g, ps].rearrange("d f h c -> d f (h c)"),
                                          bc(parts[:, pq:pq + 1].rearrange("d f h c -> d f (h c)"), [DH, 2, HG * L])),
                                         (Q[row + DH:row + 2 * DH, g, ps], parts[:, pq + 1:pq + 3]),
                                         (K[row:row + DH, g, ps], parts[:, pk + 3])):
                            sp.dma_start(dst, src).then_inc(done, 16)

            def max_rows(b, g):
                sp.wait_ge(split, b * 2 + g + 2)
                for form in range(2):
                    for part in range(3):
                        sp.dma_start(Q[96 + part:97 + part, g, 0, form].rearrange("r h (t c) -> r (h t) c", t=TPB),
                                     mparts[:, part]).then_inc(max_in[g], 16)

            load(0, 0)
            load(0, 1)
            max_rows(0, 0)
            with sp.Fori(0, B - 1) as b:
                max_rows(b, 1)
                load(b + 1, 0)
                max_rows(b + 1, 0)
                load(b + 1, 1)
            max_rows(B - 1, 1)

        @block.gpsimd
        def _(pool):
            for g in range(2):
                for ps in range(2):
                    for slot in range(3):
                        pool.dma_start(K[32 * slot + DH:32 * slot + 2 * DH, g, ps],
                                       I["sinusoids"][64 * g:64 * g + 64, K_PARTS[ps][slot], :].rearrange("(h m) c -> m h c", h=HG)).then_inc(sin_in[min(g + ps, 1)], 16)
            nc.gpsimd.memset(K[96:99, :, 0], 1.0).then_inc(ones_ready, 1)
            nc.gpsimd.memset(ones[:], 1.0).then_inc(ones_ready, 1)
            pool.wait_ge(ones_ready, 2)
            nc.gpsimd.memset(V[:], 0.0).then_inc(ones_ready, 1)
            pool.wait_ge(ones_ready, 3)
            nc.gpsimd.memset(V[:, :, :, DH:DH + 1], 1.0).then_inc(v_copied, 1)

            def copy_values(b, g):
                pool.wait_ge(ctx_done, b * 2 + g + 1)
                pool.wait_ge(v_copied, b * 2 + g + 1)
                nc.gpsimd.tensor_copy(V[:, :, :, 0:DH], s.vals[:, bass.ts(b, TPB), 64 * g:64 * (g + 1)].rearrange("p t (h d) -> p t h d", h=HG)
                                      ).then_inc(v_copied, 1)

            def moe_load(b, m):
                pool.dma_start(xg[:, m], s.rows2_in[bass.ts(b, L)].rearrange("(t p) d -> p t d", p=P)).then_inc(moe_in[m], 16)
                pool.dma_start(we[:, m], I["moe_w"][:, bass.ts(b, EPG)]).then_inc(moe_in[m], 16)
                pool.dma_start(be[:, m], I["L1_ffn_b"][None, bass.ts(b, EPG)]).then_inc(moe_in[m], 16)

            def moe_store(b, m):
                pool.wait_ge(moe_read, b * TPB + TPB + 1)
                pool.dma_start(s.rows2_out[bass.ts(b, L)].rearrange("(t p) d -> p t d", p=P), xg[:, m]).then_inc(moe_out, 16)

            copy_values(0, 0)
            pool.wait_ge(places_ready, 1)
            for i in range(NT):
                nc.gpsimd.indirect_dma_start(out=s.rows2_in, out_offset=bass.IndirectOffsetOnAxis(ap=place[:, 0, i:i + 1], axis=0),
                                             in_=s.xb[:, i, :], in_offset=None, bounds_check=2 * T - 1).then_inc(scattered, 16)
            pool.wait_ge(scattered, 16 * NT)
            moe_load(B - 1, 1)
            with pool.Fori(0, B - 1) as b:
                moe_load(b, 0)
                copy_values(b, 1)
                moe_store(b, 0)
                copy_values(b + 1, 0)
                pool.wait_ge(moe_out, b * 16 + 16)
            moe_store(B - 1, 1)
            copy_values(B - 1, 1)
            pool.wait_ge(moe_out, 16 * B)
            for i in range(NT):
                nc.gpsimd.indirect_dma_start(out=s.xb[:, i, :], out_offset=None, in_=s.rows2_out,
                                             in_offset=bass.IndirectOffsetOnAxis(ap=place[:, 1, i:i + 1], axis=0),
                                             bounds_check=T - 1).then_inc(gathered, 16)
            pool.wait_ge(gathered, 16 * NT)
            nc.gpsimd.tensor_tensor(s.xb[:], s.xb[:], bc(gates[:, :, None], [P, NT, D]), ALU.mult).then_inc(added, 1)
            pool.wait_ge(added, 1)
            nc.gpsimd.tensor_tensor(s.x[:], s.x[:], s.xb[:], ALU.add).then_inc(added, 1)
            pool.wait_ge(added, 2)
            pool.wait_ge(route_in, 80)
            nc.gpsimd.tensor_tensor(s.x[:], s.x[:], bc(bo[:, None, :], [P, NT, D]), ALU.add)
            pool.wait_ge(next_ready, 1)
            nxt = s.v_next[:].rearrange("p t (h d) -> p (t h) d", h=NH)
            nc.gpsimd.tensor_tensor(nxt, nxt, bc(s.next_gap[:].rearrange("p t h -> p (t h)")[:, :, None], [P, NT * NH, DH]), ALU.mult)

        @block.tensor
        def _(pe):
            pe.sem_inc(ctx_done, 1)
            pe.sem_inc(moe_done, 1)
            pe.sem_inc(pv_done, 2)
            pe.sem_inc(pv2_done, 2)
            pe.wait_ge(consts, 32)
            pe.wait_ge(sin_in[0], 48)

            def max_unit(b, g, it, u):
                y = bank(MAXRING[(g * MAXSTEP + it * UNITS + u) % 2])
                pe.wait_ge(max_read, by_group(b, g, MAXSTEP, it * UNITS + u + 1))
                a, z = it * P, (it + 1) * P

                def product(h, form, lo, hi, at, start, stop):
                    return nc.tensor.matmul(y[:, lo - at:hi - at], Q[0:96, g, 0, form, h, a:z], K[0:96, g, 0, h, lo:hi], start=start, stop=stop)

                if u == 0:
                    for h in range(HG):
                        nc.tensor.matmul(y[:, h * P:(h + 1) * P], identb[:], SECOND, start=True, stop=False)
                        last = product(h, 1, a, z, a - h * P, False, True)
                    last.then_inc(max_done, 1)
                    return
                h, c = (u - 1) % HG, (u - 1) // HG
                lo, hi = c * CH, (c + 1) * CH
                if lo <= a < hi:
                    nc.tensor.matmul(y[:, a - lo:z - lo], identb[:], FIRST, start=True, stop=False)
                    last = product(h, 0, a, z, lo, False, True)
                if lo < min(a, hi):
                    last = product(h, 0, lo, min(a, hi), lo, True, True)
                if max(z, lo) < hi:
                    last = product(h, 1, max(z, lo), hi, lo, True, lo > z)
                    if lo <= z:
                        last = nc.tensor.matmul(y[:, z - lo:z - lo + 1], identb[:], masks[:, 4 * P:4 * P + 1], start=False, stop=True)
                last.then_inc(max_done, 1)

            def max_turned(b, g):
                pe.wait_ge(mx_ready, by_group(b, g, 1, 2))
                nc.tensor.transpose(bank(MAXRING[(g * MAXSTEP + STEP) % 2])[0:HG * TPB, 0:P], mx[:].rearrange("p h t -> p (h t)"), s.ident[:]).then_inc(max_done, 1)

            def score_unit(b, g, jt, u):
                y = bank(RING[u % 3])
                pe.wait_ge(exp_done, by_group(b, g, STEP, jt * UNITS + u + 1))
                a, z = jt * P, (jt + 1) * P

                def product(h, form, lo, hi, at, start, stop):
                    to = y[:, lo - at:hi - at]
                    nc.tensor.matmul(to, K[0:99, g, 0, h, a:z], Q[0:99, g, 0, form, h, lo:hi], start=start, stop=False)
                    return nc.tensor.matmul(to, K[0:96, g, 1, h, a:z], Q[0:96, g, 1, form, h, lo:hi], start=False, stop=stop)

                if u == 0:
                    for h in range(HG):
                        nc.tensor.matmul(y[:, h * P:(h + 1) * P], identb[:], SECOND_T, start=True, stop=False)
                        last = product(h, 1, a, z, a - h * P, False, True)
                    last.then_inc(score_done, 1)
                    return
                h, c = (u - 1) % HG, (u - 1) // HG
                lo, hi = c * CH, (c + 1) * CH
                if lo <= a < hi:
                    nc.tensor.matmul(y[:, a - lo:z - lo], identb[:], FIRST_T, start=True, stop=False)
                    last = product(h, 0, a, z, lo, False, True)
                if max(z, lo) < hi:
                    last = product(h, 0, max(z, lo), hi, lo, True, True)
                if lo < min(a, hi):
                    last = product(h, 1, lo, min(a, hi), lo, True, a > hi)
                    if a <= hi:
                        last = nc.tensor.matmul(y[:, a - 1 - lo:a - lo], identb[:], masks[:, 4 * P + 1:4 * P + 2], start=False, stop=True)
                last.then_inc(score_done, 1)

            def values(b, g, jt, c):
                pe.wait_ge(exp_done, by_group(b, g, STEP, jt * UNITS + 1 + HG * (c + 1) + 3))
                for h in range(HG):
                    last = nc.tensor.matmul(bank(PV[c])[32 * h:32 * h + 32, :], V[:, jt, h, :], W[:, c, h, :],
                                            start=(jt == 0), stop=(jt == TPB - 1))
                last.then_inc(pv_done, 1)

            def diagonal_values(g, jt):
                y, at = bank(PV[jt // 4]), jt % 4 * P
                for h in range(HG):
                    last = nc.tensor.matmul(y[32 * h:32 * h + 32, at:at + P], V[:, jt, h, :], W2[:, jt % 2, h, :], start=False, stop=False)
                last.then_inc(pv2_done, 1)

            def moe_turn(b, m, jt):
                if jt == 0:
                    pe.wait_ge(counts_read, 1)
                    pe.wait_ge(moe_in[m], 48 if m else b * 48 + 48)
                pe.wait_ge(moe_read, b * TPB + (jt + 1))
                nc.tensor.transpose(bank(MOE)[:, 0:P], xg[:, m, jt, :], s.ident[:]).then_inc(moe_turned, 1)

            def moe_multiply(b, m, jt):
                e = jt * P // CAPACITY
                pe.wait_ge(moe_xT, b * TPB + (jt + 1))
                nc.tensor.matmul(bank(MOE)[:, P:2 * P], xgT[:], we[:, m, e, :], start=True, stop=False)
                nc.tensor.matmul(bank(MOE)[:, P:2 * P], ones[:], be[:, m, e, :], start=False, stop=True).then_inc(moe_done, 1)

            def scores_and_values(b, g, nb, ng, between, moe):
                for jt in range(TPB):
                    more = between[jt]
                    if jt == 1 and ng is not None:
                        pe.wait_ge(first_in[ng], LOADS * (nb + 1))
                    for u in range(UNITS):
                        score_unit(b, g, jt, u)
                        if moe and u == 1:
                            moe_turn(b, moe - 1, jt)
                        if moe and u == UNITS - 2:
                            moe_multiply(b, moe - 1, jt)
                        for it, v in more[u * len(more) // UNITS:(u + 1) * len(more) // UNITS]:
                            max_unit(nb, ng, it, v)
                        if u == HG and jt:
                            values(b, g, jt - 1, 1)
                        if u == HG and not jt:
                            pe.wait_ge(ctx_read, by_group(b, g, 2, 2))
                            pe.wait_ge(v_copied, by_group(b, g, 1, 2))
                        if u == 2 and jt == TPB - 1 and ng is not None:
                            max_turned(nb, ng)
                    values(b, g, jt, 0)
                    diagonal_values(g, jt)
                values(b, g, TPB - 1, 1)
                pe.wait_ge(pv_done, by_group(b, g, 2 * TPB, 2 * TPB + 2))
                pe.wait_ge(pv2_done, by_group(b, g, TPB, TPB + 2))
                pe.sem_inc(ctx_done, 1)

            def maxima_alone(b, g):
                pe.wait_ge(first_in[g], LOADS * (b + 1))
                for it in range(TPB):
                    for u in range(UNITS):
                        max_unit(b, g, it, u)
                max_turned(b, g)

            def group(b, g, nb, ng, moe):
                pe.wait_ge(second_in[g], LOADS * (b + 1))
                pe.wait_ge(max_in[g], 96 * (b + 1))
                if nb is None:
                    scores_and_values(b, g, None, None, [[]] * TPB, moe)
                    return
                steps = [[], [0], [1, 2], [3], [4], [5, 6], [7], []]
                scores_and_values(b, g, nb, ng, [[(it, u) for it in its for u in range(UNITS)] for its in steps], moe)

            maxima_alone(0, 0)
            pe.wait_ge(route_in, 80)
            pe.wait_ge(mask_ready, 1)
            flat = mask[:].rearrange("p t e -> p (t e)")
            nc.tensor.matmul(bank(MOE)[:, 0:P], before[:], flat, start=True, stop=True)
            nc.tensor.matmul(bank(MOE)[:, P:2 * P], every[:], flat, start=True, stop=True).then_inc(counted, 1)
            pe.wait_ge(sin_in[1], 144)
            pe.wait_ge(ones_ready, 3)
            pe.wait_ge(v_copied, 1)
            with pe.Fori(0, B - 1) as b:
                group(b, 0, b, 1, 0)
                group(b, 1, b + 1, 0, 1)
            group(B - 1, 0, B - 1, 1, 2)
            group(B - 1, 1, None, None, 0)

        @block.scalar
        def _(act):
            act.sem_inc(exp_done, 3)
            act.sem_inc(moe_read, 1)
            act.wait_ge(gap_ready, 1)
            nc.scalar.activation(ex[:], lg[:], ACT.Exp).then_inc(exps_ready, 1)

            def group(b, g, moe):
                for jt in range(TPB):
                    for u in range(UNITS):
                        act.wait_ge(score_done, by_group(b, g, STEP, jt * UNITS + u + 1))
                        if u == 0:
                            act.wait_ge(pv2_done, by_group(b, g, TPB, jt + 1))
                            to = W2[:, jt % 2].rearrange("p h c -> p (h c)")
                        else:
                            h, c = (u - 1) % HG, (u - 1) // HG
                            if h == 0:
                                act.wait_ge(pv_done, by_group(b, g, 2 * TPB, jt * 2 + c + 1))
                            to = W[:, c, h, :]
                        nc.scalar.activation(to, bank(RING[u % 3]), ACT.Exp, scale=SCALE).then_inc(exp_done, 1)
                        if moe and u == 3:
                            act.wait_ge(moe_turned, b * TPB + (jt + 1))
                            act.wait_ge(moe_done, b * TPB + (jt + 1))
                            nc.scalar.activation(xgT[:], bank(MOE)[:, 0:P], ACT.Copy).then_inc(moe_xT, 1)
                    if moe:
                        act.wait_ge(moe_done, b * TPB + (jt + 2))
                        nc.scalar.activation(xg[:, moe - 1, jt, :], bank(MOE)[:, P:2 * P], ACT.Copy).then_inc(moe_read, 1)

            with act.Fori(0, B - 1) as b:
                group(b, 0, 0)
                group(b, 1, 1)
            group(B - 1, 0, 2)
            act.wait_ge(split, GROUPS + 1)
            nc.scalar.activation(s.next_gap[:], s.next_gap[:], ACT.Exp, scale=SCALE).then_inc(next_ready, 1)
            group(B - 1, 1, 0)

        @block.vector
        def _(dve):
            dve.sem_inc(max_read, 2)
            dve.sem_inc(mx_ready, 1)
            dve.sem_inc(split, 1)
            dve.sem_inc(ctx_read, 2)

            LINKS = 4

            t = s.tally

            def link(ins):
                dve.wait_ge(t.sem, t.by(ins))

            def route():
                full = [P, NT, E]
                link(nc.vector.memset(keep[:], 1.0))
                t.by(nc.vector.memset(keep[:, :, 0:1], 0.0))
                link(nc.vector.reduce_max(lmax[:], s.logits[:], AX.X))
                nc.vector.tensor_tensor(lg[:], s.logits[:], bc(lmax[:, :, None], full), ALU.subtract).then_inc(gap_ready, 1)
                dve.wait_ge(exps_ready, 1)
                for i in range(NT):
                    last = t.by(nc.vector.max(top[:, i, :], ex[:, i, :]))
                dve.wait_ge(t.sem, last)
                for i in range(NT):
                    last = t.by(nc.vector.max_index(idx[:, i, :], top[:, i, :], ex[:, i, :]))
                dve.wait_ge(t.sem, last)
                link(nc.vector.tensor_copy(idf[:], idx[:, :, 0]))
                dve.wait_ge(route_in, 80)
                nc.vector.tensor_tensor(mask[:], bc(idf[:, :, None], full), bc(exp_no[:, None, :], full), ALU.is_equal).then_inc(mask_ready, 1)
                dve.wait_ge(mask_ready, 1)
                link(nc.vector.reduce_sum(lmax[:], ex[:], AX.X))
                link(nc.vector.reciprocal(lmax[:], lmax[:]))
                y = bank(MOE)
                count_before(nc, s, dve, link, mask, counted, tot, incl, keep, pos, y[:, 0:P], y[:, P:2 * P])
                dve.sem_inc(counts_read, 1)
                link(nc.vector.tensor_tensor(pos[:], pos[:], mask[:], ALU.mult))
                link(nc.vector.reduce_sum(loc[:], pos[:], AX.X))
                link(nc.vector.tensor_scalar(kept[:], loc[:], float(CAPACITY), None, ALU.is_lt))
                link(nc.vector.scalar_tensor_tensor(out=loc[:], in0=idf[:], scalar=float(CAPACITY), in1=loc[:], op0=ALU.mult, op1=ALU.add))
                link(nc.vector.tensor_tensor(gates[:], lmax[:], kept[:], ALU.mult))
                link(nc.vector.tensor_tensor(idf[:], loc[:], behind[:], ALU.subtract))
                link(nc.vector.tensor_tensor(idf[:], idf[:], kept[:], ALU.mult))
                link(nc.vector.tensor_tensor(place[:, 0], idf[:], behind[:], ALU.add))
                link(nc.vector.tensor_tensor(place[:, 1], loc[:], kept[:], ALU.mult))
                dve.sem_inc(places_ready, 1)

            def maxima(b, g):
                s3 = s.s3[:, bass.ts(b, TPB), HG * g:HG * (g + 1)]
                dve.wait_ge(mx_ready, by_group(b, g, 1, 1))
                for it in range(TPB):
                    for u in range(UNITS):
                        dve.wait_ge(max_done, by_group(b, g, MAXSTEP, it * UNITS + u + 1))
                        y = bank(MAXRING[(g * MAXSTEP + it * UNITS + u) % 2])
                        if u == 0:
                            nc.vector.reduce_max(cm[:, it, :, 2], y.rearrange("p (h c) -> p h c", h=HG), AX.X).then_inc(max_read, 1)
                        else:
                            h, c = (u - 1) % HG, (u - 1) // HG
                            nc.vector.reduce_max(cm[:, it, h, c:c + 1], y, AX.X).then_inc(max_read, 1)
                dve.wait_ge(max_read, by_group(b, g, MAXSTEP, STEP + 2))
                nc.vector.reduce_max(mx[:].rearrange("p h t -> p t h"), cm[:], AX.X).then_inc(dve_done, 1)
                dve.wait_ge(dve_done, by_group(b, g, LINKS, 1))
                mt = mx[:].rearrange("p h t -> p t h")
                nc.vector.tensor_tensor(mt, mt, s3, ALU.max).then_inc(mx_ready, 1)
                dve.wait_ge(mx_ready, by_group(b, g, 1, 2))
                nc.vector.tensor_tensor(s.next_gap[:, bass.ts(b, TPB), HG * g:HG * (g + 1)], s3, mt, ALU.subtract).then_inc(dve_done, 1)
                if g:
                    dve.wait_ge(max_in[0], 96 * (b + 1))
                elif not isinstance(b, int):
                    dve.wait_ge(max_in[1], 96 * b)
                turned = bank(MAXRING[(g * MAXSTEP + STEP) % 2])[0:HG * TPB, 0:P]
                dve.wait_ge(max_done, by_group(b, g, MAXSTEP, MAXSTEP))
                nc.vector.tensor_scalar(mparts[:, 0], turned, -1.0, None, ALU.mult).then_inc(dve_done, 1)
                dve.wait_ge(dve_done, by_group(b, g, LINKS, 3))
                nc.vector.scalar_tensor_tensor(out=mrest[:], in0=turned, scalar=-1.0, in1=mparts[:, 0],
                                               op0=ALU.mult, op1=ALU.subtract).then_inc(max_read, 1)
                dve.wait_ge(max_read, by_group(b, g, MAXSTEP, MAXSTEP + 2))
                nc.vector.tensor_copy(mparts[:, 1], mrest[:]).then_inc(dve_done, 1)
                dve.wait_ge(dve_done, by_group(b, g, LINKS, 4))
                nc.vector.tensor_tensor(mparts[:, 2], mrest[:], mparts[:, 1], ALU.subtract).then_inc(split, 1)

            def context(b, g):
                dve.wait_ge(ctx_done, by_group(b, g, 1, 2))
                nc.vector.tensor_copy(s.U[:, g, bass.ts(b * 2, CH)], bank(PV[0])).then_inc(ctx_read, 1)
                nc.vector.tensor_copy(s.U[:, g, bass.ts(b * 2 + 1, CH)], bank(PV[1])).then_inc(ctx_read, 1)

            maxima(0, 0)
            route()
            with dve.Fori(0, B - 1) as b:
                maxima(b, 1)
                context(b, 0)
                maxima(b + 1, 0)
                context(b, 1)
            maxima(B - 1, 1)
            context(B - 1, 0)
            context(B - 1, 1)


def second_layer_out(nc, s, I, out):
    sem = s.sem
    dve_done = s.tally.sem
    consts = sem("l1_out_constants")
    u_turned, u_read, ctx_ready, cT_done, cT_copied = (
        sem("context_turned"), sem("context_turned_read"), sem("token_context_ready"), sem("ctxT_done"), sem("ctxT_copied"))
    o_done, out_ready, out_sent = sem("l1_o_done"), sem("out_ready"), sem("out_sent")
    bank = s.bank
    U_BANKS, T_BANKS, O_BANKS = (0, 1, 2), (3, 4), (5, 6)
    NP = NT // 2
    with ExitStack() as ctx:
        def sb(name, shape, dt=F32):
            return ctx.enter_context(nc.sbuf_tensor(name, shape, dt))

        wo = sb("Wo", [P, D])
        num = sb("context_num", [P, 2, 2 * NH, DH])
        den = sb("context_den", [P, 2, 2 * NH])
        cT = sb("ctxT", [P, 2, 2 * P])
        block = ctx.enter_context(nc.Block())

        @block.sync
        def _(sp):
            sp.dma_start(wo[:], I["L1_attn_Wo"]).then_inc(consts, 16)
            flat = out.rearrange("b (t p) d -> p (b t) d", p=P)
            for k in range(NP):
                sp.wait_ge(out_ready, k + 1)
                sp.dma_start(flat[:, 2 * k:2 * k + 2], s.x[:, 2 * k:2 * k + 2]).then_inc(out_sent, 16)
            sp.wait_ge(out_sent, 16 * NP)

        @block.tensor
        def _(pe):
            def turn_contexts(k):
                if k >= 3:
                    pe.wait_ge(u_read, k - 2)
                for i in range(2):
                    for g in range(2):
                        t = 2 * k + i
                        last = nc.tensor.transpose(bank(U_BANKS[k % 3])[:, (2 * i + g) * P:(2 * i + g + 1) * P], s.U[:, g, t * P:(t + 1) * P], s.ident[:])
                last.then_inc(u_turned, 1)

            def turn_back(k):
                pe.wait_ge(ctx_ready, k + 1)
                if k >= 2:
                    pe.wait_ge(cT_copied, k - 1)
                for i in range(2):
                    last = nc.tensor.transpose(bank(T_BANKS[k % 2])[:, i * P:(i + 1) * P],
                                               num[:, k % 2, NH * i:NH * (i + 1), :].rearrange("p h d -> p (h d)"), s.ident[:])
                last.then_inc(cT_done, 1)

            def output(k):
                pe.wait_ge(cT_copied, k + 1)
                if k >= 2:
                    pe.wait_ge(out_ready, k - 1)
                for i in range(2):
                    last = nc.tensor.matmul(bank(O_BANKS[k % 2])[:, i * P:(i + 1) * P], cT[:, k % 2, i * P:(i + 1) * P], wo[:], start=True, stop=True)
                last.then_inc(o_done, 1)

            for k in range(3):
                turn_contexts(k)
            pe.wait_ge(consts, 16)
            for k in range(NP):
                turn_back(k)
                if k:
                    output(k - 1)
                if k + 3 < NP:
                    turn_contexts(k + 3)
            output(NP - 1)

        @block.scalar
        def _(act):
            for k in range(NP):
                act.wait_ge(cT_done, k + 1)
                if k >= 2:
                    act.wait_ge(o_done, k - 1)
                nc.scalar.activation(cT[:, k % 2], bank(T_BANKS[k % 2])[:, 0:2 * P], ACT.Copy).then_inc(cT_copied, 1)

        @block.vector
        def _(dve):
            t = s.tally

            def link(ins):
                dve.wait_ge(dve_done, t.by(ins))

            e3 = s.next_gap[:].rearrange("p t h -> p (t h)")
            ev = s.v_next[:].rearrange("p t (h d) -> p (t h) d", h=NH)

            def context(k):
                m = k % 2
                dve.wait_ge(u_turned, k + 1)
                if k >= 2:
                    dve.wait_ge(cT_done, k - 1)
                y = bank(U_BANKS[k % 3]).rearrange("p (h d) -> p h d", d=32)
                hs = slice(2 * NH * k, 2 * NH * (k + 1))
                t.by(nc.vector.tensor_tensor(den[:, m], y[:, :, DH], e3[:, hs], ALU.add))
                link(nc.vector.tensor_tensor(num[:, m], y[:, :, 0:DH], ev[:, hs, :], ALU.add))
                dve.sem_inc(u_read, 1)
                link(nc.vector.reciprocal(den[:, m], den[:, m]))
                nc.vector.tensor_tensor(num[:, m], num[:, m], bc(den[:, m, :, None], [P, 2 * NH, DH]), ALU.mult).then_inc(ctx_ready, 1)

            def finish(k):
                dve.wait_ge(o_done, k + 1)
                xs = s.x[:, 2 * k:2 * k + 2]
                nc.vector.tensor_tensor(xs, xs, bank(O_BANKS[k % 2])[:, 0:2 * P].rearrange("p (t d) -> p t d", t=2), ALU.add).then_inc(out_ready, 1)

            for k in range(NP):
                context(k)
                if k:
                    finish(k - 1)
            finish(NP - 1)


def build(nc, I, out):
    with ExitStack() as ctx:
        s = Shared()

        def sb(name, shape, dt=F32):
            return ctx.enter_context(nc.sbuf_tensor(name, shape, dt))

        s.sem = lambda name: ctx.enter_context(nc.semaphore(name))
        s.tally = Tally(s.sem("dve_steps"))
        banks = [ctx.enter_context(nc.psum_tensor(f"bank{i}", [P, CH], F32)) for i in range(8)]
        s.bank = lambda i: banks[i][:]
        s.rows_in = nc.dram_tensor("rows_by_expert", (SLOTS * P, D + 1), F32, kind="Internal").ap()
        s.rows_out = nc.dram_tensor("expert_results", (1 + 2 * T + SLOTS * P, D), F32, kind="Internal").ap()
        s.rows2_in = nc.dram_tensor("rows_by_second_expert", (2 * T, D), F32, kind="Internal").ap()
        s.rows2_out = nc.dram_tensor("second_expert_results", (T, D), F32, kind="Internal").ap()
        s.expert_w_in = s.sem("expert_weights_loaded")
        s.sel_in = s.sem("selectors_loaded")
        s.ident = sb("identity", [P, P])
        s.vec = sb("vectors_sb", [P, 24])
        s.x = sb("x", [P, NT, D])
        with ExitStack() as l0:
            def sb0(name, shape, dt=F32, c=l0):
                return c.enter_context(nc.sbuf_tensor(name, shape, dt))
            s.xn = sb0("xn", [P, NT, D])
            s.scores = sb0("scores", [P, NT, 8])
            s.wt = sb0("expert_weights_of_tokens", [P, 2, NT])
            s.pos = sb0("positions", [P, 2, NT], U32)
            s.slot_e = sb0("slot_expert", [P, SLOTS], I32)
            s.A = sb0("A", [P, DG, NS])
            s.zs = sb0("silu_z", [P, DG, T])
            s.u = sb0("u", [P, DG, T])
            s.delta = sb0("delta", [P, DG, T])
            s.du = sb0("delta_u", [P, DG, T])
            s.bc3 = sb0("bc_parts", [96, T], BF16)
            s.sel = sb0("selectors", [96, 2, NS, P], BF16)
            with ExitStack() as c:
                s.xnT = sb0("xnT", [P, T], c=c)
                s.gate_w = sb0("gate_w", [P, 8], c=c)
                s.taps = sb0("taps", [P, DG, KC], c=c)
                norms_and_projections(nc, s, I)
            with ExitStack() as c:
                s.w1 = sb0("w1", [P, 8, 512], c=c)
                s.w3 = sb0("w3", [P, 8, 512], c=c)
                s.w2 = sb0("w2", [P, 8, 4, P], c=c)
                selective_scan(nc, s, I)
                experts(nc, s, I)
            first_layer_out(nc, s, I)
        with ExitStack() as l1:
            def sb1(name, shape, dt=F32, c=l1):
                return c.enter_context(nc.sbuf_tensor(name, shape, dt))
            s.parts = nc.dram_tensor("operand_parts", (B, 2, DH, 3 * 4, HG, L), BF16, kind="Internal").ap()
            s.xb = sb1("xb", [P, NT, D])
            s.logits = sb1("logits", [P, NT, 8])
            s.vals = sb1("values", [P, NT, D])
            s.v_next = sb1("next_values", [P, NT, D])
            s.s3 = sb1("next_key_scores", [P, NT, NH])
            s.next_gap = sb1("next_key_gap", [P, NT, NH])
            s.U = sb1("contexts", [P, 2, T])
            attention_operands(nc, s, I)
            attention(nc, s, I)
            second_layer_out(nc, s, I, out)


BIG = -1e30


def constants():
    import numpy as np

    bf = mybir.dt.np(BF16)
    k, m = np.arange(P)[:, None], np.arange(P)[None, :]
    out = {"ident": np.eye(P, dtype=np.float32), "ident_bf": np.eye(P).astype(bf)}
    out["before"] = (k < m).astype(np.float32)
    out["every"] = np.ones((P, P), np.float32)
    sel = np.zeros((96, 2, NS, P), np.float32)
    for part in range(3):
        for which in range(2):
            for n in range(NS):
                sel[32 * part + NS * which + n, which, n, :] = 1.0
    out["selectors"] = sel.astype(bf)
    first = np.where(m > k, BIG, 0.0)
    second = np.where(m < k + 2, BIG, 0.0)
    corner = np.zeros((P, 2))
    corner[P - 1, 0] = BIG
    corner[0, 1] = BIG
    out["masks"] = np.concatenate([first, second, first.T, second.T, corner], 1).astype(bf)
    w = np.exp(np.arange(0, D, 2, dtype=np.float32) * np.float32(-np.log(10000.0) / D)).astype(np.float64)
    w = np.repeat(w, 2)[:, None]
    sign = np.where(np.arange(D) % 2 == 0, -1.0, 1.0)[:, None]
    i = np.arange(L)[None, :]
    turn = [np.cos((L - 1 - i) * w), sign * np.sin((L - 1 - i) * w), np.cos((i + 2) * w), -sign * np.sin((i + 2) * w)]
    out["turns"] = np.stack(turn, 1).astype(np.float32)
    table = np.where(sign < 0, np.sin(i * w), np.cos(i * w)).astype(np.float32)
    hi = table.astype(bf)
    mid = (table - hi.astype(np.float32)).astype(bf)
    lo = (table - hi.astype(np.float32) - mid.astype(np.float32)).astype(bf)
    out["sinusoids"] = np.stack([hi, mid, lo], 1)
    out["head_selector"] = (k // 16 == np.arange(D // 16)[None, :]).astype(np.float32)
    out["rows_behind"] = (T + k + P * np.arange(NT)[None, :]).astype(np.float32)
    token = k + P * np.arange(NT)[None, :]
    out["result_places"] = np.stack([1 + token, 1 + T + token], 1).astype(np.float32)
    out["unused_places"] = (1 + 2 * T + k + P * np.arange(SLOTS)[None, :]).astype(np.float32)
    slot = np.arange(NT * 2 + 8, dtype=np.float32)
    out["slot_numbers"] = np.broadcast_to(slot, (P, slot.size)).copy()
    out["expert_numbers"] = np.broadcast_to(np.arange(8, dtype=np.float32), (P, 8)).copy()
    return out


def layouts(v):
    import numpy as np

    a = {k: np.asarray(x) for k, x in v.items()}
    o = {k: a[k] for k in ("L0_attn_x", "L0_attn_A_log", "L1_attn_Wo", "L1_ffn_wg", "L1_ffn_b")}
    o["L0_attn_conv_w"] = a["L0_attn_conv_w"][:, 0, :]
    o["in_w_t"] = a["L0_attn_in_w"].T
    xw = a["L0_attn_xproj_w"].T
    o["xproj_t"] = xw[:, :R]
    o["xproj_bc_t"] = np.concatenate([xw[:, R:]] * 3, 1)
    o["dt_w_t"] = a["L0_attn_dt_w"].T
    o["out_w_t"] = a["L0_attn_out_w"].T
    o["gate_w_t"] = a["L0_ffn_gate_w"].T
    o["w1_t"] = a["L0_ffn_w1"].transpose(2, 0, 1)
    o["w3_t"] = a["L0_ffn_w3"].transpose(2, 0, 1)
    o["w2_t"] = a["L0_ffn_w2"].reshape(8, D, 4, P).transpose(3, 0, 2, 1)
    heads = D // 16

    def blocks(w):
        z = np.zeros((D, D), w.dtype)
        for h in range(heads):
            z[16 * h:16 * h + 16, 16 * h:16 * h + 16] = w
        return z

    wpt = a["L1_attn_Wp"].T
    swapped = wpt.reshape(16, 8, 2)[:, :, ::-1].reshape(16, 16)
    o["head_w"] = np.stack([blocks(a["L1_attn_Wq"]), blocks(a["L1_attn_Wk"]), blocks(a["L1_attn_Wv"]),
                            blocks(wpt), blocks(swapped)], 1)
    rep = lambda x: np.concatenate([x] * heads)
    two = lambda x: [x[:P], x[P:]]
    cols = [a["L0_attn_norm_g"], a["L0_attn_norm_b"], *two(a["L0_attn_conv_b"]), *two(a["L0_attn_dt_b"]), *two(a["L0_attn_D"]),
            a["L1_attn_ln_gamma"], a["L1_attn_ln_beta"], rep(a["L1_attn_bq"]), rep(a["L1_attn_bk"]),
            a["L1_attn_u_bias"].reshape(D), a["L1_attn_v_bias"].reshape(D)]
    cols += [np.zeros(P, np.float32)] * (24 - len(cols))
    o["vectors"] = np.stack(cols, 1)
    o["rows"] = np.stack([rep(a["L1_attn_bq"]), a["L1_attn_u_bias"].reshape(D), rep(a["L1_attn_bk"]), rep(a["L1_attn_bv"]),
                          a["L1_attn_bo"]], 0)
    o["moe_w"] = a["L1_ffn_W"].transpose(2, 0, 1)
    o.update(constants())
    return {k: np.ascontiguousarray(x) for k, x in o.items()}


def kernel(**inputs):
    import concourse.bacc as bacc
    from concourse.bass_utils import run_bass_kernel_spmd

    nc = bacc.Bacc("TRN2", target_bir_lowering=False, num_devices=1)
    arrays = layouts(inputs)
    aps = {k: nc.dram_tensor("in_" + k, x.shape, mybir.dt.from_np(x.dtype), kind="ExternalInput").ap() for k, x in arrays.items()}
    out = nc.dram_tensor("out", (B, L, D), F32, kind="ExternalOutput").ap()
    build(nc, aps, out)
    r = run_bass_kernel_spmd(nc, [{"in_" + k: x for k, x in arrays.items()}], core_ids=[0])
    return r.results[0]["out"]
```
